# Optimizing a Trainium2 kernel written in Bass

```python
import numpy as np
import jax
import jax.numpy as jnp

def _softmax(x, axis=-1):
    return jax.nn.softmax(x, axis=axis)

def _gelu(x):
    return jax.nn.gelu(x, approximate=True)

def _silu(x):
    return jax.nn.silu(x)

def _sigmoid(x):
    return jax.nn.sigmoid(x)

def _layernorm(x, axis=-1, eps=1e-05):
    m = jnp.mean(x, axis=axis, keepdims=True)
    v = jnp.var(x, axis=axis, keepdims=True)
    return (x - m) / jnp.sqrt(v + eps)

def _scatter_add(tgt, idx, src, axis=0):
    return tgt.at[idx].add(src)

def _segment_sum(src, seg, n):
    return jax.ops.segment_sum(src, seg, n)
kernel_name = 'mk_flamingo_gated_d4_seqx_r8_2ff7d9'

def setup_inputs(seed: int=0):
    np.random.seed(seed)
    _w = jnp.asarray

    def _rec_inputs():
        import jax
        import jax.numpy as jnp
        _rk = jax.random.key(seed)
        x = -0.0005146 + 1 * jax.random.normal(jax.random.fold_in(_rk, 1), (4, 512, 128), jnp.float32)
        _lenS = 512 - jax.random.randint(jax.random.fold_in(_rk, 7), (4,), 0, max(1, 512 // 4) + 1, jnp.int32)
        _lenS2 = 154 - jax.random.randint(jax.random.fold_in(_rk, 8), (4,), 0, max(1, 154 // 4) + 1, jnp.int32)
        _ctx_1024P = jax.random.normal(jax.random.fold_in(_rk, 11), (4, 16, 128), jnp.float32)
        _ctx_1024c = jax.random.dirichlet(jax.random.fold_in(_rk, 511), 0.3 * jnp.ones((16,), jnp.float32), (4, 154))
        _ctx_1024t = jnp.einsum('bsk,bkd->bsd', _ctx_1024c, _ctx_1024P)
        _ctx_1024t = _ctx_1024t * jax.lax.rsqrt(jnp.mean(jnp.square(_ctx_1024t)) + 1e-12) * 0.953939
        ctx_1024 = -0.000392918 + 0.999932 * (_ctx_1024t + 0.3 * jax.random.normal(jax.random.fold_in(_rk, 611), (4, 154, 128), jnp.float32))
        _validS = jnp.arange(512)[None, :] < _lenS[:, None]
        _validS2 = jnp.arange(154)[None, :] < _lenS2[:, None]
        _causal = jnp.tril(jnp.ones((512, 512), dtype=bool))
        mask_BxSxS2_bf0 = jnp.logical_not(jnp.ones((4, 512, 154), dtype=bool))
        _g = jax.random.normal(jax.random.fold_in(_rk, 9001), (2, 4), jnp.float32)
        _g = jnp.sign(_g) * jnp.maximum(jnp.abs(_g), 1.0) + (_g == 0) * 1.0
        g_xattn = _g[0]
        g_ffn = _g[1]
        return (x, ctx_1024, mask_BxSxS2_bf0, g_xattn, g_ffn)
    x, ctx_1024, mask_BxSxS2_bf0, g_xattn, g_ffn = _rec_inputs()

    def _L0_xattn_setup():
        import jax, jax.numpy as jnp
        import numpy as np
        DIM = 128
        DIM_HEAD = 64
        HEADS = 16
        INNER = DIM_HEAD * HEADS
        EPS = 1e-05

        def layer_norm(x, g, b):
            m = jnp.mean(x, axis=-1, keepdims=True)
            v = jnp.mean(jnp.square(x - m), axis=-1, keepdims=True)
            return (x - m) * jax.lax.rsqrt(v + EPS) * g + b
        key = jax.random.key(seed)
        ks = jax.random.split(key, 8)
        B, N_IMG, N_LAT = (4, 512, 64)
        std = 1.0 / np.sqrt(DIM)
        return {'image_embeds': jax.random.normal(ks[0], (B, N_IMG, DIM), dtype=jnp.float32), 'latents': jax.random.normal(ks[1], (B, N_LAT, DIM), dtype=jnp.float32), 'ln1_g': jnp.ones((DIM,), jnp.float32), 'ln1_b': jnp.zeros((DIM,), jnp.float32), 'ln2_g': jnp.ones((DIM,), jnp.float32), 'ln2_b': jnp.zeros((DIM,), jnp.float32), 'Wq': jax.random.normal(ks[2], (DIM, INNER), dtype=jnp.float32) * std, 'Wkv': jax.random.normal(ks[3], (DIM, 2 * INNER), dtype=jnp.float32) * std, 'Wo': jax.random.normal(ks[4], (INNER, DIM), dtype=jnp.float32) * std}
    _L0_xattn_all = _L0_xattn_setup()
    _L0_xattn_in = {k: v for k, v in _L0_xattn_all.items() if k in ('ln1_g', 'ln1_b', 'ln2_g', 'ln2_b', 'Wq', 'Wkv', 'Wo')}
    del _L0_xattn_all

    def _L0_ffn_setup():
        import jax, jax.numpy as jnp
        import numpy as np
        D_MODEL = 128
        D_FF = 512
        NUM_EXPERTS = 8
        key = jax.random.key(seed)
        ks = jax.random.split(key, 8)
        scale_in = 1.0 / np.sqrt(D_MODEL)
        scale_ff = 1.0 / np.sqrt(D_FF)
        x = jax.random.normal(ks[0], (4, 256, D_MODEL), dtype=jnp.float32)
        gate_w = jax.random.uniform(ks[1], (NUM_EXPERTS, D_MODEL), jnp.float32, -scale_in, scale_in)
        gate_b = jax.random.uniform(ks[2], (NUM_EXPERTS,), jnp.float32, -scale_in, scale_in)
        expert_bias = jnp.zeros((NUM_EXPERTS,), dtype=jnp.float32)
        w1 = jax.random.uniform(ks[3], (NUM_EXPERTS, D_MODEL, D_FF), jnp.float32, -scale_in, scale_in)
        b1 = jax.random.uniform(ks[4], (NUM_EXPERTS, D_FF), jnp.float32, -scale_in, scale_in)
        w2 = jax.random.uniform(ks[5], (NUM_EXPERTS, D_FF, D_MODEL), jnp.float32, -scale_ff, scale_ff)
        b2 = jax.random.uniform(ks[6], (NUM_EXPERTS, D_MODEL), jnp.float32, -scale_ff, scale_ff)
        return {'x': x, 'gate_w': gate_w, 'gate_b': gate_b, 'expert_bias': expert_bias, 'w1': w1, 'b1': b1, 'w2': w2, 'b2': b2}
    _L0_ffn_all = _L0_ffn_setup()
    _L0_ffn_in = {k: v for k, v in _L0_ffn_all.items() if k in ('gate_w', 'gate_b', 'expert_bias', 'w1', 'b1', 'w2', 'b2')}
    del _L0_ffn_all

    def _L1_xattn_setup():
        import jax, jax.numpy as jnp
        import numpy as np
        B, SQ, SK, D = (4, 256, 256, 128)
        key = jax.random.key(seed)
        ks = jax.random.split(key, 8)
        s = 1.0 / np.sqrt(D)
        return {'input_seq': jax.random.normal(ks[0], (B, SQ, D), jnp.float32), 'condition_seq': jax.random.normal(ks[1], (B, SK, D), jnp.float32), 'Wq': jax.random.normal(ks[2], (D, D), jnp.float32) * s, 'bq': jnp.zeros((D,), jnp.float32), 'Wk': jax.random.normal(ks[3], (D, D), jnp.float32) * s, 'bk': jnp.zeros((D,), jnp.float32), 'Wv': jax.random.normal(ks[4], (D, D), jnp.float32) * s, 'bv': jnp.zeros((D,), jnp.float32)}
    _L1_xattn_all = _L1_xattn_setup()
    _L1_xattn_in = {k: v for k, v in _L1_xattn_all.items() if k in ('Wq', 'bq', 'Wk', 'bk', 'Wv', 'bv')}
    del _L1_xattn_all

    def _L1_ffn_setup():
        import jax, jax.numpy as jnp
        import numpy as np
        H = 16
        E = 8
        EPS = 1e-05

        def _layernorm(x, g, b):
            mu = jnp.mean(x, axis=-1, keepdims=True)
            var = jnp.mean(jnp.square(x - mu), axis=-1, keepdims=True)
            return (x - mu) * jax.lax.rsqrt(var + EPS) * g + b
        key = jax.random.key(seed)
        T, B, C = (128, 8, 128)
        ks = jax.random.split(key, 12)
        s = 0.02
        return {'x': jax.random.normal(ks[0], (T, B, C), jnp.float32), 'in_proj_w': jax.random.normal(ks[1], (3 * C, C), jnp.float32) * s, 'in_proj_b': jnp.zeros((3 * C,), jnp.float32), 'out_w': jax.random.normal(ks[2], (C, C), jnp.float32) * s, 'out_b': jnp.zeros((C,), jnp.float32), 'ln1_g': jnp.ones((C,), jnp.float32), 'ln1_b': jnp.zeros((C,), jnp.float32), 'router_w': jax.random.normal(ks[3], (E, C), jnp.float32) * s, 'router_b': jnp.zeros((E,), jnp.float32), 'w1': jax.random.normal(ks[4], (E, C, C), jnp.float32) * s, 'b1': jnp.zeros((E, C), jnp.float32), 'w2': jax.random.normal(ks[5], (E, C, C), jnp.float32) * s, 'b2': jnp.zeros((E, C), jnp.float32), 'ln2_g': jnp.ones((C,), jnp.float32), 'ln2_b': jnp.zeros((C,), jnp.float32)}
    _L1_ffn_all = _L1_ffn_setup()
    _L1_ffn_in = {k: v for k, v in _L1_ffn_all.items() if k in ('in_proj_w', 'in_proj_b', 'out_w', 'out_b', 'ln1_g', 'ln1_b', 'router_w', 'router_b', 'w1', 'b1', 'w2', 'b2', 'ln2_g', 'ln2_b')}
    del _L1_ffn_all

    def _L2_xattn_setup():
        import jax, jax.numpy as jnp
        import numpy as np
        import math
        B, LQ, LK = (2, 256, 256)
        DIM = 128
        H = 16
        DH = DIM // H
        key = jax.random.key(seed)
        ks = jax.random.split(key, 12)
        s = 1.0 / math.sqrt(DIM)
        return {'query': jax.random.normal(ks[0], (B, LQ, DIM), jnp.float32), 'key': jax.random.normal(ks[1], (B, LK, DIM), jnp.float32), 'value': jax.random.normal(ks[2], (B, LK, DIM), jnp.float32), 'mask': jnp.zeros((B, LQ, LK), dtype=bool), 'Wq': jax.random.normal(ks[3], (DIM, DIM), jnp.float32) * s, 'bq': jax.random.normal(ks[4], (DIM,), jnp.float32) * s, 'Wk': jax.random.normal(ks[5], (DIM, DIM), jnp.float32) * s, 'bk': jax.random.normal(ks[6], (DIM,), jnp.float32) * s, 'Wv': jax.random.normal(ks[7], (DIM, DIM), jnp.float32) * s, 'bv': jax.random.normal(ks[8], (DIM,), jnp.float32) * s, 'Wo': jax.random.normal(ks[9], (DIM, DIM), jnp.float32) * s, 'bo': jax.random.normal(ks[10], (DIM,), jnp.float32) * s}
    _L2_xattn_all = _L2_xattn_setup()
    _L2_xattn_in = {k: v for k, v in _L2_xattn_all.items() if k in ('Wq', 'bq', 'Wk', 'bk', 'Wv', 'bv', 'Wo', 'bo')}
    del _L2_xattn_all

    def _L2_ffn_setup():
        import jax, jax.numpy as jnp
        import numpy as np
        D_IN, D_HID = (128, 512)

        def _ternary(key, shape):
            return jax.random.randint(key, shape, -1, 2).astype(jnp.float32)

        def _tlin(x, w, s):
            return jnp.einsum('bsi,oi->bso', x, w) * s
        key = jax.random.key(seed)
        ks = jax.random.split(key, 12)
        inv = lambda fan: 1.0 / np.sqrt(fan).astype(np.float32)
        return {'x': jax.random.normal(ks[0], (4, 256, D_IN), dtype=jnp.float32), 'w1_w': _ternary(ks[1], (D_HID, D_IN)), 'w1_s': jax.random.uniform(ks[2], (D_HID,), dtype=jnp.float32) * inv(D_IN), 'w2_w': _ternary(ks[3], (D_HID, D_IN)), 'w2_s': jax.random.uniform(ks[4], (D_HID,), dtype=jnp.float32) * inv(D_IN), 'h1_w': _ternary(ks[5], (D_HID, D_HID)), 'h1_s': jax.random.uniform(ks[6], (D_HID,), dtype=jnp.float32) * inv(D_HID), 'h2_w': _ternary(ks[7], (D_HID, D_HID)), 'h2_s': jax.random.uniform(ks[8], (D_HID,), dtype=jnp.float32) * inv(D_HID), 'w3_w': _ternary(ks[9], (D_IN, D_HID)), 'w3_s': jax.random.uniform(ks[10], (D_IN,), dtype=jnp.float32) * inv(D_HID)}
    _L2_ffn_all = _L2_ffn_setup()
    _L2_ffn_in = {k: v for k, v in _L2_ffn_all.items() if k in ('w1_w', 'w1_s', 'w2_w', 'w2_s', 'h1_w', 'h1_s', 'h2_w', 'h2_s', 'w3_w', 'w3_s')}
    del _L2_ffn_all

    def _L3_xattn_setup():
        import jax, jax.numpy as jnp
        import numpy as np
        B, NT, NM, C, H, FF = (8, 128, 256, 128, 8, 512)

        def _ln(x, g, b):
            m = x.mean(-1, keepdims=True)
            v = jnp.mean((x - m) ** 2, axis=-1, keepdims=True)
            return (x - m) / jnp.sqrt(v + 1e-05) * g + b
        key = jax.random.key(seed)
        ks = jax.random.split(key, 8)
        w = lambda k, shape, s=0.02: jax.random.normal(k, shape, dtype=jnp.float32) * s
        return {'tgt': jax.random.normal(ks[0], (B, NT, C), dtype=jnp.float32), 'memory': jax.random.normal(ks[1], (B, NM, C), dtype=jnp.float32), 'qkv_w': w(ks[2], (3 * C, C)), 'qkv_b': jnp.zeros((3 * C,), jnp.float32), 'sa_out_w': w(ks[3], (C, C)), 'sa_out_b': jnp.zeros((C,), jnp.float32), 'in_proj_w': w(ks[4], (3 * C, C)), 'in_proj_b': jnp.zeros((3 * C,), jnp.float32), 'mha_out_w': w(ks[5], (C, C)), 'mha_out_b': jnp.zeros((C,), jnp.float32), 'lin1_w': w(ks[6], (FF, C)), 'lin1_b': jnp.zeros((FF,), jnp.float32), 'lin2_w': w(ks[7], (C, FF)), 'lin2_b': jnp.zeros((C,), jnp.float32), 'ln1_g': jnp.ones((C,), jnp.float32), 'ln1_b': jnp.zeros((C,), jnp.float32), 'ln2_g': jnp.ones((C,), jnp.float32), 'ln2_b': jnp.zeros((C,), jnp.float32), 'ln3_g': jnp.ones((C,), jnp.float32), 'ln3_b': jnp.zeros((C,), jnp.float32)}
    _L3_xattn_all = _L3_xattn_setup()
    _L3_xattn_in = {k: v for k, v in _L3_xattn_all.items() if k in ('qkv_w', 'qkv_b', 'sa_out_w', 'sa_out_b', 'in_proj_w', 'in_proj_b', 'mha_out_w', 'mha_out_b', 'lin1_w', 'lin1_b', 'lin2_w', 'lin2_b', 'ln1_g', 'ln1_b', 'ln2_g', 'ln2_b', 'ln3_g', 'ln3_b')}
    del _L3_xattn_all

    def _L3_ffn_setup():
        import jax, jax.numpy as jnp
        import numpy as np
        HIDDEN = 128
        HEAD_DIM = 64
        N_EXPERTS = 16
        MIN_EXPERTS = 2
        B, T = (4, 256)

        def _normalize(x, axis):
            n = jnp.sqrt(jnp.sum(x * x, axis=axis, keepdims=True))
            return x / jnp.maximum(n, 1e-12)

        def _ste(x):
            hard = jax.lax.stop_gradient((x > 0).astype(x.dtype))
            return hard + x - jax.lax.stop_gradient(x)

        def _gating(hidden_states, sim_matrix, gates):
            b, t, c = hidden_states.shape
            flat = hidden_states.reshape(b * t, c)
            logits = _normalize(flat, -1) @ _normalize(sim_matrix, 0) - jax.nn.sigmoid(gates)
            gated = jax.nn.relu(logits)
            mask = _ste(gated)
            inactive = jnp.sum(mask, axis=1) == 0
            _, fb_idx = jax.lax.top_k(logits, MIN_EXPERTS)
            fb = jnp.zeros_like(mask).at[jnp.arange(b * t)[:, None], fb_idx].set(1.0)
            fb_applied = inactive[:, None] & (fb > 0)
            mask = jnp.where(fb_applied, 1.0, mask)
            masked_logits = jnp.where(mask > 0, gated, -jnp.inf)
            return jax.nn.softmax(masked_logits, axis=-1).reshape(b, t, -1)
        key = jax.random.key(seed)
        ks = jax.random.split(key, 6)
        xav_qkv = float(np.sqrt(6.0 / (HIDDEN + HEAD_DIM)))
        return {'hidden_states': jax.random.normal(ks[0], (B, T, HIDDEN), dtype=jnp.float32), 'sim_matrix': jax.random.normal(ks[1], (HIDDEN, N_EXPERTS), dtype=jnp.float32), 'gates': jnp.zeros((N_EXPERTS,), dtype=jnp.float32), 'q_proj': jax.random.uniform(ks[2], (N_EXPERTS, HIDDEN, HEAD_DIM), jnp.float32, -xav_qkv, xav_qkv), 'k_proj': jax.random.uniform(ks[3], (N_EXPERTS, HIDDEN, HEAD_DIM), jnp.float32, -xav_qkv, xav_qkv), 'v_proj': jax.random.uniform(ks[4], (N_EXPERTS, HIDDEN, HEAD_DIM), jnp.float32, -xav_qkv, xav_qkv), 'o_proj': jax.random.uniform(ks[5], (N_EXPERTS, HEAD_DIM, HIDDEN), jnp.float32, -xav_qkv, xav_qkv)}
    _L3_ffn_all = _L3_ffn_setup()
    _L3_ffn_in = {k: v for k, v in _L3_ffn_all.items() if k in ('sim_matrix', 'gates', 'q_proj', 'k_proj', 'v_proj', 'o_proj')}
    del _L3_ffn_all
    return {'x': x, 'ctx_1024': ctx_1024, 'mask_BxSxS2_bf0': mask_BxSxS2_bf0, 'g_xattn': g_xattn, 'g_ffn': g_ffn, 'L0_xattn_ln1_g': _L0_xattn_in['ln1_g'], 'L0_xattn_ln1_b': _L0_xattn_in['ln1_b'], 'L0_xattn_ln2_g': _L0_xattn_in['ln2_g'], 'L0_xattn_ln2_b': _L0_xattn_in['ln2_b'], 'L0_xattn_Wq': _L0_xattn_in['Wq'], 'L0_xattn_Wkv': _L0_xattn_in['Wkv'], 'L0_xattn_Wo': _L0_xattn_in['Wo'], 'L0_ffn_gate_w': _L0_ffn_in['gate_w'], 'L0_ffn_gate_b': _L0_ffn_in['gate_b'], 'L0_ffn_expert_bias': _L0_ffn_in['expert_bias'], 'L0_ffn_w1': _L0_ffn_in['w1'], 'L0_ffn_b1': _L0_ffn_in['b1'], 'L0_ffn_w2': _L0_ffn_in['w2'], 'L0_ffn_b2': _L0_ffn_in['b2'], 'L1_xattn_Wq': _L1_xattn_in['Wq'], 'L1_xattn_bq': _L1_xattn_in['bq'], 'L1_xattn_Wk': _L1_xattn_in['Wk'], 'L1_xattn_bk': _L1_xattn_in['bk'], 'L1_xattn_Wv': _L1_xattn_in['Wv'], 'L1_xattn_bv': _L1_xattn_in['bv'], 'L1_ffn_in_proj_w': _L1_ffn_in['in_proj_w'], 'L1_ffn_in_proj_b': _L1_ffn_in['in_proj_b'], 'L1_ffn_out_w': _L1_ffn_in['out_w'], 'L1_ffn_out_b': _L1_ffn_in['out_b'], 'L1_ffn_ln1_g': _L1_ffn_in['ln1_g'], 'L1_ffn_ln1_b': _L1_ffn_in['ln1_b'], 'L1_ffn_router_w': _L1_ffn_in['router_w'], 'L1_ffn_router_b': _L1_ffn_in['router_b'], 'L1_ffn_w1': _L1_ffn_in['w1'], 'L1_ffn_b1': _L1_ffn_in['b1'], 'L1_ffn_w2': _L1_ffn_in['w2'], 'L1_ffn_b2': _L1_ffn_in['b2'], 'L1_ffn_ln2_g': _L1_ffn_in['ln2_g'], 'L1_ffn_ln2_b': _L1_ffn_in['ln2_b'], 'L2_xattn_Wq': _L2_xattn_in['Wq'], 'L2_xattn_bq': _L2_xattn_in['bq'], 'L2_xattn_Wk': _L2_xattn_in['Wk'], 'L2_xattn_bk': _L2_xattn_in['bk'], 'L2_xattn_Wv': _L2_xattn_in['Wv'], 'L2_xattn_bv': _L2_xattn_in['bv'], 'L2_xattn_Wo': _L2_xattn_in['Wo'], 'L2_xattn_bo': _L2_xattn_in['bo'], 'L2_ffn_w1_w': _L2_ffn_in['w1_w'], 'L2_ffn_w1_s': _L2_ffn_in['w1_s'], 'L2_ffn_w2_w': _L2_ffn_in['w2_w'], 'L2_ffn_w2_s': _L2_ffn_in['w2_s'], 'L2_ffn_h1_w': _L2_ffn_in['h1_w'], 'L2_ffn_h1_s': _L2_ffn_in['h1_s'], 'L2_ffn_h2_w': _L2_ffn_in['h2_w'], 'L2_ffn_h2_s': _L2_ffn_in['h2_s'], 'L2_ffn_w3_w': _L2_ffn_in['w3_w'], 'L2_ffn_w3_s': _L2_ffn_in['w3_s'], 'L3_xattn_qkv_w': _L3_xattn_in['qkv_w'], 'L3_xattn_qkv_b': _L3_xattn_in['qkv_b'], 'L3_xattn_sa_out_w': _L3_xattn_in['sa_out_w'], 'L3_xattn_sa_out_b': _L3_xattn_in['sa_out_b'], 'L3_xattn_in_proj_w': _L3_xattn_in['in_proj_w'], 'L3_xattn_in_proj_b': _L3_xattn_in['in_proj_b'], 'L3_xattn_mha_out_w': _L3_xattn_in['mha_out_w'], 'L3_xattn_mha_out_b': _L3_xattn_in['mha_out_b'], 'L3_xattn_lin1_w': _L3_xattn_in['lin1_w'], 'L3_xattn_lin1_b': _L3_xattn_in['lin1_b'], 'L3_xattn_lin2_w': _L3_xattn_in['lin2_w'], 'L3_xattn_lin2_b': _L3_xattn_in['lin2_b'], 'L3_xattn_ln1_g': _L3_xattn_in['ln1_g'], 'L3_xattn_ln1_b': _L3_xattn_in['ln1_b'], 'L3_xattn_ln2_g': _L3_xattn_in['ln2_g'], 'L3_xattn_ln2_b': _L3_xattn_in['ln2_b'], 'L3_xattn_ln3_g': _L3_xattn_in['ln3_g'], 'L3_xattn_ln3_b': _L3_xattn_in['ln3_b'], 'L3_ffn_sim_matrix': _L3_ffn_in['sim_matrix'], 'L3_ffn_gates': _L3_ffn_in['gates'], 'L3_ffn_q_proj': _L3_ffn_in['q_proj'], 'L3_ffn_k_proj': _L3_ffn_in['k_proj'], 'L3_ffn_v_proj': _L3_ffn_in['v_proj'], 'L3_ffn_o_proj': _L3_ffn_in['o_proj']}

def reference(x, ctx_1024, mask_BxSxS2_bf0, g_xattn, g_ffn, L0_xattn_ln1_g, L0_xattn_ln1_b, L0_xattn_ln2_g, L0_xattn_ln2_b, L0_xattn_Wq, L0_xattn_Wkv, L0_xattn_Wo, L0_ffn_gate_w, L0_ffn_gate_b, L0_ffn_expert_bias, L0_ffn_w1, L0_ffn_b1, L0_ffn_w2, L0_ffn_b2, L1_xattn_Wq, L1_xattn_bq, L1_xattn_Wk, L1_xattn_bk, L1_xattn_Wv, L1_xattn_bv, L1_ffn_in_proj_w, L1_ffn_in_proj_b, L1_ffn_out_w, L1_ffn_out_b, L1_ffn_ln1_g, L1_ffn_ln1_b, L1_ffn_router_w, L1_ffn_router_b, L1_ffn_w1, L1_ffn_b1, L1_ffn_w2, L1_ffn_b2, L1_ffn_ln2_g, L1_ffn_ln2_b, L2_xattn_Wq, L2_xattn_bq, L2_xattn_Wk, L2_xattn_bk, L2_xattn_Wv, L2_xattn_bv, L2_xattn_Wo, L2_xattn_bo, L2_ffn_w1_w, L2_ffn_w1_s, L2_ffn_w2_w, L2_ffn_w2_s, L2_ffn_h1_w, L2_ffn_h1_s, L2_ffn_h2_w, L2_ffn_h2_s, L2_ffn_w3_w, L2_ffn_w3_s, L3_xattn_qkv_w, L3_xattn_qkv_b, L3_xattn_sa_out_w, L3_xattn_sa_out_b, L3_xattn_in_proj_w, L3_xattn_in_proj_b, L3_xattn_mha_out_w, L3_xattn_mha_out_b, L3_xattn_lin1_w, L3_xattn_lin1_b, L3_xattn_lin2_w, L3_xattn_lin2_b, L3_xattn_ln1_g, L3_xattn_ln1_b, L3_xattn_ln2_g, L3_xattn_ln2_b, L3_xattn_ln3_g, L3_xattn_ln3_b, L3_ffn_sim_matrix, L3_ffn_gates, L3_ffn_q_proj, L3_ffn_k_proj, L3_ffn_v_proj, L3_ffn_o_proj):
    import jax
    import jax.numpy as jnp

    def _L0_xattn_ref(image_embeds, latents, ln1_g, ln1_b, ln2_g, ln2_b, Wq, Wkv, Wo):
        import jax, jax.numpy as jnp
        import numpy as np
        DIM = 128
        DIM_HEAD = 64
        HEADS = 16
        INNER = DIM_HEAD * HEADS
        EPS = 1e-05

        def layer_norm(x, g, b):
            m = jnp.mean(x, axis=-1, keepdims=True)
            v = jnp.mean(jnp.square(x - m), axis=-1, keepdims=True)
            return (x - m) * jax.lax.rsqrt(v + EPS) * g + b
        B, S_lat, _ = latents.shape
        x = layer_norm(image_embeds, ln1_g, ln1_b)
        l = layer_norm(latents, ln2_g, ln2_b)
        q = l @ Wq
        kv_in = jnp.concatenate([x, l], axis=1)
        kv = kv_in @ Wkv
        k, v = jnp.split(kv, 2, axis=-1)

        def to_heads(t):
            return t.reshape(t.shape[0], t.shape[1], HEADS, DIM_HEAD).transpose(0, 2, 1, 3)
        q, k, v = (to_heads(q), to_heads(k), to_heads(v))
        scale = 1.0 / np.sqrt(np.sqrt(DIM_HEAD))
        w = jnp.einsum('bhqd,bhkd->bhqk', q * scale, k * scale)
        w = jax.nn.softmax(w.astype(jnp.float32), axis=-1).astype(q.dtype)
        out = jnp.einsum('bhqk,bhkd->bhqd', w, v)
        out = out.transpose(0, 2, 1, 3).reshape(B, S_lat, INNER)
        return out @ Wo

    def _L0_ffn_ref(x, gate_w, gate_b, expert_bias, w1, b1, w2, b2):
        import jax, jax.numpy as jnp
        import numpy as np
        D_MODEL = 128
        D_FF = 512
        NUM_EXPERTS = 8
        gate_logits = jnp.einsum('bsd,ed->bse', x, gate_w) + gate_b + expert_bias
        top_idx = jnp.argmax(gate_logits, axis=-1)
        out = jnp.zeros_like(x)
        for e in range(NUM_EXPERTS):
            mask = (top_idx == e)[..., None].astype(x.dtype)
            h = jax.nn.relu(jnp.einsum('bsd,df->bsf', x, w1[e]) + b1[e])
            y = jnp.einsum('bsf,fd->bsd', h, w2[e]) + b2[e]
            out = out + mask * y
        return out

    def _L1_xattn_ref(input_seq, condition_seq, Wq, bq, Wk, bk, Wv, bv):
        import jax, jax.numpy as jnp
        import numpy as np
        B, SQ, SK, D = (4, 256, 256, 128)
        q = jnp.einsum('bsd,ed->bse', input_seq, Wq) + bq
        k = jnp.einsum('btd,ed->bte', condition_seq, Wk) + bk
        v = jnp.einsum('btd,ed->bte', condition_seq, Wv) + bv
        scores = jnp.einsum('bse,bte->bst', q, k)
        attn = jax.nn.softmax(scores, axis=-1)
        attended = jnp.einsum('bst,bte->bse', attn, v)
        return attended

    def _L1_ffn_ref(x, in_proj_w, in_proj_b, out_w, out_b, ln1_g, ln1_b, router_w, router_b, w1, b1, w2, b2, ln2_g, ln2_b):
        import jax, jax.numpy as jnp
        import numpy as np
        H = 16
        E = 8
        EPS = 1e-05

        def _layernorm(x, g, b):
            mu = jnp.mean(x, axis=-1, keepdims=True)
            var = jnp.mean(jnp.square(x - mu), axis=-1, keepdims=True)
            return (x - mu) * jax.lax.rsqrt(var + EPS) * g + b
        T, B, C = x.shape
        D = C // H
        qkv = x @ in_proj_w.T + in_proj_b
        q, k, v = jnp.split(qkv, 3, axis=-1)
        q = q.reshape(T, B, H, D)
        k = k.reshape(T, B, H, D)
        v = v.reshape(T, B, H, D)
        scale = 1.0 / np.sqrt(D).astype(np.float32)
        scores = jnp.einsum('tbhd,sbhd->bhts', q, k) * scale
        attn = jax.nn.softmax(scores, axis=-1)
        ctx = jnp.einsum('bhts,sbhd->tbhd', attn, v).reshape(T, B, C)
        attn_out = ctx @ out_w.T + out_b
        h = _layernorm(x + attn_out, ln1_g, ln1_b)
        flat = h.reshape(-1, C)
        logits = flat @ router_w.T + router_b
        probs = jax.nn.softmax(logits, axis=-1)
        _, top_i = jax.lax.top_k(probs, 2)
        assign = jnp.max(top_i, axis=-1)
        out = jnp.zeros_like(flat)
        for e in range(E):
            he = jax.nn.gelu(flat @ w1[e].T + b1[e], approximate=False)
            oe = he @ w2[e].T + b2[e]
            out = jnp.where((assign == e)[:, None], oe, out)
        moe_out = out.reshape(T, B, C)
        return _layernorm(h + moe_out, ln2_g, ln2_b)

    def _L2_xattn_ref(query, key, value, mask, Wq, bq, Wk, bk, Wv, bv, Wo, bo):
        import jax, jax.numpy as jnp
        import numpy as np
        import math
        B, LQ, LK = (2, 256, 256)
        DIM = 128
        H = 16
        DH = DIM // H
        b = query.shape[0]

        def shape(x):
            return x.reshape(b, -1, H, DH).transpose(0, 2, 1, 3)
        q = shape(query @ Wq.T + bq)
        k = shape(key @ Wk.T + bk)
        v = shape(value @ Wv.T + bv)
        q = q / math.sqrt(DH)
        scores = jnp.einsum('bhqd,bhkd->bhqk', q, k).astype(jnp.float32)
        scores = jnp.where(mask[:, None, :, :], jnp.float32(-1e+18), scores)
        attn = jax.nn.softmax(scores, axis=-1).astype(q.dtype)
        context = jnp.einsum('bhqk,bhkd->bhqd', attn, v)
        context = context.transpose(0, 2, 1, 3).reshape(b, -1, H * DH)
        return context @ Wo.T + bo

    def _L2_ffn_ref(x, w1_w, w1_s, w2_w, w2_s, h1_w, h1_s, h2_w, h2_s, w3_w, w3_s):
        import jax, jax.numpy as jnp
        import numpy as np
        D_IN, D_HID = (128, 512)

        def _ternary(key, shape):
            return jax.random.randint(key, shape, -1, 2).astype(jnp.float32)

        def _tlin(x, w, s):
            return jnp.einsum('bsi,oi->bso', x, w) * s
        h = jax.nn.silu(_tlin(x, w1_w, w1_s)) * _tlin(x, w2_w, w2_s)
        h = jax.nn.gelu(_tlin(h, h1_w, h1_s), approximate=False)
        h = jax.nn.gelu(_tlin(h, h2_w, h2_s), approximate=False)
        return _tlin(h, w3_w, w3_s)

    def _L3_xattn_ref(tgt, memory, qkv_w, qkv_b, sa_out_w, sa_out_b, in_proj_w, in_proj_b, mha_out_w, mha_out_b, lin1_w, lin1_b, lin2_w, lin2_b, ln1_g, ln1_b, ln2_g, ln2_b, ln3_g, ln3_b):
        import jax, jax.numpy as jnp
        import numpy as np
        B, NT, NM, C, H, FF = (8, 128, 256, 128, 8, 512)

        def _ln(x, g, b):
            m = x.mean(-1, keepdims=True)
            v = jnp.mean((x - m) ** 2, axis=-1, keepdims=True)
            return (x - m) / jnp.sqrt(v + 1e-05) * g + b
        Bx, N, Cx = tgt.shape
        qkv = tgt @ qkv_w.T + qkv_b
        q, k, v = jnp.split(qkv, 3, axis=-1)
        scores = jnp.einsum('bnc,bmc->bnm', q, k) * jnp.sqrt(jnp.float32(Cx))
        diag = jnp.eye(N, dtype=bool)
        scores = jnp.where(diag[None, :, :], scores, -jnp.inf)
        attn = jax.nn.softmax(scores, axis=-1)
        sa = jnp.einsum('bnm,bmc->bnc', attn, v) @ sa_out_w.T + sa_out_b
        x = _ln(tgt + sa, ln1_g, ln1_b)
        d = Cx // H
        wq, wk, wv = jnp.split(in_proj_w, 3, axis=0)
        bq, bk, bv = jnp.split(in_proj_b, 3, axis=0)
        qh = (x @ wq.T + bq).reshape(Bx, N, H, d).transpose(0, 2, 1, 3)
        kh = (memory @ wk.T + bk).reshape(Bx, -1, H, d).transpose(0, 2, 1, 3)
        vh = (memory @ wv.T + bv).reshape(Bx, -1, H, d).transpose(0, 2, 1, 3)
        a = jax.nn.softmax(jnp.einsum('bhnd,bhmd->bhnm', qh, kh) / jnp.sqrt(jnp.float32(d)), axis=-1)
        ca = jnp.einsum('bhnm,bhmd->bhnd', a, vh).transpose(0, 2, 1, 3).reshape(Bx, N, Cx)
        ca = ca @ mha_out_w.T + mha_out_b
        x = _ln(x + ca, ln2_g, ln2_b)
        ff = jax.nn.relu(x @ lin1_w.T + lin1_b) @ lin2_w.T + lin2_b
        return _ln(x + ff, ln3_g, ln3_b)

    def _L3_ffn_ref(hidden_states, sim_matrix, gates, q_proj, k_proj, v_proj, o_proj):
        import jax, jax.numpy as jnp
        import numpy as np
        HIDDEN = 128
        HEAD_DIM = 64
        N_EXPERTS = 16
        MIN_EXPERTS = 2
        B, T = (4, 256)

        def _normalize(x, axis):
            n = jnp.sqrt(jnp.sum(x * x, axis=axis, keepdims=True))
            return x / jnp.maximum(n, 1e-12)

        def _ste(x):
            hard = jax.lax.stop_gradient((x > 0).astype(x.dtype))
            return hard + x - jax.lax.stop_gradient(x)

        def _gating(hidden_states, sim_matrix, gates):
            b, t, c = hidden_states.shape
            flat = hidden_states.reshape(b * t, c)
            logits = _normalize(flat, -1) @ _normalize(sim_matrix, 0) - jax.nn.sigmoid(gates)
            gated = jax.nn.relu(logits)
            mask = _ste(gated)
            inactive = jnp.sum(mask, axis=1) == 0
            _, fb_idx = jax.lax.top_k(logits, MIN_EXPERTS)
            fb = jnp.zeros_like(mask).at[jnp.arange(b * t)[:, None], fb_idx].set(1.0)
            fb_applied = inactive[:, None] & (fb > 0)
            mask = jnp.where(fb_applied, 1.0, mask)
            masked_logits = jnp.where(mask > 0, gated, -jnp.inf)
            return jax.nn.softmax(masked_logits, axis=-1).reshape(b, t, -1)
        b, t, c = hidden_states.shape
        rw = _gating(hidden_states, sim_matrix, gates)
        q = jnp.einsum('bte,bted->btd', rw, jnp.einsum('btc,ecd->bted', hidden_states, q_proj))
        k = jnp.einsum('bte,bted->btd', rw, jnp.einsum('btc,ecd->bted', hidden_states, k_proj))
        v = jnp.einsum('bte,bted->btd', rw, jnp.einsum('btc,ecd->bted', hidden_states, v_proj))
        scale = 1.0 / jnp.sqrt(jnp.asarray(HEAD_DIM, dtype=q.dtype))
        scores = jnp.einsum('bqd,bkd->bqk', q, k) * scale
        causal = jnp.tril(jnp.ones((t, t), dtype=bool))
        scores = jnp.where(causal, scores, -jnp.inf)
        attn = jnp.einsum('bqk,bkd->bqd', jax.nn.softmax(scores, axis=-1), v)
        mixed = attn[:, :, None, :] * rw[..., None]
        return jnp.einsum('bted,edc->btc', mixed, o_proj)
    x = x + jnp.tanh(g_xattn[0]) * _L0_xattn_ref(ctx_1024, _layernorm(x, axis=-1), L0_xattn_ln1_g, L0_xattn_ln1_b, L0_xattn_ln2_g, L0_xattn_ln2_b, L0_xattn_Wq, L0_xattn_Wkv, L0_xattn_Wo)
    x = x + jnp.tanh(g_ffn[0]) * _L0_ffn_ref(_layernorm(x, axis=-1), L0_ffn_gate_w, L0_ffn_gate_b, L0_ffn_expert_bias, L0_ffn_w1, L0_ffn_b1, L0_ffn_w2, L0_ffn_b2)
    x = x + jnp.tanh(g_xattn[1]) * _L1_xattn_ref(_layernorm(x, axis=-1), ctx_1024, L1_xattn_Wq, L1_xattn_bq, L1_xattn_Wk, L1_xattn_bk, L1_xattn_Wv, L1_xattn_bv)
    x = x + jnp.tanh(g_ffn[1]) * _L1_ffn_ref(_layernorm(x, axis=-1), L1_ffn_in_proj_w, L1_ffn_in_proj_b, L1_ffn_out_w, L1_ffn_out_b, L1_ffn_ln1_g, L1_ffn_ln1_b, L1_ffn_router_w, L1_ffn_router_b, L1_ffn_w1, L1_ffn_b1, L1_ffn_w2, L1_ffn_b2, L1_ffn_ln2_g, L1_ffn_ln2_b)
    x = x + jnp.tanh(g_xattn[2]) * _L2_xattn_ref(_layernorm(x, axis=-1), ctx_1024, ctx_1024, mask_BxSxS2_bf0, L2_xattn_Wq, L2_xattn_bq, L2_xattn_Wk, L2_xattn_bk, L2_xattn_Wv, L2_xattn_bv, L2_xattn_Wo, L2_xattn_bo)
    x = x + jnp.tanh(g_ffn[2]) * _L2_ffn_ref(_layernorm(x, axis=-1), L2_ffn_w1_w, L2_ffn_w1_s, L2_ffn_w2_w, L2_ffn_w2_s, L2_ffn_h1_w, L2_ffn_h1_s, L2_ffn_h2_w, L2_ffn_h2_s, L2_ffn_w3_w, L2_ffn_w3_s)
    x = x + jnp.tanh(g_xattn[3]) * _L3_xattn_ref(_layernorm(x, axis=-1), ctx_1024, L3_xattn_qkv_w, L3_xattn_qkv_b, L3_xattn_sa_out_w, L3_xattn_sa_out_b, L3_xattn_in_proj_w, L3_xattn_in_proj_b, L3_xattn_mha_out_w, L3_xattn_mha_out_b, L3_xattn_lin1_w, L3_xattn_lin1_b, L3_xattn_lin2_w, L3_xattn_lin2_b, L3_xattn_ln1_g, L3_xattn_ln1_b, L3_xattn_ln2_g, L3_xattn_ln2_b, L3_xattn_ln3_g, L3_xattn_ln3_b)
    x = x + jnp.tanh(g_ffn[3]) * _L3_ffn_ref(_layernorm(x, axis=-1), L3_ffn_sim_matrix, L3_ffn_gates, L3_ffn_q_proj, L3_ffn_k_proj, L3_ffn_v_proj, L3_ffn_o_proj)
    return x

_drawn_inputs = setup_inputs


def setup_inputs(seed=0):
    import zlib

    import numpy as np

    out = dict(_drawn_inputs(seed))
    spreads = {'L0_xattn_ln1_g': (1.0, 0.2),
     'L0_xattn_ln1_b': (0.0, 0.1),
     'L0_xattn_ln2_g': (1.0, 0.2),
     'L0_xattn_ln2_b': (0.0, 0.1),
     'L0_ffn_expert_bias': (0.0, 0.1),
     'L1_xattn_bq': (0.0, 0.1),
     'L1_xattn_bk': (0.0, 0.1),
     'L1_xattn_bv': (0.0, 0.1),
     'L1_ffn_in_proj_b': (0.0, 0.1),
     'L1_ffn_out_b': (0.0, 0.1),
     'L1_ffn_ln1_g': (1.0, 0.2),
     'L1_ffn_ln1_b': (0.0, 0.1),
     'L1_ffn_router_b': (0.0, 0.1),
     'L1_ffn_b1': (0.0, 0.1),
     'L1_ffn_b2': (0.0, 0.1),
     'L1_ffn_ln2_g': (1.0, 0.2),
     'L1_ffn_ln2_b': (0.0, 0.1),
     'L3_xattn_qkv_b': (0.0, 0.1),
     'L3_xattn_sa_out_b': (0.0, 0.1),
     'L3_xattn_in_proj_b': (0.0, 0.1),
     'L3_xattn_mha_out_b': (0.0, 0.1),
     'L3_xattn_lin1_b': (0.0, 0.1),
     'L3_xattn_lin2_b': (0.0, 0.1),
     'L3_xattn_ln1_g': (1.0, 0.2),
     'L3_xattn_ln1_b': (0.0, 0.1),
     'L3_xattn_ln2_g': (1.0, 0.2),
     'L3_xattn_ln2_b': (0.0, 0.1),
     'L3_xattn_ln3_g': (1.0, 0.2),
     'L3_xattn_ln3_b': (0.0, 0.1),
     'L3_ffn_gates': (0.0, 0.1)}
    factors = {}
    for name, (base, spread) in spreads.items():
        noise = np.random.default_rng([zlib.crc32(name.encode()), seed]).standard_normal(out[name].shape)
        drawn = base * np.exp(spread * noise) if base else spread * noise
        out[name] = jnp.asarray(drawn.astype(out[name].dtype))
    for name, factor in factors.items():
        out[name] = (out[name] * factor).astype(out[name].dtype)
    return out
```

```python
from contextlib import ExitStack

import numpy as np

import concourse.bass as bass
from concourse import mybir

ALU = mybir.AluOpType
ACT = mybir.ActivationFunctionType
F32 = mybir.dt.float32
BF16 = mybir.dt.bfloat16
U8 = mybir.dt.uint8
U16 = mybir.dt.uint16
AX_X = mybir.AxisListType.X

P = 128
BATCH, SEQ, CTX = 4, 512, 154
TOKENS = BATCH * SEQ
TILES = TOKENS // P
QT = SEQ // P
CTX_ROWS = BATCH * CTX
CTX_TILES = -(-CTX_ROWS // P)
CTX_LAST = CTX_ROWS - (CTX_TILES - 1) * P
CTX_REST = CTX - P
BANK = 512
EPS = 1e-5
MASKED = -1e18
CAUSAL = -1e30

H0, D0 = 16, 64
PAIRS = H0 // 2
KEYS0 = SEQ + CTX
KT0 = -(-KEYS0 // P)
EXPERTS, FF = 8, 512
FT = FF // P
E3, D3 = 16, 64


def _cols(v):
    return v.reshape(-1, P).T


def _kt(w):
    k = w.shape[0] // P
    return w.reshape(k, P, -1).transpose(1, 0, 2).reshape(P, -1)


WEIGHTS = [
    {
        "ln1_g": (1, lambda i: _cols(i["L0_xattn_ln1_g"])), "ln1_b": (1, lambda i: _cols(i["L0_xattn_ln1_b"])),
        "ln2_g": (1, lambda i: _cols(i["L0_xattn_ln2_g"])), "ln2_b": (1, lambda i: _cols(i["L0_xattn_ln2_b"])),
        "wq": (1024, lambda i: i["L0_xattn_Wq"]), "wkv": (2048, lambda i: i["L0_xattn_Wkv"]),
        "wo": (1024, lambda i: _kt(i["L0_xattn_Wo"])),
    },
    {
        "gate": (EXPERTS, lambda i: i["L0_ffn_gate_w"].T),
        "w1": (EXPERTS * FF, lambda i: i["L0_ffn_w1"].transpose(1, 0, 2).reshape(P, -1)),
        "b1": (EXPERTS * FT, lambda i: _cols(i["L0_ffn_b1"].reshape(-1))),
        "w2": (EXPERTS * FF, lambda i: _kt(i["L0_ffn_w2"].reshape(-1, P))),
    },
    {
        "wq": (P, lambda i: i["L1_xattn_Wq"].T), "wk": (P, lambda i: i["L1_xattn_Wk"].T),
        "wv": (P, lambda i: i["L1_xattn_Wv"].T),
        "bq": (1, lambda i: _cols(i["L1_xattn_bq"])), "bk": (1, lambda i: _cols(i["L1_xattn_bk"])),
    },
    {
        "in": (3 * P, lambda i: i["L1_ffn_in_proj_w"].T), "out": (P, lambda i: i["L1_ffn_out_w"].T),
        "router": (EXPERTS, lambda i: i["L1_ffn_router_w"].T),
        "w1": (EXPERTS * P, lambda i: i["L1_ffn_w1"].transpose(2, 0, 1).reshape(P, -1)),
        "w2": (EXPERTS * P, lambda i: i["L1_ffn_w2"].transpose(2, 0, 1).reshape(P, -1)),
        "b1": (EXPERTS, lambda i: i["L1_ffn_b1"].T),
    },
    {
        "wq": (P, lambda i: i["L2_xattn_Wq"].T), "wk": (P, lambda i: i["L2_xattn_Wk"].T),
        "wv": (P, lambda i: i["L2_xattn_Wv"].T), "wo": (P, lambda i: i["L2_xattn_Wo"].T),
        "bq": (1, lambda i: _cols(i["L2_xattn_bq"])), "bk": (1, lambda i: _cols(i["L2_xattn_bk"])),
        "bv": (1, lambda i: _cols(i["L2_xattn_bv"])),
    },
    {
        "w1": (FF, lambda i: i["L2_ffn_w1_w"].T), "w2": (FF, lambda i: i["L2_ffn_w2_w"].T),
        "h1": (FT * FF, lambda i: _kt(i["L2_ffn_h1_w"].T)), "h2": (FT * FF, lambda i: _kt(i["L2_ffn_h2_w"].T)),
        "w3": (FT * P, lambda i: _kt(i["L2_ffn_w3_w"].T)),
        "s1": (FT, lambda i: _cols(i["L2_ffn_w1_s"])), "s2": (FT, lambda i: _cols(i["L2_ffn_w2_s"])),
        "sh1": (FT, lambda i: _cols(i["L2_ffn_h1_s"])), "sh2": (FT, lambda i: _cols(i["L2_ffn_h2_s"])),
    },
    {
        "qkv": (3 * P, lambda i: i["L3_xattn_qkv_w"].T), "sa_out": (P, lambda i: i["L3_xattn_sa_out_w"].T),
        "in": (3 * P, lambda i: i["L3_xattn_in_proj_w"].T), "mha_out": (P, lambda i: i["L3_xattn_mha_out_w"].T),
        "lin1": (FF, lambda i: i["L3_xattn_lin1_w"].T), "lin2": (FT * P, lambda i: _kt(i["L3_xattn_lin2_w"].T)),
        "in_b": (3, lambda i: _cols(i["L3_xattn_in_proj_b"])), "lin1_b": (FT, lambda i: _cols(i["L3_xattn_lin1_b"])),
    },
    {
        "sim": (E3, lambda i: i["L3_ffn_sim_matrix"]),
        "qk": (E3 * 2 * D3, lambda i: np.concatenate([i["L3_ffn_q_proj"], i["L3_ffn_k_proj"]], 2)
               .transpose(1, 0, 2).reshape(P, -1)),
        "v": (E3 * D3, lambda i: i["L3_ffn_v_proj"].transpose(1, 0, 2).reshape(P, -1)),
        "o": (E3 // 2 * P, lambda i: _kt(i["L3_ffn_o_proj"].reshape(-1, P))),
    },
]

ROWS = {
    "g_xattn": 4, "g_ffn": 4, "L0_ffn_gate_b": 8, "L0_ffn_expert_bias": 8, "L1_xattn_bv": P,
    "L1_ffn_in_proj_b": 3 * P, "L1_ffn_out_b": P, "L1_ffn_ln1_g": P, "L1_ffn_ln1_b": P, "L1_ffn_router_b": 8,
    "L1_ffn_ln2_g": P, "L1_ffn_ln2_b": P, "L2_xattn_bo": P, "L2_ffn_w3_s": P, "L3_xattn_qkv_b": 3 * P,
    "L3_xattn_sa_out_b": P, "L3_xattn_mha_out_b": P, "L3_xattn_lin2_b": P, "L3_xattn_ln1_g": P,
    "L3_xattn_ln1_b": P, "L3_xattn_ln2_g": P, "L3_xattn_ln2_b": P, "L3_xattn_ln3_g": P, "L3_xattn_ln3_b": P,
    "L3_ffn_gates": 16,
}


def _offsets(widths):
    at, out = 0, {}
    for name, n in widths.items():
        out[name] = (at, n)
        at += n
    return out, at


def flat_chunks(heads):
    n = heads * CTX
    return [(c * P, min(P, n - c * P)) for c in range(-(-n // P))]


def constants():
    eye = np.eye(P, dtype=np.float32)
    c = {"eye": eye}
    for heads in (16, 8):
        d = P // heads
        c[f"head{heads}"] = (np.arange(P)[:, None] // d == np.arange(heads)[None]).astype(np.float32)
        chunks = flat_chunks(heads)
        m = np.zeros((P, len(chunks), heads), np.float32)
        for n, (f0, rows) in enumerate(chunks):
            for r in range(rows):
                m[r, n, (f0 + r) // CTX] = 1.0
        c[f"block{heads}"] = m.reshape(P, -1)
    c["down8"] = np.tile(np.arange(8, 0, -1, dtype=np.float32), (P, 1))
    c["down16"] = np.tile(np.arange(16, 0, -1, dtype=np.float32), (P, 1))
    c["fold"] = np.tile(np.eye(D3, dtype=np.float32), (2, 2))
    b = {"eye_b": eye}
    b["causal"] = np.where(np.arange(P)[None] <= np.arange(P)[:, None], 0.0, CAUSAL).astype(np.float32)
    one = np.zeros((P, E3, P), np.float32)
    two = np.zeros((P, E3 // 2, P), np.float32)
    for part in range(3):
        for e in range(E3):
            one[32 * part + e, e, :] = 1.0
            two[32 * part + e, e // 2, (e % 2) * D3:(e % 2 + 1) * D3] = 1.0
    b["spread1"], b["spread2"] = one.reshape(P, -1), two.reshape(P, -1)
    f = np.concatenate(list(c.values()), 1)
    bb = (np.concatenate(list(b.values()), 1).view(np.uint32) >> 16).astype(np.uint16)
    return f, {k: v.shape[1] for k, v in c.items()}, bb, {k: v.shape[1] for k, v in b.items()}


class Step:

    def __init__(self, engine, emit, after):
        self.engine, self.emit, self.after = engine, emit, after
        self.sem, self.value, self.wanted = None, None, False


def _flat(after):
    for a in after:
        if isinstance(a, (list, tuple)):
            yield from _flat(a)
        elif a is not None:
            yield a


class Engine:
    def __init__(self, name):
        self.name, self.queue, self.sem = name, [], None

    def do(self, emit, *after):
        step = Step(self, emit, list(_flat(after)))
        for a in step.after:
            a.wanted = True
        step.sem = self.sem
        self.queue.append(step)
        return step

    def count(self):
        at = {}
        for s in self.queue:
            if s.wanted and s.value is None:
                at[s.sem] = at.get(s.sem, 0) + 1
                s.value = at[s.sem]

    def run(self, eng):
        seen = {}
        for s in self.queue:
            need = {}
            for a in s.after:
                need[a.sem] = max(need.get(a.sem, 0), a.value)
            for sem, value in need.items():
                if seen.get(sem, 0) < value:
                    eng.wait_ge(sem, value)
                    seen[sem] = value
            last = s.emit(eng)
            if s.wanted:
                last.then_inc(s.sem, 16 if isinstance(s, Load) else 1)


class Load(Step):
    pass


class Bank:

    def __init__(self, ap):
        self.ap, self.free = ap, []


class Ring:

    def __init__(self, aps):
        self.slots, self.at = [Bank(a) for a in aps], -1

    def next(self):
        self.at = (self.at + 1) % len(self.slots)
        return self.slots[self.at]


class Program:
    def __init__(self, nc, ctx, dram, const_widths, const_b_widths):
        self.nc, self.ctx, self.dram = nc, ctx, dram
        self.pe, self.ve, self.ac, self.po, self.sp = (Engine(n) for n in
                                                       ("tensor", "vector", "scalar", "gpsimd", "sync"))
        self.engines = [self.pe, self.ve, self.ac, self.po, self.sp]
        self.loads = []
        self.widths = {"const": const_widths, "const_b": const_b_widths}
        self.evacuations = 0

    def sb(self, name, shape, dt=F32):
        return self.ctx.enter_context(self.nc.sbuf_tensor(name, shape, dt))

    def stage(self, name):
        for e in self.engines[:4]:
            e.sem = self.ctx.enter_context(self.nc.semaphore(f"{e.name}_{name}"))

    def load_sem(self, name):
        return self.ctx.enter_context(self.nc.semaphore(f"dma_{name}"))

    def dma(self, name, out, in_, *after, sem=None, turn=1, engine=None):
        engine = engine or self.sp
        step = Load(engine, lambda e: e.dma_start(out, in_), list(_flat(after)))
        for a in step.after:
            a.wanted = True
        step.sem = sem or self.load_sem(name)
        step.value, step.wanted = 16 * turn, True
        engine.queue.append(step)
        self.loads.append(step)
        return step

    def evacuate(self, out, psum, *after):
        self.evacuations += 1
        if self.evacuations % 2:
            return self.ac.do(lambda e: e.activation(out, psum, ACT.Copy), *after)
        return self.ve.do(lambda e: e.tensor_copy(out, psum), *after)

    def finish(self):
        for e in self.engines:
            e.count()
        with self.nc.Block() as block:
            for e in self.engines:
                place = {"tensor": block.tensor, "vector": block.vector, "scalar": block.scalar,
                         "gpsimd": block.gpsimd, "sync": block.sync}[e.name]
                place(lambda eng, e=e: e.run(eng))

    def carve(self, *shape, dt=F32):
        n = int(np.prod(shape))
        words = n if dt == F32 else -(-n // 2)
        ap = self.work[:, self.work_at:self.work_at + words]
        self.work_at += words
        assert self.work_at <= self.work_words, self.work_at
        if dt != F32:
            ap = ap.bitcast(dt)
        if len(shape) == 2:
            return ap.rearrange("p (a b) -> p a b", a=shape[0])
        if len(shape) == 3:
            return ap.rearrange("p (a b c) -> p a b c", a=shape[0], b=shape[1])
        if len(shape) == 4:
            return ap.rearrange("p (a b c d) -> p a b c d", a=shape[0], b=shape[1], c=shape[2])
        return ap

    def begin(self, name):
        before = [e.queue[-1] for e in self.engines[:4] if e.queue]
        self.stage(name)
        self.work_at = 0
        self.before = before
        for e in self.engines[:4]:
            e.fence = e.do(lambda g: g.nop(), *before)

    def norm_groups(self, src, dst, ready, n=TILES, rows=P, gain=None, bias=None):
        ve, po = self.ve, self.po
        stats, mv = self.carve(n, 6), self.carve(n, 2)
        var, rstd = self.carve(n), self.carve(n)
        full = n if rows == P else n - 1
        groups = [(P, a, min(a + QT, full)) for a in range(0, full, QT)] + ([(rows, full, n)] if full < n else [])
        out, power = [None] * n, {}

        def measure(r, a, b):
            for t in range(a, b):
                s = ve.do(lambda e, t=t: e.bn_stats(stats[0:r, t, :], src[0:r, t, :]), ready[t])
            for t in range(a, b):
                m = ve.do(lambda e, t=t: e.bn_aggr(mv[0:r, t, :], stats[0:r, t, :]), s)
            s = ve.do(lambda e: e.tensor_scalar(var[0:r, a:b], mv[0:r, a:b, 1], EPS, None, ALU.add), m)
            power[a] = po.do(lambda e: e.tensor_tensor(rstd[0:r, a:b], var[0:r, a:b], self.minus_half[0:r, 0:b - a], ALU.pow),
                             s, self.halves)

        def scale(r, a, b):
            for t in range(a, b):
                out[t] = ve.do(lambda e, t=t: e.tensor_scalar(dst[0:r, t, :], src[0:r, t, :], mv[0:r, t, 0:1],
                                                              rstd[0:r, t:t + 1], ALU.subtract, ALU.mult), power[a])
            if gain is not None:
                o, wide = dst[0:r, a:b, :], [r, b - a, P]
                s = ve.do(lambda e: e.tensor_tensor(o, o, gain[0:r].unsqueeze(1).to_broadcast(wide), ALU.mult), out[a:b])
                s = ve.do(lambda e: e.tensor_tensor(o, o, bias[0:r].unsqueeze(1).to_broadcast(wide), ALU.add), s)
                out[a:b] = [s] * (b - a)

        return [(lambda g=g: measure(*g), lambda g=g: scale(*g)) for g in groups], out

    def normalize(self, *args, **kwargs):
        groups, out = self.norm_groups(*args, **kwargs)
        last = None
        for measure, scale in groups:
            measure()
            if last:
                last()
            last = scale
        last()
        return out

    def turn(self, src, dst, ready, rows=P, n=TILES, scale=None, shift=None, after=()):
        out = []
        for g in range(0, n, 4):
            bank = self.banks.next()
            tiles = range(g, min(g + 4, n))
            width = sum(rows if t == n - 1 else P for t in tiles)
            for t in tiles:
                r = rows if t == n - 1 else P
                s = self.pe.do(lambda e, t=t, r=r, c=(t - g) * P, b=bank.ap: e.transpose(
                    b[:, c:c + r], src[0:r, t, :], self.eye[0:r, 0:r]), ready[t], bank.free, self.setup)
            o, i = dst[:, g * P:g * P + width], bank.ap[:, 0:width]
            if scale is not None:
                if (g // 4) % 2:
                    v = self.ve.do(lambda e, o=o, i=i: e.tensor_scalar(o, i, scale, shift, ALU.mult, ALU.add), s, *after)
                else:
                    v = self.ac.do(lambda e, o=o, i=i: e.activation(o, i, ACT.Identity, bias=shift, scale=scale), s, *after)
            else:
                v = self.evacuate(o, i, s, *after)
            bank.free = [v]
            out += [v] * len(tiles)
        return out

    def add_to_x(self, tile, psum, gate, ready, row=None, factor=None, op=ALU.add):
        ve, x = self.ve, self.x[:, tile, :]
        g = self.gates[:, gate:gate + 1]
        if row is None:
            self.x_last[tile] = ve.do(lambda e: e.scalar_tensor_tensor(x, psum, g, x, ALU.mult, ALU.add),
                                      ready, self.x_last[tile], self.rows_ready)
            return self.x_last[tile]
        t = self.scratch[:, tile % 4, :]
        if factor is None:
            s = ve.do(lambda e: e.tensor_tensor(t, psum, row, op), ready, self.rows_ready, self.scratch_free[tile % 4])
        else:
            s = ve.do(lambda e: e.scalar_tensor_tensor(t, psum, factor, row, ALU.mult, ALU.add), ready,
                      self.scratch_free[tile % 4])
        self.x_last[tile] = ve.do(lambda e: e.scalar_tensor_tensor(x, t, g, x, ALU.mult, ALU.add), s, self.x_last[tile])
        self.scratch_free[tile % 4] = self.x_last[tile]
        return s

    def open(self):
        ve, po, pe, nc = self.ve, self.po, self.pe, self.nc
        self.stage("setup")
        d = self.dram
        psum = self.ctx.enter_context(nc.psum_tensor("banks", [P, 8 * BANK], F32))
        self.psum = psum
        self.banks = Ring([psum[:, b * BANK:(b + 1) * BANK] for b in range(8)])
        self.x = self.sb("x", [P, TILES, P])
        self.xn = self.sb("xn", [P, TILES, P])
        self.xt = self.sb("xt", [P, TOKENS])
        self.context = self.sb("context", [P, BATCH, 2 * CTX])
        self.scratch = self.sb("scratch", [P, 4, P])
        self.gates = self.sb("gates", [P, 8])
        self.x_last = [None] * TILES
        self.scratch_free = [None] * 4
        self.minus_half = self.sb("minus_half", [P, TILES])
        self.half = self.sb("half", [P, TILES])
        slots = {"a": self.sb("weights_a", [P, 4116]), "b": self.sb("weights_b", [P, 8232]),
                 "c": self.sb("weights_c", [P, 3480])}
        self.work_words = 21800
        self.work = self.sb("work", [P, self.work_words])
        const, cw = self.sb("const", [P, sum(self.widths["const"].values())]), self.widths["const"]
        cb = self.sb("const_b", [P, sum(self.widths["const_b"].values())], BF16)
        rows_at, rows_n = _offsets(ROWS)
        rows = self.sb("rows", [P, rows_n])
        self.small = self.sb("small", [8, 2 * P])
        self.row = {k: rows[:, a:a + n] for k, (a, n) in rows_at.items()}
        self.c = {k: const[:, a:a + n] for k, (a, n) in _offsets(cw)[0].items()}
        self.cb = {k: cb[:, a:a + n] for k, (a, n) in _offsets(self.widths["const_b"])[0].items()}
        self.eye = self.c["eye"]

        self.w, self.w_ready, self.weight_plan = [], [], []
        for k, (slot, base) in enumerate([("a", 0), ("b", 0), ("c", 0), ("c", 386), ("c", 386 + 2576),
                                          ("b", 0), ("b", 5648), ("a", 0)]):
            at, n = _offsets({name: w for name, (w, _) in WEIGHTS[k].items()})
            assert base + n <= slots[slot].shape[1], (k, base + n)
            self.w.append({name: slots[slot][:, base + a:base + a + m] for name, (a, m) in at.items()})
            self.weight_plan.append((slots[slot][:, base:base + n], d[f"weights{k}"]))

        self.begin_work()
        self.ctx_rows = ctx_rows = self.carve(CTX_TILES, P)
        xr = d["x"].rearrange("(t p) d -> p t d", p=P)
        self.load_x = [self.dma(f"x{b}", self.x[:, QT * b:QT * b + QT, :], xr[:, QT * b:QT * b + QT, :])
                       for b in range(BATCH)]
        load_c = self.dma("const", const[:, :], d["const"])
        full = CTX_TILES - 1
        self.load_ctx = [self.dma("context", ctx_rows[:, 0:full, :],
                                  d["ctx"][0:full * P, :].rearrange("(t p) d -> p t d", p=P)),
                         self.dma("context_last", ctx_rows[0:CTX_LAST, full, :], d["ctx"][full * P:CTX_ROWS, :])]
        self.load_weights(0)
        load_rows = self.dma("rows", rows[:, :], d["rows"].to_broadcast([P, rows_n]))
        load_cb = self.dma("const_b", cb[:, :].bitcast(U16), d["const_b"])
        load_small = self.dma("small", self.small[:, :], d["small"])
        for k in (1, 2, 3, 4):
            self.load_weights(k)

        halves = [po.do(lambda e: e.memset(self.minus_half[:, :], -0.5)), po.do(lambda e: e.memset(self.half[:, :], 0.5))]
        clean = ve.do(lambda e: e.memset(psum[:, 5 * BANK:6 * BANK], 0.0))
        self.setup, self.halves = [load_c, clean], halves
        self.ctxn_t = self.sb("ctxn_t", [P, CTX_ROWS])

        def late():
            tanh = self.ac.do(lambda e: e.activation(self.gates[:, :], rows[:, 0:8], ACT.Tanh), load_rows)
            self.rows_ready = [load_rows, load_small, load_cb, tanh]
        self.late_tables = late

    def open_context(self):
        ctxn, whole = self.carve(CTX_TILES, P), self.carve(CTX_ROWS)
        w, ve = self.w[0], self.ve
        ready = self.normalize(self.ctx_rows, ctxn, [self.load_ctx] * CTX_TILES, CTX_TILES, CTX_LAST)
        self.ctxn_ready = self.turn(ctxn, self.ctxn_t, ready, rows=CTX_LAST, n=CTX_TILES,
                                    scale=w["ln1_g"], shift=w["ln1_b"], after=(self.w_ready[0],))
        turned = self.turn(self.ctx_rows, whole, [self.load_ctx] * CTX_TILES, rows=CTX_LAST, n=CTX_TILES)
        by_batch = whole.rearrange("p (b k) -> p b k", b=BATCH)
        self.context_ready = [self.po.do(lambda e, c=c: e.tensor_copy(self.context[:, :, c * CTX:(c + 1) * CTX], by_batch),
                                         turned) for c in range(2)]

    def begin_work(self):
        self.work_at = 0

    def load_weights(self, k, *after):
        out, src = self.weight_plan[k]
        self.w_ready += [None] * (k + 1 - len(self.w_ready))
        self.w_ready[k] = self.dma(f"weights{k}", out, src, *after)

    def image_attention(self):
        pe, ve, ac, po = self.pe, self.ve, self.ac, self.po
        w, x = self.w[0], self.x
        first = self.normalize(x[:, 0:QT, :], self.xn[:, 0:QT, :], [self.load_x[0]] * QT, QT)
        second = self.normalize(self.xn[:, 0:QT, :], self.xn[:, 0:QT, :], first, QT)
        ln2 = {"scale": w["ln2_g"], "shift": w["ln2_b"], "after": (self.w_ready[0],)}
        latents = self.turn(self.xn[:, 0:QT, :], self.xt[:, 0:SEQ], second, n=QT, **ln2)
        self.open_context()
        self.begin("image")

        q_split = Ring([self.carve(2, SEQ, dt=BF16) for _ in range(2)])
        k_split = Ring([self.carve(2, 2, KEYS0, dt=BF16) for _ in range(2)])
        values = Ring([self.carve(KT0, P) for _ in range(3)])
        probs = Ring([self.carve(KEYS0) for _ in range(4)])
        probs_t = Ring([self.carve(2, KT0, 2 * P) for _ in range(2)])
        sums = Ring([self.carve(4) for _ in range(2)])
        inverse = Ring([self.carve(4) for _ in range(2)])
        spread = Ring([self.carve(2, 2, D0) for _ in range(2)])
        neg_max = Ring([self.carve(1) for _ in range(4)])
        mixed = self.carve(PAIRS, SEQ)
        mixed_free = [None, None]
        scores = Ring([self.psum[:, 0:2 * BANK], self.psum[:, 2 * BANK:4 * BANK]])
        turned = [Bank(self.psum[:, 4 * BANK:5 * BANK]), Bank(self.psum[:, 5 * BANK:6 * BANK])]
        out_bank = Bank(self.psum[:, 6 * BANK:7 * BANK])
        side = Bank(self.psum[:, 7 * BANK:8 * BANK])
        for bank in (*scores.slots, *turned, out_bank, side):
            bank.free = [b.free for b in self.banks.slots]
        self.banks = Ring([])
        self.banks.slots = turned

        copy_sems = {(s, h): self.load_sem(f"keys{s}{h}") for s in range(2) for h in range(2)}
        copy_turn = {key: 0 for key in copy_sems}
        groups = [(b, p) for b in range(BATCH) for p in range(PAIRS)]
        state = {}

        def project_q(g, n):
            b, p = g
            st = state[g] = {"q": q_split.next(), "k": k_split.next(), "v": values.next(), "n": n}
            m = pe.do(lambda e: e.matmul(side.ap[:, 0:SEQ], w["wq"][:, p * P:(p + 1) * P],
                                         self.xt[:, b * SEQ:(b + 1) * SEQ], start=True, stop=True),
                      latents[4 * b + 3], side.free)
            q, hi = st["q"].ap, []
            for h in (0, 1):
                own = slice(64 * h, 64 * h + 64)
                hi.append(ac.do(lambda e, h=h, own=own: e.activation(q[own, h, :], side.ap[own, 0:SEQ], ACT.Copy, scale=D0 ** -0.5),
                                m, st["q"].free))
            side.free = [None]

            def low(h):
                own, other = slice(64 * h, 64 * h + 64), slice(64 - 64 * h, 128 - 64 * h)
                return ve.do(lambda e, h=h, own=own, other=other: e.scalar_tensor_tensor(
                    q[other, h, :], side.ap[own, 0:SEQ], D0 ** -0.5, q[own, h, :], ALU.mult, ALU.subtract), hi[h], st["q"].free)

            def rest():
                for h in (0, 1):
                    st[f"q{h}"] = low(h)
                side.free = [hi, st["q0"], st["q1"]]
            return rest

        def project_k(g, part):
            b, p = g
            st = state[g]
            src, n, c0 = ((self.xt[:, b * SEQ:(b + 1) * SEQ], SEQ, 0) if part == 0 else
                          (self.ctxn_t[:, b * CTX:(b + 1) * CTX], CTX, SEQ))
            m = pe.do(lambda e: e.matmul(side.ap[:, 0:n], w["wkv"][:, p * P:(p + 1) * P], src, start=True, stop=True),
                      side.free, self.ctxn_ready if part else None)
            if part == 1:
                for c, r0, rows in ((P * 2, 0, P), (P * 3, P, CTX_REST)):
                    m = pe.do(lambda e, c=c, r0=r0, rows=rows: e.matmul(
                        side.ap[0:rows, c:c + P], self.ctxn_t[:, b * CTX + r0:b * CTX + r0 + rows],
                        w["wkv"][:, 1024 + p * P:1024 + (p + 1) * P], start=True, stop=True))
            k, hi = st["k"].ap, []
            for h in (0, 1):
                own = slice(64 * h, 64 * h + 64)
                hi.append(ac.do(lambda e, h=h, own=own: e.activation(k[own, h, 0, c0:c0 + n], side.ap[own, 0:n], ACT.Copy),
                                m, st["k"].free))
            if part == 1:
                v, free = st["v"].ap, st["v"].free
                st["v_ready"] = [
                    ac.do(lambda e: e.activation(v[:, 4, :], side.ap[:, 2 * P:3 * P], ACT.Copy), free),
                    ac.do(lambda e: e.activation(v[0:CTX_REST, 5, :], side.ap[0:CTX_REST, 3 * P:4 * P], ACT.Copy))]

            def rest():
                low = []
                for h in (0, 1):
                    own = slice(64 * h, 64 * h + 64)
                    low.append(ve.do(lambda e, h=h, own=own: e.tensor_tensor(
                        k[own, h, 1, c0:c0 + n], side.ap[own, 0:n], k[own, h, 0, c0:c0 + n], ALU.subtract), hi[h],
                        st["v_ready"] if part else None))
                    if part == 1:
                        slot, other = st["n"] % 2, slice(64 - 64 * h, 128 - 64 * h)
                        copy_turn[slot, h] += 1
                        st[f"k{h}"] = self.dma("keys", k[other, h, :, :], k[own, h, :, :], low[h], st["k"].free,
                                               sem=copy_sems[slot, h], turn=copy_turn[slot, h])
                side.free = [low]
            return rest

        def project_v(g, n):
            b, p = g
            st = state[g]
            for t in range(QT):
                m = pe.do(lambda e, t=t: e.matmul(
                    side.ap[:, t * P:(t + 1) * P], self.xt[:, b * SEQ + t * P:b * SEQ + (t + 1) * P],
                    w["wkv"][:, 1024 + p * P:1024 + (p + 1) * P], start=True, stop=True), side.free)
            a = ac.do(lambda e: e.activation(st["v"].ap[:, 0:QT, :], side.ap.rearrange("p (t n) -> p t n", t=QT), ACT.Copy),
                      m, st["v"].free)
            side.free = [a]
            st["v_ready"].append(a)

        pieces = {0: project_q, 2: lambda g, n: project_k(g, 0), 4: lambda g, n: project_k(g, 1),
                  6: project_v}
        for s in sorted(pieces):
            rest = pieces[s](groups[0], 0)
            if rest:
                rest()

        def scores_of(u, h, j):
            g, half = u["group"], u["half"]
            st, slot, qt = state[g], scores.next(), 2 * half + j
            lhs = st["q"].ap[:, h, qt * P:(qt + 1) * P]
            k = st["k"].ap
            for a, z in ((0, SEQ), (SEQ, KEYS0)):
                for part in (0, 1):
                    m = pe.do(lambda e, a=a, z=z, part=part: e.matmul(slot.ap[:, a:z], lhs, k[:, h, part, a:z],
                                                                      start=part == 0, stop=part == 1),
                              slot.free, st["q0"], st["q1"], st[f"k{h}"])
            st.setdefault("scores", []).append(m)
            big, prob, col = neg_max.next(), probs.next(), 2 * j + h
            v = ve.do(lambda e: e.tensor_reduce(big.ap, slot.ap[:, 0:KEYS0], AX_X, ALU.max, negate=True), m, big.free)
            a = ac.do(lambda e: e.activation(prob.ap, slot.ap[:, 0:KEYS0], ACT.Exp, bias=big.ap,
                                             accum_out=u["sums"].ap[:, col:col + 1]), v, prob.free, u["sums"].free)
            big.free, slot.free = [a], [a]
            u.setdefault("exps", []).append(a)
            return prob, a

        def turn_probs(u, h, j, prob, ready):
            for n, (bank, tiles) in enumerate(zip(turned, (range(0, 4), range(4, KT0)))):
                for t in tiles:
                    rows = min(P, KEYS0 - t * P)
                    m = pe.do(lambda e, t=t, rows=rows, c=(t - tiles[0]) * P, bank=bank: e.transpose(
                        bank.ap[0:rows, c:c + P], prob.ap[:, t * P:t * P + rows], self.eye), ready, bank.free)
                out = u["probs"].ap[:, h, tiles[0]:tiles[-1] + 1, j * P:(j + 1) * P]
                src = bank.ap[:, 0:P * len(tiles)].rearrange("p (t n) -> p t n", t=len(tiles))
                if n == 0:
                    s = ac.do(lambda e, out=out, src=src: e.activation(out, src, ACT.Copy), m, u["probs"].free)
                else:
                    s = ve.do(lambda e, out=out, src=src: e.tensor_copy(out, src), m, u["probs"].free)
                bank.free = [s]
                u.setdefault("turned", []).append(s)
            prob.free = [m]

        def weigh(u, tiles):
            st = state[u["group"]]
            for t in tiles:
                rows = min(P, KEYS0 - t * P)
                for h in (0, 1):
                    m = pe.do(lambda e, t=t, rows=rows, h=h: e.matmul(
                        out_bank.ap[64 * h:64 * h + 64, 0:2 * P], st["v"].ap[0:rows, t, 64 * h:64 * h + 64],
                        u["probs"].ap[0:rows, h, t, :], start=t == 0, stop=t == KT0 - 1),
                        u["turned"], st["v_ready"], out_bank.free)
            if tiles[-1] == KT0 - 1:
                u["weighed"] = m
                u["probs"].free = [m]

        def invert(u):
            u["inverse"], u["spread"] = inverse.next(), spread.next()
            r, s = u["inverse"].ap, u["spread"].ap
            v = ve.do(lambda e: e.reciprocal(r, u["sums"].ap), u["exps"], u["inverse"].free)
            u["sums"].free = [v]
            by_head = r.rearrange("p (j h) -> p j h", j=2).unsqueeze(3).to_broadcast([P, 2, 2, D0])
            u["spread_done"] = po.do(lambda e: e.tensor_copy(s, by_head), v, u["spread"].free)
            u["inverse"].free = [u["spread_done"]]

        def scale_out(u):
            (b, p), half = u["group"], u["half"]
            for j in (0, 1):
                m = pe.do(lambda e, j=j: e.transpose(out_bank.ap[:, (2 + j) * P:(3 + j) * P],
                                                     u["spread"].ap[:, j, :, :].rearrange("p h d -> p (h d)"), self.eye),
                          u["spread_done"])
            u["spread"].free = [m]
            out = mixed[:, p, half * 2 * P:(half + 1) * 2 * P]
            a = ac.do(lambda e: e.activation(out, out_bank.ap[:, 2 * P:4 * P], ACT.Copy), m, mixed_free[half])
            s = ve.do(lambda e: e.tensor_tensor(out, out_bank.ap[:, 0:2 * P], out, ALU.mult), a)
            out_bank.free = [s]
            u["mixed"] = s
            if half == 1:
                st = state[u["group"]]
                st["q"].free = st["k"].free = list(st["scores"])
                st["v"].free = [u["weighed"]]

        def project_out(b, t, ready):
            for p in range(PAIRS):
                m = pe.do(lambda e, p=p: e.matmul(side.ap[:, 0:P], mixed[:, p, t * P:(t + 1) * P],
                                                  w["wo"][:, p * P:(p + 1) * P], start=p == 0, stop=p == PAIRS - 1),
                          ready, side.free)
            mixed_free[t // 2] = m
            side.free = [self.add_to_x(b * QT + t, side.ap[:, 0:P], 0, m)]

        units = [{"group": g, "half": half} for g in groups for half in (0, 1)]
        subs = [(u, h, j) for u in units for h in (0, 1) for j in (0, 1)]
        chores = [self.late_tables]
        for b in range(1, BATCH):
            rows = slice(QT * b, QT * b + QT)
            (once,), steps = self.norm_groups(x[:, rows, :], self.xn[:, rows, :], [self.load_x[b]] * QT, QT)
            (again,), done = self.norm_groups(self.xn[:, rows, :], self.xn[:, rows, :], steps, QT)
            chores += [*once, *again, lambda b=b, rows=rows, done=done: latents.extend(self.turn(
                self.xn[:, rows, :], self.xt[:, b * SEQ:(b + 1) * SEQ], done, n=QT, **ln2))]
        parts = [(0, 1), (2, 3), (4,), (5,)]
        waiting, rest = [], None
        for i in range(len(subs) + 15):
            if i < len(subs):
                u, h, j = subs[i]
                if i % 4 == 0:
                    u["sums"], u["probs"] = sums.next(), probs_t.next()
                waiting.append((u, h, j, *scores_of(u, h, j)))
            if rest:
                rest()
                rest = None
            back = (i - 3) // 4 - 1
            if 0 <= back < len(units):
                part = (i - 3) % 4
                if part == 0:
                    invert(units[back])
                weigh(units[back], parts[part])
                if part == 3:
                    scale_out(units[back])
            if i >= 2 and waiting:
                turn_probs(*waiting.pop(0))
            if chores and i >= 4:
                chores.pop(0)()
            late = i - 8 * PAIRS - 7
            if late >= 0 and late % (8 * PAIRS) in (0, 2, 4, 6):
                b = late // (8 * PAIRS)
                own = units[2 * PAIRS * b:2 * PAIRS * (b + 1)]
                project_out(b, late % (8 * PAIRS) // 2, [v["mixed"] for v in own])
            if i // 8 + 1 < len(groups) and i % 8 in pieces:
                rest = pieces[i % 8](groups[i // 8 + 1], i // 8 + 1)
        self.banks = Ring([self.psum[:, b * BANK:(b + 1) * BANK] for b in range(8)])
        for bank in self.banks.slots:
            bank.free = [side.free]

    def one_hot_of_max(self, values, down, n, *ready):
        ve = self.ve
        top, key, hot = self.carve(TILES), self.carve(TILES, n), self.carve(TILES, n)
        best = self.carve(TILES)
        wide = [P, TILES, n]
        places = down.unsqueeze(1).to_broadcast(wide)
        a = ve.do(lambda e: e.tensor_reduce(top, values, AX_X, ALU.max), *ready)
        b = ve.do(lambda e: e.tensor_tensor(hot, values, top.unsqueeze(2).to_broadcast(wide), ALU.is_equal), a)
        c = ve.do(lambda e: e.tensor_tensor(key, hot, places, ALU.mult), b)
        d = ve.do(lambda e: e.tensor_reduce(best, key, AX_X, ALU.max), c)
        f = ve.do(lambda e: e.tensor_tensor(hot, places, best.unsqueeze(2).to_broadcast(wide), ALU.is_equal), d)
        return hot, best, f

    def token_products(self, weights, n, ready, row, *others):
        bank = self.banks.next()
        out = self.carve(TILES, n)
        for t in range(TILES):
            m = self.pe.do(lambda e, t=t: e.matmul(bank.ap[:, t * n:(t + 1) * n], self.xt[:, t * P:(t + 1) * P], weights,
                                                   start=True, stop=True), ready[t], bank.free, *others)
        src = bank.ap[:, 0:TILES * n].rearrange("p (t n) -> p t n", t=TILES)
        if row is None:
            s = self.ve.do(lambda e: e.tensor_copy(out, src), m)
        else:
            s = self.ve.do(lambda e: e.tensor_tensor(out, src, row.unsqueeze(1).to_broadcast([P, TILES, n]), ALU.add), m)
        bank.free = [s]
        return out, s

    def turn_small(self, src, n, ready):
        out, steps = self.carve(TOKENS), []
        for b in range(BATCH):
            bank = self.banks.next()
            for j in range(QT):
                m = self.pe.do(lambda e, t=QT * b + j, j=j, bank=bank: e.transpose(
                    bank.ap[0:n, j * P:(j + 1) * P], src[:, t, :], self.eye), ready, bank.free)
            s = self.evacuate(out[0:n, b * SEQ:(b + 1) * SEQ], bank.ap[0:n, :], m)
            bank.free = [s]
            steps.append(s)
        return out, steps

    def top1_experts(self):
        pe, ve, ac = self.pe, self.ve, self.ac
        self.begin("experts")
        self.load_weights(7, self.before)
        w = self.w[1]
        normed = self.normalize(self.x, self.xn, [self.x_last[t] for t in range(TILES)])
        turned = self.turn(self.xn, self.xt, normed)
        logits, s = self.token_products(w["gate"], EXPERTS, turned, self.row["L0_ffn_gate_b"], self.w_ready[1], self.rows_ready)
        s = ve.do(lambda e: e.tensor_tensor(logits, logits, self.row["L0_ffn_expert_bias"].unsqueeze(1)
                                            .to_broadcast([P, TILES, EXPERTS]), ALU.add), s)
        hot, _, s_hot = self.one_hot_of_max(logits, self.c["down8"], EXPERTS, s)
        hot_t, hot_t_ready = self.turn_small(hot, EXPERTS, s_hot)
        weight = self.carve(TILES, EXPERTS)
        s_weight = ve.do(lambda e: e.tensor_scalar(weight, hot, self.gates[:, 4:5], None, ALU.mult), s_hot)

        hidden = Ring([self.carve(FT, SEQ) for _ in range(2)])
        for b in range(BATCH):
            bank = self.banks.next()
            for j in range(QT):
                t = QT * b + j
                m = pe.do(lambda e, t=t, j=j, bank=bank: e.matmul(
                    bank.ap[:, j * P:(j + 1) * P], hot_t[0:EXPERTS, t * P:(t + 1) * P], self.small[:, 0:P],
                    start=True, stop=True), hot_t_ready[b], bank.free, self.rows_ready)
            bank.free = [self.add_to_x(QT * b + j, bank.ap[:, j * P:(j + 1) * P], 4, m) for j in range(QT)]

        def up(b, x):
            h, steps = hidden.next(), []
            for f in range(FT):
                bank = self.banks.next()
                m = pe.do(lambda e, f=f, bank=bank: e.matmul(
                    bank.ap, w["w1"][:, x * FF + f * P:x * FF + (f + 1) * P], self.xt[:, b * SEQ:(b + 1) * SEQ],
                    start=True, stop=True), bank.free)
                col = w["b1"][:, x * FT + f:x * FT + f + 1]
                if f % 4 == 3:
                    s = ve.do(lambda e, f=f, bank=bank, col=col: e.tensor_scalar(h.ap[:, f, :], bank.ap, col, 0.0, ALU.add, ALU.max),
                              m, h.free)
                else:
                    s = ac.do(lambda e, f=f, bank=bank, col=col: e.activation(h.ap[:, f, :], bank.ap, ACT.Relu, bias=col), m, h.free)
                bank.free = [s]
                steps.append(s)
            return b, x, h, steps

        def down(b, x, h, steps):
            bank = self.banks.next()
            for j in range(QT):
                for f in range(FT):
                    m = pe.do(lambda e, j=j, f=f: e.matmul(
                        bank.ap[:, j * P:(j + 1) * P], h.ap[:, f, j * P:(j + 1) * P],
                        w["w2"][:, (x * FT + f) * P:(x * FT + f + 1) * P], start=f == 0, stop=f == FT - 1), steps, bank.free)
            h.free = [m]
            bank.free = []
            for j in range(QT):
                t = QT * b + j
                self.x_last[t] = ve.do(lambda e, t=t, j=j: e.scalar_tensor_tensor(
                    self.x[:, t, :], bank.ap[:, j * P:(j + 1) * P], weight[:, t, x:x + 1], self.x[:, t, :],
                    ALU.mult, ALU.add), m, s_weight, self.x_last[t])
                bank.free.append(self.x_last[t])

        waiting = None
        for b in range(BATCH):
            for x in range(EXPERTS):
                now = up(b, x)
                if waiting:
                    down(*waiting)
                waiting = now
        down(*waiting)

    def one_head(self):
        pe, ve, ac = self.pe, self.ve, self.ac
        self.begin("onehead")
        self.load_weights(5, self.before)
        self.load_weights(6, self.before)
        w = self.w[2]
        normed = self.normalize(self.x, self.xn, [self.x_last[t] for t in range(TILES)])
        turned = self.turn(self.xn, self.xt, normed)
        q_t, q_ready = self.project(w["wq"], w["bq"], self.xt, turned, self.w_ready[2])
        k_t, k_ready = self.project_context(w["wk"], w["bk"], self.w_ready[2])
        v, v_ready = self.carve(2 * BATCH, P), []
        for b in range(BATCH):
            bank = self.banks.next()
            for n, rows in ((0, P), (1, CTX_REST)):
                m = pe.do(lambda e, b=b, n=n, rows=rows, bank=bank: e.matmul(
                    bank.ap[0:rows, n * P:(n + 1) * P], self.context[:, b, n * P:n * P + rows], w["wv"],
                    start=True, stop=True), bank.free, self.context_ready)
            s = [ve.do(lambda e, b=b, n=n, rows=rows, bank=bank: e.tensor_copy(
                v[0:rows, 2 * b + n, :], bank.ap[0:rows, n * P:(n + 1) * P]), m) for n, rows in ((0, P), (1, CTX_REST))]
            bank.free = s
            v_ready.append(s)
        probs = Ring([self.carve(QT, CTX) for _ in range(2)])
        probs_t = Ring([self.carve(2, SEQ) for _ in range(2)])
        small = [(self.carve(QT), self.carve(QT), self.carve(QT)) for _ in range(BATCH)]

        def scores_of(b):
            neg, total, inv = small[b]
            prob, exps = probs.next(), []
            for g, tiles in enumerate(((0, 1), (2, 3))):
                bank = self.banks.next()
                for n, t in enumerate(tiles):
                    m = pe.do(lambda e, n=n, t=t, bank=bank: e.matmul(
                        bank.ap[:, n * CTX:(n + 1) * CTX], q_t[:, (QT * b + t) * P:(QT * b + t + 1) * P],
                        k_t[:, b * CTX:(b + 1) * CTX], start=True, stop=True), q_ready[QT * b + t], k_ready, bank.free)
                src = bank.ap[:, 0:2 * CTX].rearrange("p (t k) -> p t k", t=2)
                s = ve.do(lambda e, g=g, src=src: e.tensor_reduce(neg[:, 2 * g:2 * g + 2], src, AX_X, ALU.max, negate=True), m)
                bank.free = []
                for n, t in enumerate(tiles):
                    a = ac.do(lambda e, n=n, t=t, src=src: e.activation(prob.ap[:, t, :], src[:, n, :], ACT.Exp, bias=neg[:, t:t + 1],
                                                                        accum_out=total[:, t:t + 1]), s, prob.free)
                    bank.free.append(a)
                exps += bank.free
            r = ve.do(lambda e: e.reciprocal(inv, total), exps)
            return b, prob, exps, inv, r

        def weigh(b, prob, exps, inv, r):
            pt, steps = probs_t.next(), []
            for n, rows in ((0, P), (1, CTX_REST)):
                bank = self.banks.next()
                for t in range(QT):
                    m = pe.do(lambda e, n=n, t=t, rows=rows, bank=bank: e.transpose(
                        bank.ap[0:rows, t * P:(t + 1) * P], prob.ap[:, t, n * P:n * P + rows], self.eye), exps, bank.free)
                s = self.evacuate(pt.ap[0:rows, n, :], bank.ap[0:rows, :], m, pt.free)
                bank.free = [s]
                steps.append(s)
            prob.free = [m]
            bank = self.banks.next()
            for t in range(QT):
                for n, rows in ((0, P), (1, CTX_REST)):
                    m = pe.do(lambda e, n=n, t=t, rows=rows: e.matmul(
                        bank.ap[:, t * P:(t + 1) * P], pt.ap[0:rows, n, t * P:(t + 1) * P], v[0:rows, 2 * b + n, :],
                        start=n == 0, stop=n == 1), steps, v_ready[b], bank.free)
            pt.free = [m]
            bank.free = [self.add_to_x(QT * b + t, bank.ap[:, t * P:(t + 1) * P], 1, [m, r], row=self.row["L1_xattn_bv"],
                                       factor=inv[:, t:t + 1]) for t in range(QT)]

        waiting = None
        for b in range(BATCH):
            now = scores_of(b)
            if waiting:
                weigh(*waiting)
            waiting = now
        weigh(*waiting)

    def project(self, weights, bias, src, ready, *others, scale=None, out=None):
        out = self.carve(TOKENS) if out is None else out
        steps = []
        for b in range(BATCH):
            bank = self.banks.next()
            m = self.pe.do(lambda e, b=b, bank=bank: e.matmul(bank.ap, weights, src[:, b * SEQ:(b + 1) * SEQ], start=True, stop=True),
                           ready[QT * b:QT * b + QT], bank.free, *others)
            o = out[:, b * SEQ:(b + 1) * SEQ]
            if scale is None and b % 2:
                s = self.ac.do(lambda e, o=o, bank=bank: e.activation(o, bank.ap, ACT.Identity, bias=bias), m)
            else:
                s = self.ve.do(lambda e, o=o, bank=bank: e.tensor_scalar(o, bank.ap, bias, 1.0 if scale is None else scale,
                                                                         ALU.add, ALU.mult), m)
            bank.free = [s]
            steps += [s] * QT
        return out, steps

    def project_context(self, weights, bias, *others):
        out, steps = self.carve(CTX_ROWS), []
        for b in range(0, BATCH, 2):
            bank = self.banks.next()
            for n in (0, 1):
                m = self.pe.do(lambda e, b=b, n=n, bank=bank: e.matmul(
                    bank.ap[:, n * CTX:(n + 1) * CTX], weights, self.context[:, b + n, 0:CTX], start=True, stop=True),
                    self.context_ready, bank.free, *others)
            s = self.ac.do(lambda e, b=b, bank=bank: e.activation(out[:, b * CTX:(b + 2) * CTX], bank.ap[:, 0:2 * CTX],
                                                                  ACT.Identity, bias=bias), m)
            bank.free = [s]
            steps.append(s)
        return out, steps

    def batch_attention(self):
        pe, ve, ac, po = self.pe, self.ve, self.ac, self.po
        self.begin("batch")
        w, y = self.w[3], self.xn
        heads, d = 16, 8
        normed = self.normalize(self.x, y, [self.x_last[t] for t in range(TILES)])
        turned = self.turn(y, self.xt, normed)
        qkv, qkv_ready = self.carve(TILES, 3 * P), []
        for t in range(TILES):
            bank = self.banks.next()
            m = pe.do(lambda e, t=t, bank=bank: e.matmul(bank.ap[:, 0:3 * P], self.xt[:, t * P:(t + 1) * P], w["in"],
                                                         start=True, stop=True), turned[t], bank.free, self.w_ready[3])
            s = ve.do(lambda e, t=t, bank=bank: e.tensor_tensor(qkv[:, t, :], bank.ap[:, 0:3 * P],
                                                                self.row["L1_ffn_in_proj_b"], ALU.add), m, self.rows_ready)
            bank.free = [s]
            qkv_ready.append(s)
        part = lambda n: qkv[:, :, n * P:(n + 1) * P]
        pairs = [P, BATCH, QT, P]
        places = QT * heads
        product = [self.carve(BATCH * QT, P) for _ in range(2)]
        product_free = [None, None]
        score = self.carve(BATCH, BATCH, places)
        done = []
        for t in range(BATCH):
            o, slot = product[t % 2], t % 2
            a = ve.do(lambda e, t=t, o=o: e.tensor_tensor(
                o.rearrange("p (s j) c -> p s j c", s=BATCH), part(0)[:, QT * t:QT * t + QT, :].unsqueeze(1).to_broadcast(pairs),
                part(1).rearrange("p (s j) c -> p s j c", s=BATCH), ALU.mult), qkv_ready, product_free[slot])
            b = ve.do(lambda e, t=t, o=o: e.tensor_reduce(
                score[:, t, :, :].rearrange("p s c -> p (s c)"), o.rearrange("p s (h d) -> p (s h) d", d=d), AX_X, ALU.add), a)
            product_free[slot] = b
            done.append(b)
        by_key = score.rearrange("p t s c -> p t c s")
        most, total = self.carve(BATCH, places), self.carve(BATCH, places)
        over = lambda v: v.unsqueeze(2).to_broadcast([P, BATCH, BATCH, places])
        s = ve.do(lambda e: e.tensor_reduce(most, by_key, AX_X, ALU.max), done)
        s = ve.do(lambda e: e.tensor_tensor(score, score, over(most), ALU.subtract), s)
        s = ac.do(lambda e: e.activation(score, score, ACT.Exp, scale=d ** -0.5), s)
        s = ve.do(lambda e: e.tensor_reduce(total, by_key, AX_X, ALU.add), s)
        s = ve.do(lambda e: e.reciprocal(total, total), s)
        s = ve.do(lambda e: e.tensor_tensor(score, score, over(total), ALU.mult), s)
        mixed = self.carve(TILES, P)
        mixed_ready = []
        for t in range(BATCH):
            o, slot = product[t % 2], t % 2
            a = ve.do(lambda e, t=t, o=o: e.tensor_tensor(
                o.rearrange("p s (h d) -> p s h d", d=d),
                score[:, t, :, :].rearrange("p s (j h) -> p (s j) h", j=QT).unsqueeze(3).to_broadcast([P, TILES, heads, d]),
                part(2).rearrange("p s (h d) -> p s h d", d=d), ALU.mult), s, product_free[slot])
            b = ve.do(lambda e, t=t, o=o: e.tensor_reduce(
                mixed[:, QT * t:QT * t + QT, :].rearrange("p j c -> p (j c)"),
                o.rearrange("p (s j) c -> p (j c) s", s=BATCH), AX_X, ALU.add), a)
            product_free[slot] = b
            mixed_ready += [b] * QT
        turned = self.turn(mixed, self.xt, mixed_ready, after=(qkv_ready,))
        h = self.token_layer([(self.xt, w["out"])], turned, self.row["L1_ffn_out_b"], y)
        ready = self.normalize(y, y, h, gain=self.row["L1_ffn_ln1_g"], bias=self.row["L1_ffn_ln1_b"])
        turned = self.turn(y, self.xt, ready)

        probs, s = self.token_products(w["router"], EXPERTS, turned, self.row["L1_ffn_router_b"])
        wide = [P, TILES, EXPERTS]
        top, mass = self.carve(TILES), self.carve(TILES)
        s = ve.do(lambda e: e.tensor_reduce(top, probs, AX_X, ALU.max), s)
        s = ve.do(lambda e: e.tensor_tensor(probs, probs, top.unsqueeze(2).to_broadcast(wide), ALU.subtract), s)
        s = ac.do(lambda e: e.activation(probs, probs, ACT.Exp), s)
        s = ve.do(lambda e: e.tensor_reduce(mass, probs, AX_X, ALU.add), s)
        s = ve.do(lambda e: e.reciprocal(mass, mass), s)
        s = ve.do(lambda e: e.tensor_tensor(probs, probs, mass.unsqueeze(2).to_broadcast(wide), ALU.mult), s)
        hot1, key1, s = self.one_hot_of_max(probs, self.c["down8"], EXPERTS, s)
        s = ve.do(lambda e: e.scalar_tensor_tensor(probs, hot1, -4.0, probs, ALU.mult, ALU.add), s)
        hot2, key2, s = self.one_hot_of_max(probs, self.c["down8"], EXPERTS, s)
        s = ve.do(lambda e: e.tensor_tensor(key1, key1, key2, ALU.min), s)
        hot = hot1
        s_hot = ve.do(lambda e: e.tensor_tensor(hot, self.c["down8"].unsqueeze(1).to_broadcast(wide),
                                                key1.unsqueeze(2).to_broadcast(wide), ALU.is_equal), s)
        hot_t, hot_t_ready = self.turn_small(hot, EXPERTS, s_hot)
        last = list(ready)
        for b in range(BATCH):
            bank = self.banks.next()
            for j in range(QT):
                t = QT * b + j
                m = pe.do(lambda e, t=t, j=j, bank=bank: e.matmul(
                    bank.ap[:, j * P:(j + 1) * P], hot_t[0:EXPERTS, t * P:(t + 1) * P], self.small[:, P:2 * P],
                    start=True, stop=True), hot_t_ready[b], bank.free)
            o = y[:, QT * b:QT * b + QT, :]
            s = ve.do(lambda e, o=o, bank=bank: e.tensor_tensor(o, o, bank.ap.rearrange("p (t n) -> p t n", t=QT), ALU.add),
                      m, turned)
            bank.free = [s]
            for j in range(QT):
                last[QT * b + j] = s

        hidden = Ring([self.carve(SEQ) for _ in range(3)])

        def up(b, x):
            bank, g = self.banks.next(), hidden.next()
            m = pe.do(lambda e: e.matmul(bank.ap, w["w1"][:, x * P:(x + 1) * P], self.xt[:, b * SEQ:(b + 1) * SEQ],
                                         start=True, stop=True), bank.free)
            s = ac.do(lambda e: e.activation(g.ap, bank.ap, ACT.Gelu, bias=w["b1"][:, x:x + 1]), m, g.free)
            bank.free = [s]
            return b, x, g, s

        def down(b, x, g, ready):
            bank = self.banks.next()
            for j in range(QT):
                m = pe.do(lambda e, j=j: e.matmul(bank.ap[:, j * P:(j + 1) * P], g.ap[:, j * P:(j + 1) * P],
                                                  w["w2"][:, x * P:(x + 1) * P], start=True, stop=True), ready, bank.free)
            g.free, bank.free = [m], []
            for j in range(QT):
                t = QT * b + j
                last[t] = ve.do(lambda e, t=t, j=j: e.scalar_tensor_tensor(
                    y[:, t, :], bank.ap[:, j * P:(j + 1) * P], hot[:, t, x:x + 1], y[:, t, :], ALU.mult, ALU.add), m, last[t])
                bank.free.append(last[t])

        waiting = []
        for b in range(BATCH):
            for x in range(EXPERTS):
                waiting.append(up(b, x))
                if len(waiting) > 2:
                    down(*waiting.pop(0))
        for rest in waiting:
            down(*rest)
        ready = self.normalize(y, y, last, gain=self.row["L1_ffn_ln2_g"], bias=self.row["L1_ffn_ln2_b"])
        for t in range(TILES):
            self.add_to_x(t, y[:, t, :], 5, ready[t])

    def token_layer(self, parts, ready, row, into):
        out = []
        for b in range(BATCH):
            bank = self.banks.next()
            for j in range(QT):
                t = QT * b + j
                for n, (src, weights) in enumerate(parts):
                    m = self.pe.do(lambda e, t=t, j=j, n=n, src=src, weights=weights, bank=bank: e.matmul(
                        bank.ap[:, j * P:(j + 1) * P], src[:, t * P:(t + 1) * P], weights,
                        start=n == 0, stop=n == len(parts) - 1), ready[t], bank.free)
            o = into[:, QT * b:QT * b + QT, :]
            src = bank.ap.rearrange("p (t n) -> p t n", t=QT)
            s1 = self.ve.do(lambda e, o=o, src=src: e.tensor_tensor(o, src, o, ALU.add), m)
            bank.free = [s1]
            s2 = self.ve.do(lambda e, o=o: e.tensor_tensor(o, o, row.unsqueeze(1).to_broadcast([P, QT, P]), ALU.add), s1)
            out += [s2] * QT
        return out

    def context_attention(self, heads, q_t, q_ready, k_t, k_ready, wv, bv, masked=None, finish=None):
        pe, ve, ac, po = self.pe, self.ve, self.ac, self.po
        d = P // heads
        chunks = flat_chunks(heads)
        head_of, block = self.c[f"head{heads}"], self.c[f"block{heads}"].rearrange("p (c h) -> p c h", h=heads)
        keys = Ring([self.carve(heads, CTX)])
        values = Ring([self.carve(len(chunks), P) for _ in range(2)])
        probs = Ring([self.carve(heads * CTX) for _ in range(2)])
        probs_t = Ring([self.carve(len(chunks), 2 * P)])
        small = Ring([self.carve(heads) for _ in range(6)])
        spread = Ring([self.carve(heads, d) for _ in range(2)])
        factor = Ring([self.carve(2 * P) for _ in range(2)])
        mixed = Ring([self.carve(2 * P) for _ in range(2)])
        groups = [(h, min(3, heads - h)) for h in range(0, heads, 3)]
        operands = {}

        def prepare(b):
            k = keys.next()
            ks = po.do(lambda e: e.tensor_tensor(
                k.ap, k_t[:, b * CTX:(b + 1) * CTX].unsqueeze(1).to_broadcast([P, heads, CTX]),
                head_of.unsqueeze(2).to_broadcast([P, heads, CTX]), ALU.mult), k_ready, k.free)
            v, steps = values.next(), []
            for c in range(0, len(chunks), 4):
                bank, batch = self.banks.next(), chunks[c:c + 4]
                for n, (f0, rows) in enumerate(batch):
                    s = f0 % CTX
                    m = pe.do(lambda e, n=n, s=s, rows=rows, bank=bank: e.matmul(
                        bank.ap[0:rows, n * P:(n + 1) * P], self.context[:, b, s:s + rows], wv, start=True, stop=True),
                        bank.free, self.context_ready)
                bank.free = []
                full = [n for n, (_, rows) in enumerate(batch) if rows == P]
                runs = ([(0, len(full), P)] if full else []) + [(n, n + 1, rows) for n, (_, rows) in enumerate(batch) if rows < P]
                for n0, n1, rows in runs:
                    k_n = n1 - n0
                    step = ve.do(lambda e, c=c, n0=n0, n1=n1, rows=rows, k_n=k_n, bank=bank: e.tensor_tensor(
                        v.ap[0:rows, c + n0:c + n1, :].rearrange("p c (h d) -> p c h d", h=heads),
                        bank.ap[0:rows, n0 * P:n1 * P].rearrange("p (c h d) -> p c h d", c=k_n, h=heads),
                        block[0:rows, c + n0:c + n1, :].unsqueeze(3).to_broadcast([rows, k_n, heads, d]), ALU.mult), m, v.free)
                    bank.free.append(step)
                    steps.append(step)
            operands[b] = (k, ks, v, steps)

        def scores_of(b, t):
            k, ks, _, _ = operands[b]
            tile, prob = QT * b + t, probs.next()
            neg, total, exps = small.next(), small.next(), []
            for h0, n in groups:
                bank = self.banks.next()
                src = bank.ap[:, 0:n * CTX]
                m = pe.do(lambda e, h0=h0, n=n, src=src: e.matmul(
                    src, q_t[:, tile * P:(tile + 1) * P], k.ap[:, h0:h0 + n, :].rearrange("p h k -> p (h k)"),
                    start=True, stop=masked is None), q_ready[tile], ks, bank.free)
                if masked is not None:
                    m = pe.do(lambda e, n=n, src=src: e.matmul(
                        src.rearrange("p (h k) -> p h k", h=n), self.cb["eye_b"], masked[0][:, tile, :].unsqueeze(1).to_broadcast([P, n, CTX]),
                        start=False, stop=True), masked[1])
                s = ve.do(lambda e, h0=h0, n=n, src=src: e.tensor_reduce(
                    neg.ap[:, h0:h0 + n], src.rearrange("p (h k) -> p h k", h=n), AX_X, ALU.max, negate=True), m, neg.free)
                bank.free = []
                for h in range(h0, h0 + n):
                    a = ac.do(lambda e, h=h, h0=h0, src=src: e.activation(
                        prob.ap[:, h * CTX:(h + 1) * CTX], src[:, (h - h0) * CTX:(h - h0 + 1) * CTX], ACT.Exp,
                        bias=neg.ap[:, h:h + 1], accum_out=total.ap[:, h:h + 1]), s, prob.free, total.free)
                exps.append(a)
                bank.free = [a]
            k.free = [m]
            neg.free = [a]
            r = ve.do(lambda e: e.reciprocal(total.ap, total.ap), exps)
            sp = spread.next()
            wide = po.do(lambda e: e.tensor_copy(sp.ap, total.ap.unsqueeze(2).to_broadcast([P, heads, d])), r, sp.free)
            total.free = [wide]
            return b, t, prob, exps, sp, wide

        unit = {}

        def turn_probs(b, t, prob, exps, sp, wide):
            j = t % 2
            if j == 0:
                unit["pt"], unit["steps"], unit["factor"] = probs_t.next(), [], factor.next()
                unit["side"] = None
            pt = unit["pt"]
            for c in range(0, len(chunks), 4):
                bank, batch = self.banks.next(), chunks[c:c + 4]
                for n, (f0, rows) in enumerate(batch):
                    m = pe.do(lambda e, n=n, f0=f0, rows=rows, bank=bank: e.transpose(
                        bank.ap[0:rows, n * P:(n + 1) * P], prob.ap[:, f0:f0 + rows], self.eye), exps, bank.free)
                full = sum(rows == P for _, rows in batch)
                bank.free = []
                on_ac = (c // 4) % 2 == 0
                for n0, n1, rows in ([(0, full, P)] if full else []) + ([(full, full + 1, batch[-1][1])] if full < len(batch) else []):
                    o = pt.ap[0:rows, c + n0:c + n1, j * P:(j + 1) * P]
                    i = bank.ap[0:rows, n0 * P:n1 * P].rearrange("p (c q) -> p c q", c=n1 - n0)
                    if on_ac:
                        s = ac.do(lambda e, o=o, i=i: e.activation(o, i, ACT.Copy), m, pt.free)
                    else:
                        s = ve.do(lambda e, o=o, i=i: e.tensor_copy(o, i), m, pt.free)
                    bank.free.append(s)
                    unit["steps"].append(s)
            prob.free = [m]
            bank = self.banks.next()
            m = pe.do(lambda e, bank=bank: e.transpose(bank.ap[:, 0:P], sp.ap.rearrange("p h d -> p (h d)"), self.eye), wide, bank.free)
            sp.free = [m]
            f = unit["factor"]
            s = ac.do(lambda e, bank=bank, f=f: e.activation(f.ap[:, j * P:(j + 1) * P], bank.ap[:, 0:P], ACT.Copy), m, f.free)
            bank.free = [s]
            unit["steps"].append(s)
            if j == 1:
                weigh(b, t // 2)

        def weigh(b, half):
            _, _, v, v_ready = operands[b]
            bank, pt, f, steps = self.banks.next(), unit["pt"], unit["factor"], unit["steps"]
            for c, (_, rows) in enumerate(chunks):
                m = pe.do(lambda e, c=c, rows=rows: e.matmul(bank.ap[:, 0:2 * P], v.ap[0:rows, c, :], pt.ap[0:rows, c, :],
                                                             start=c == 0, stop=c == len(chunks) - 1), steps, v_ready, bank.free)
            pt.free, v.free = [m], [m]
            o = mixed.next()
            s = ve.do(lambda e: e.tensor_tensor(o.ap, bank.ap[:, 0:2 * P], f.ap, ALU.mult), m, o.free)
            bank.free, f.free = [s], [s]
            s = ve.do(lambda e: e.tensor_scalar(o.ap, o.ap, bv, None, ALU.add), s)
            finish(b, half, o, s)

        waiting = None
        for b in range(BATCH):
            prepare(b)
            for t in range(QT):
                now = scores_of(b, t)
                if waiting:
                    turn_probs(*waiting)
                waiting = now
        turn_probs(*waiting)

    def masked_attention(self):
        pe, ve = self.pe, self.ve
        self.begin("masked")
        w, heads = self.w[4], 16
        mask = self.carve(TILES, CTX, dt=BF16)
        raw = self.xt[:, 0:TILES * CTX // 4].bitcast(U8).rearrange("p (t k) -> p t k", t=TILES)
        load = self.dma("mask", raw, self.dram["mask"].rearrange("(t p) k -> p t k", p=P), self.before)
        mask_ready = ve.do(lambda e: e.tensor_scalar(mask, raw, MASKED, None, ALU.mult), load)
        normed = self.normalize(self.x, self.xn, [self.x_last[t] for t in range(TILES)])
        turned = self.turn(self.xn, self.xt, normed, after=(mask_ready,))
        q_t, q_ready = self.project(w["wq"], w["bq"], self.xt, turned, self.w_ready[4], scale=(P // heads) ** -0.5,
                                    out=self.xn[:, :, :].rearrange("p t d -> p (t d)"))
        k_t, k_ready = self.project_context(w["wk"], w["bk"], self.w_ready[4])

        def finish(b, half, o, ready):
            bank = self.banks.next()
            for j in (0, 1):
                m = pe.do(lambda e, j=j: e.matmul(bank.ap[:, j * P:(j + 1) * P], o.ap[:, j * P:(j + 1) * P], w["wo"],
                                                  start=True, stop=True), ready, bank.free)
            o.free = [m]
            bank.free = [self.add_to_x(QT * b + 2 * half + j, bank.ap[:, j * P:(j + 1) * P], 2, m, row=self.row["L2_xattn_bo"])
                         for j in (0, 1)]

        self.context_attention(heads, q_t, q_ready, k_t, k_ready, w["wv"], w["bv"], (mask, mask_ready), finish)

    def scaled_feed_forward(self):
        pe, ve, ac = self.pe, self.ve, self.ac
        self.begin("scaled")
        w = self.w[5]
        normed = self.normalize(self.x, self.xn, [self.x_last[t] for t in range(TILES)])
        turned = self.turn(self.xn, self.xt, normed)
        gated = self.carve(BATCH, FT, SEQ)
        silu = Ring([self.carve(SEQ) for _ in range(3)])
        hidden = [Ring([self.carve(FT, SEQ) for _ in range(2)]) for _ in range(2)]
        gated_ready = []
        for b in range(BATCH):
            steps = []
            for f in range(FT):
                bank_a, bank_g, s = self.banks.next(), self.banks.next(), silu.next()
                for bank, name in ((bank_a, "w1"), (bank_g, "w2")):
                    m = pe.do(lambda e, b=b, f=f, bank=bank, name=name: e.matmul(
                        bank.ap, w[name][:, f * P:(f + 1) * P], self.xt[:, b * SEQ:(b + 1) * SEQ], start=True, stop=True),
                        turned[QT * b + QT - 1], bank.free, self.w_ready[5])
                a = ac.do(lambda e, f=f, bank=bank_a, s=s: e.activation(s.ap, bank.ap, ACT.Silu, scale=w["s1"][:, f:f + 1]), m, s.free)
                v = ve.do(lambda e, b=b, f=f, bank=bank_g, s=s: e.scalar_tensor_tensor(
                    gated[:, b, f, :], bank.ap, w["s2"][:, f:f + 1], s.ap, ALU.mult, ALU.mult), a)
                bank_a.free, bank_g.free, s.free = [a], [v], [v]
                steps.append(v)
            gated_ready.append(steps)

        def layer(src, ready, weights, scales, ring):
            out, steps = ring.next(), []
            for o in range(FT):
                bank = self.banks.next()
                for i in range(FT):
                    m = pe.do(lambda e, o=o, i=i, bank=bank: e.matmul(
                        bank.ap, weights[:, i * FF + o * P:i * FF + (o + 1) * P], src[:, i, :], start=i == 0, stop=i == FT - 1),
                        ready, bank.free)
                s = ac.do(lambda e, o=o, bank=bank: e.activation(out.ap[:, o, :], bank.ap, ACT.Gelu, scale=scales[:, o:o + 1]),
                          m, out.free)
                bank.free = [s]
                steps.append(s)
            return out, steps, m

        def last(b, h, ready):
            bank = self.banks.next()
            for j in range(QT):
                for i in range(FT):
                    m = pe.do(lambda e, i=i, j=j: e.matmul(bank.ap[:, j * P:(j + 1) * P], h.ap[:, i, j * P:(j + 1) * P],
                                                           w["w3"][:, i * P:(i + 1) * P], start=i == 0, stop=i == FT - 1),
                              ready, bank.free)
            h.free = [m]
            bank.free = [self.add_to_x(QT * b + j, bank.ap[:, j * P:(j + 1) * P], 6, m, row=self.row["L2_ffn_w3_s"], op=ALU.mult)
                         for j in range(QT)]

        first, second = {}, {}
        for b in range(BATCH + 2):
            if b < BATCH:
                first[b] = layer(gated[:, b, :, :], gated_ready[b], w["h1"], w["sh1"], hidden[0])
            if 0 <= b - 1 < BATCH:
                h, ready, _ = first[b - 1]
                second[b - 1] = layer(h.ap, ready, w["h2"], w["sh2"], hidden[1])
                h.free = [second[b - 1][2]]
            if 0 <= b - 2 < BATCH:
                last(b - 2, second[b - 2][0], second[b - 2][1])

    def decoder_block(self):
        pe, ve, ac = self.pe, self.ve, self.ac
        self.begin("decoder")
        w, y, heads = self.w[6], self.xn, 8
        d = P // heads
        normed = self.normalize(self.x, y, [self.x_last[t] for t in range(TILES)])
        turned = self.turn(y, self.xt, normed)
        values = self.carve(TILES, P)
        qkv = Ring([self.carve(3 * P) for _ in range(3)])
        junk = Ring([self.carve(P) for _ in range(2)])
        score, delta = self.carve(TILES), self.carve(TILES)
        steps, kept = [], []
        for t in range(TILES):
            bank, q = self.banks.next(), qkv.next()
            m = pe.do(lambda e, t=t, bank=bank: e.matmul(bank.ap[:, 0:3 * P], self.xt[:, t * P:(t + 1) * P], w["qkv"],
                                                         start=True, stop=True), turned[t], bank.free, self.w_ready[6])
            s1 = ve.do(lambda e, q=q, bank=bank: e.tensor_tensor(q.ap[:, 0:2 * P], bank.ap[:, 0:2 * P],
                                                                 self.row["L3_xattn_qkv_b"][:, 0:2 * P], ALU.add), m, q.free)
            s2 = ve.do(lambda e, t=t, bank=bank: e.tensor_tensor(values[:, t, :], bank.ap[:, 2 * P:3 * P],
                                                                 self.row["L3_xattn_qkv_b"][:, 2 * P:3 * P], ALU.add), m)
            bank.free = [s1, s2]
            kept.append(s2)
            z = junk.next()
            s3 = ve.do(lambda e, t=t, q=q, z=z: e.tensor_tensor_reduce(
                z.ap, q.ap[:, 0:P], q.ap[:, P:2 * P], float(P) ** 0.5, 0.0, ALU.mult, ALU.add, score[:, t:t + 1]), s1, z.free)
            q.free, z.free = [s3], [s3]
            steps.append(s3)
        s = ve.do(lambda e: e.tensor_tensor(delta, score, score, ALU.subtract), steps)
        s = ac.do(lambda e: e.activation(delta, delta, ACT.Exp), s)
        s = ve.do(lambda e: e.reciprocal(score, delta), s)
        s = ve.do(lambda e: e.tensor_tensor(delta, delta, score, ALU.mult), s)
        s = ve.do(lambda e: e.tensor_tensor(values, values, delta.unsqueeze(2).to_broadcast([P, TILES, P]), ALU.mult), s, kept)
        turned = self.turn(values, self.xt, [s] * TILES)
        ready = self.token_layer([(self.xt, w["sa_out"])], turned, self.row["L3_xattn_sa_out_b"], y)
        ready = self.normalize(y, y, ready, gain=self.row["L3_xattn_ln1_g"], bias=self.row["L3_xattn_ln1_b"])
        turned = self.turn(y, self.xt, ready)
        q_t, q_ready = self.project(w["in"][:, 0:P], w["in_b"][:, 0:1], self.xt, turned, scale=d ** -0.5,
                                    out=values.rearrange("p t d -> p (t d)"))
        k_t, k_ready = self.project_context(w["in"][:, P:2 * P], w["in_b"][:, 1:2])
        after_mix = []

        def finish(b, half, o, ready):
            bank = self.banks.next()
            for j in (0, 1):
                m = pe.do(lambda e, j=j: e.matmul(bank.ap[:, j * P:(j + 1) * P], o.ap[:, j * P:(j + 1) * P], w["mha_out"],
                                                  start=True, stop=True), ready, bank.free)
            o.free = [m]
            t0 = QT * b + 2 * half
            rows = y[:, t0:t0 + 2, :]
            s1 = ve.do(lambda e: e.tensor_tensor(rows, bank.ap[:, 0:2 * P].rearrange("p (t n) -> p t n", t=2), rows, ALU.add), m)
            bank.free = [s1]
            s2 = ve.do(lambda e: e.tensor_tensor(rows, rows, self.row["L3_xattn_mha_out_b"].unsqueeze(1).to_broadcast([P, 2, P]),
                                                 ALU.add), s1)
            after_mix.extend([s2, s2])

        self.context_attention(heads, q_t, q_ready, k_t, k_ready, w["in"][:, 2 * P:3 * P], w["in_b"][:, 2:3], None, finish)
        ready = self.normalize(y, y, after_mix, gain=self.row["L3_xattn_ln2_g"], bias=self.row["L3_xattn_ln2_b"])
        turned = self.turn(y, self.xt, ready)
        hidden = self.carve(FT, SEQ)
        free, done = None, []
        for b in range(BATCH):
            steps = []
            for f in range(FT):
                bank = self.banks.next()
                m = pe.do(lambda e, b=b, f=f, bank=bank: e.matmul(bank.ap, w["lin1"][:, f * P:(f + 1) * P],
                                                                  self.xt[:, b * SEQ:(b + 1) * SEQ], start=True, stop=True),
                          turned[QT * b + QT - 1], bank.free)
                s = ac.do(lambda e, f=f, bank=bank: e.activation(hidden[:, f, :], bank.ap, ACT.Relu, bias=w["lin1_b"][:, f:f + 1]),
                          m, free)
                bank.free = [s]
                steps.append(s)
            bank = self.banks.next()
            for j in range(QT):
                for f in range(FT):
                    m = pe.do(lambda e, f=f, j=j, bank=bank: e.matmul(
                        bank.ap[:, j * P:(j + 1) * P], hidden[:, f, j * P:(j + 1) * P], w["lin2"][:, f * P:(f + 1) * P],
                        start=f == 0, stop=f == FT - 1), steps, bank.free)
            free = m
            o = y[:, QT * b:QT * b + QT, :]
            s1 = ve.do(lambda e, o=o, bank=bank: e.tensor_tensor(o, bank.ap.rearrange("p (t n) -> p t n", t=QT), o, ALU.add), m)
            bank.free = [s1]
            s2 = ve.do(lambda e, o=o: e.tensor_tensor(o, o, self.row["L3_xattn_lin2_b"].unsqueeze(1).to_broadcast([P, QT, P]), ALU.add), s1)
            done += [s2] * QT
        ready = self.normalize(y, y, done, gain=self.row["L3_xattn_ln3_g"], bias=self.row["L3_xattn_ln3_b"])
        for t in range(TILES):
            self.add_to_x(t, y[:, t, :], 3, ready[t])

    def mixture_attention(self):
        pe, ve, ac, po = self.pe, self.ve, self.ac, self.po
        self.begin("mixture")
        w, y = self.w[7], self.xn
        normed = self.normalize(self.x, y, [self.x_last[t] for t in range(TILES)])
        turned = self.turn(y, self.xt, normed)
        square, sim = self.carve(E3), self.carve(E3)
        ones = self.carve(P)
        s_one = po.do(lambda e: e.memset(ones, 1.0))
        s = ve.do(lambda e: e.tensor_tensor(square, w["sim"], w["sim"], ALU.mult), self.w_ready[7])
        bank = self.banks.next()
        m = pe.do(lambda e, bank=bank: e.matmul(bank.ap[:, 0:E3], ones, square, start=True, stop=True), s, s_one, bank.free)
        s = ve.do(lambda e, bank=bank: e.tensor_copy(square, bank.ap[:, 0:E3]), m)
        bank.free = [s]
        s = po.do(lambda e: e.tensor_tensor(square, square, self.half[:, 0:E3], ALU.pow), s)
        s = ve.do(lambda e: e.tensor_scalar(square, square, 1e-12, None, ALU.max), s)
        s = ve.do(lambda e: e.reciprocal(square, square), s)
        sim_ready = ve.do(lambda e: e.tensor_tensor(sim, w["sim"], square, ALU.mult), s)
        length, junk = self.carve(TILES), Ring([self.carve(P) for _ in range(2)])
        steps = []
        for t in range(TILES):
            z = junk.next()
            s = ve.do(lambda e, t=t, z=z: e.tensor_tensor_reduce(z.ap, y[:, t, :], y[:, t, :], 1.0, 0.0, ALU.mult, ALU.add,
                                                                 length[:, t:t + 1]), normed[t], z.free)
            z.free = [s]
            steps.append(s)
        s = po.do(lambda e: e.tensor_tensor(length, length, self.half[:, :], ALU.pow), steps)
        s = ve.do(lambda e: e.tensor_scalar(length, length, 1e-12, None, ALU.max), s)
        s_len = ve.do(lambda e: e.reciprocal(length, length), s)
        gate = self.carve(E3)
        s = ac.do(lambda e: e.activation(gate, self.row["L3_ffn_gates"], ACT.Exp, scale=-1.0))
        s = ve.do(lambda e: e.tensor_scalar(gate, gate, 1.0, None, ALU.add), s)
        s_gate = ve.do(lambda e: e.reciprocal(gate, gate), s)
        logits, s = self.token_products(sim, E3, turned, None, sim_ready)
        wide = [P, TILES, E3]
        per_token = lambda v: v.unsqueeze(2).to_broadcast(wide)
        s = ve.do(lambda e: e.tensor_tensor(logits, logits, per_token(length), ALU.mult), s, s_len)
        s = ve.do(lambda e: e.tensor_tensor(logits, logits, gate.unsqueeze(1).to_broadcast(wide), ALU.subtract), s, s_gate)
        active, idle, rest = self.carve(TILES, E3), self.carve(TILES), self.carve(TILES, E3)
        s1 = ve.do(lambda e: e.tensor_scalar(active, logits, 0.0, None, ALU.is_gt), s)
        s2 = ve.do(lambda e: e.tensor_reduce(idle, active, AX_X, ALU.add), s1)
        s_idle = ve.do(lambda e: e.tensor_scalar(idle, idle, 0.0, None, ALU.is_equal), s2)
        hot1, _, s3 = self.one_hot_of_max(logits, self.c["down16"], E3, s)
        s3 = ve.do(lambda e: e.scalar_tensor_tensor(rest, hot1, CAUSAL, logits, ALU.mult, ALU.add), s3)
        hot2, _, s3 = self.one_hot_of_max(rest, self.c["down16"], E3, s3)
        s3 = ve.do(lambda e: e.tensor_tensor(hot1, hot1, hot2, ALU.add), s3)
        s3 = ve.do(lambda e: e.tensor_tensor(hot1, hot1, per_token(idle), ALU.mult), s3, s_idle)
        s3 = ve.do(lambda e: e.tensor_tensor(active, active, hot1, ALU.add), s3)
        mix, top, total = logits, self.carve(TILES), self.carve(TILES)
        s3 = ve.do(lambda e: e.tensor_scalar(active, active, 1.0, -CAUSAL, ALU.subtract, ALU.mult), s3)
        s3 = ve.do(lambda e: e.scalar_tensor_tensor(mix, logits, 0.0, active, ALU.max, ALU.add), s3)
        s3 = ve.do(lambda e: e.tensor_reduce(top, mix, AX_X, ALU.max), s3)
        s3 = ve.do(lambda e: e.tensor_tensor(mix, mix, per_token(top), ALU.subtract), s3)
        s3 = ac.do(lambda e: e.activation(mix, mix, ACT.Exp), s3)
        s3 = ve.do(lambda e: e.tensor_reduce(total, mix, AX_X, ALU.add), s3)
        s3 = ve.do(lambda e: e.reciprocal(total, total), s3)
        s_mix = ve.do(lambda e: e.tensor_tensor(mix, mix, per_token(total), ALU.mult), s3)
        mix_t, mix_t_ready = self.turn_small(mix, E3, s_mix)
        parts = self.carve(TOKENS, dt=BF16)
        rest_t = self.carve(TOKENS)
        s_zero = po.do(lambda e: e.memset(parts[0:96, :], 0.0))
        s = ve.do(lambda e: e.tensor_copy(parts[0:E3, :], mix_t[0:E3, :]), mix_t_ready, s_zero)
        s = ve.do(lambda e: e.tensor_tensor(rest_t[0:E3, :], mix_t[0:E3, :], parts[0:E3, :], ALU.subtract), s)
        s = ve.do(lambda e: e.tensor_copy(parts[32:32 + E3, :], rest_t[0:E3, :]), s)
        second = self.carve(TOKENS, dt=BF16)
        s = ve.do(lambda e: e.tensor_copy(second[0:E3, :], rest_t[0:E3, :]), s)
        s_parts = ve.do(lambda e: e.tensor_tensor(parts[64:64 + E3, :], rest_t[0:E3, :], second[0:E3, :], ALU.subtract), s)
        spread1 = self.cb["spread1"].rearrange("p (e m) -> p e m", e=E3)
        spread2 = self.cb["spread2"].rearrange("p (e m) -> p e m", e=E3 // 2)

        def weights_of(selector, b):
            bank = self.banks.next()
            m = pe.do(lambda e: e.matmul(bank.ap, selector, parts[0:96, b * SEQ:(b + 1) * SEQ], start=True, stop=True),
                      s_parts, bank.free, self.setup)
            return bank, m

        scaled = Ring([self.carve(SEQ) for _ in range(4)])
        q_ring, k_ring = Ring([self.carve(SEQ) for _ in range(2)]), Ring([self.carve(SEQ) for _ in range(2)])
        v_half, v_full = Ring([self.carve(SEQ)]), Ring([self.carve(QT, P) for _ in range(2)])
        fixed = Ring([self.psum[:, n * BANK:(n + 1) * BANK] for n in (6, 7)])
        for slot, own in zip(fixed.slots, self.banks.slots[6:8]):
            slot.free = own.free
        self.banks = Ring([self.psum[:, n * BANK:(n + 1) * BANK] for n in range(6)])
        for slot in self.banks.slots:
            slot.free = [s_parts, turned, mix_t_ready]

        def project(b):
            bank_qk, bank_v = fixed.next(), fixed.next()
            halves = [None, None]
            pending = []

            def products(x, z, s):
                m = pe.do(lambda e, x=x, z=z: e.matmul(bank_qk.ap, w["qk"][:, x * P:(x + 1) * P], z.ap,
                                                       start=x == 0, stop=x == E3 - 1), s, bank_qk.free)
                o = slice(64 * (x % 2), 64 * (x % 2) + 64)
                m2 = pe.do(lambda e, x=x, z=z, o=o: e.matmul(bank_v.ap[o, :], w["v"][:, x * D3:(x + 1) * D3], z.ap,
                                                             start=x < 2, stop=x >= E3 - 2), bank_v.free)
                z.free = [m2]
                return m2

            for x in range(E3):
                wb, m = weights_of(spread1[0:96, x, :], b)
                z = scaled.next()
                s = ve.do(lambda e, wb=wb, z=z: e.tensor_tensor(z.ap, wb.ap, self.xt[:, b * SEQ:(b + 1) * SEQ], ALU.mult), m, z.free)
                wb.free = [s]
                pending.append((x, z, s))
                if len(pending) > 2:
                    last = products(*pending.pop(0))
            for p in pending:
                last = products(*p)
            q, k, vh, vf = q_ring.next(), k_ring.next(), v_half.next(), v_full.next()
            sq = ac.do(lambda e: e.activation(q.ap[0:D3, :], bank_qk.ap[0:D3, :], ACT.Copy), last, q.free)
            sk = ac.do(lambda e: e.activation(k.ap[0:D3, :], bank_qk.ap[D3:P, :], ACT.Copy), last, k.free)
            sv = ac.do(lambda e: e.activation(vh.ap, bank_v.ap, ACT.Copy), last, vh.free)
            bank_qk.free, bank_v.free = [sq, sk], [sv]
            bank = self.banks.next()
            for j in range(QT):
                m = pe.do(lambda e, j=j, bank=bank: e.matmul(bank.ap[:, j * P:(j + 1) * P], vh.ap[:, j * P:(j + 1) * P],
                                                             self.c["fold"], start=True, stop=True), sv, bank.free)
            vh.free = [m]
            s = ve.do(lambda e, bank=bank: e.tensor_copy(vf.ap.rearrange("p t n -> p (t n)"), bank.ap), m, vf.free)
            bank.free = [s]
            return b, q, k, vf, [sq, sk], s

        probs, probs_t = Ring([self.carve(SEQ) for _ in range(2)]), Ring([self.carve(QT, P) for _ in range(2)])
        attended = Ring([self.carve(SEQ) for _ in range(2)])
        mixed = Ring([self.carve(SEQ) for _ in range(3)])
        col = Ring([self.carve(3) for _ in range(4)])

        def attend(b, q, k, vf, qk_ready, v_ready):
            out_bank = self.banks.next()
            a_t = attended.next()
            for t in range(QT):
                n = (t + 1) * P
                bank, prob, c = self.banks.next(), probs.next(), col.next()
                if bank is out_bank:
                    bank = self.banks.next()
                for k0, k1 in ([(0, t * P)] if t else []) + [(t * P, n)]:
                    m = pe.do(lambda e, t=t, n=n, k0=k0, k1=k1, bank=bank: e.matmul(
                        bank.ap[:, k0:k1], q.ap[0:D3, t * P:n], k.ap[0:D3, k0:k1], start=True, stop=k1 < n), qk_ready, bank.free)
                m = pe.do(lambda e, t=t, n=n, bank=bank: e.matmul(bank.ap[:, t * P:n], self.cb["eye_b"], self.cb["causal"],
                                                                  start=False, stop=True))
                s = ve.do(lambda e, n=n, bank=bank, c=c: e.tensor_reduce(c.ap[:, 0:1], bank.ap[:, 0:n], AX_X, ALU.max, negate=True),
                          m, c.free)
                s = ve.do(lambda e, c=c: e.tensor_scalar(c.ap[:, 0:1], c.ap[:, 0:1], D3 ** -0.5, None, ALU.mult), s)
                s = ac.do(lambda e, n=n, bank=bank, c=c, prob=prob: e.activation(
                    prob.ap[:, 0:n], bank.ap[:, 0:n], ACT.Exp, bias=c.ap[:, 0:1], scale=D3 ** -0.5, accum_out=c.ap[:, 1:2]),
                    s, prob.free)
                bank.free = [s]
                s = ve.do(lambda e, c=c: e.reciprocal(c.ap[:, 2:3], c.ap[:, 1:2]), s)
                s = ve.do(lambda e, n=n, c=c, prob=prob: e.tensor_scalar(prob.ap[:, 0:n], prob.ap[:, 0:n], c.ap[:, 2:3], None,
                                                                         ALU.mult), s)
                c.free = [s]
                bank, pt = self.banks.next(), probs_t.next()
                if bank is out_bank:
                    bank = self.banks.next()
                for kt in range(t + 1):
                    m = pe.do(lambda e, kt=kt, bank=bank, prob=prob: e.transpose(
                        bank.ap[:, kt * P:(kt + 1) * P], prob.ap[:, kt * P:(kt + 1) * P], self.eye), s, bank.free)
                prob.free = [m]
                s = self.evacuate(pt.ap[:, 0:t + 1, :].rearrange("p t n -> p (t n)"), bank.ap[:, 0:n], m, pt.free)
                bank.free = [s]
                for kt in range(t + 1):
                    m = pe.do(lambda e, t=t, kt=kt, pt=pt: e.matmul(out_bank.ap[:, t * P:(t + 1) * P], vf.ap[:, kt, :],
                                                                    pt.ap[:, kt, :], start=kt == 0, stop=kt == t),
                              s, v_ready, out_bank.free)
                pt.free = [m]
            q.free = k.free = vf.free = [m]
            s = ac.do(lambda e: e.activation(a_t.ap, out_bank.ap, ACT.Copy), m, a_t.free)
            out_bank.free = [s]
            bank_o = [fixed.next()]
            o = bank_o[0]
            first_free = o.free
            pending = []

            def products(p, z, s):
                for j in range(QT):
                    m = pe.do(lambda e, p=p, z=z, j=j: e.matmul(
                        o.ap[:, j * P:(j + 1) * P], z.ap[:, j * P:(j + 1) * P], w["o"][:, p * P:(p + 1) * P],
                        start=p == 0 and j == 0, stop=p == E3 // 2 - 1, skip_group_check=True), s, first_free)
                z.free = [m]
                return m

            for p in range(E3 // 2):
                wb, m = weights_of(spread2[0:96, p, :], b)
                z = mixed.next()
                sz = ve.do(lambda e, wb=wb, z=z: e.tensor_tensor(z.ap, wb.ap, a_t.ap, ALU.mult), m, z.free, s)
                wb.free = [sz]
                pending.append((p, z, sz))
                if len(pending) > 1:
                    last = products(*pending.pop(0))
            for p in pending:
                last = products(*p)
            a_t.free = [sz]
            o.free = [self.add_to_x(QT * b + j, o.ap[:, j * P:(j + 1) * P], 7, last) for j in range(QT)]

        waiting = None
        for b in range(BATCH):
            now = project(b)
            if waiting:
                attend(*waiting)
            waiting = now
        attend(*waiting)

    def close(self):
        self.begin("close")
        out = self.dram["out"].rearrange("(t p) d -> p t d", p=P)
        store = self.dma("out", out, self.x[:, :, :], [e.fence for e in self.engines[:4]])
        self.sp.do(lambda e: e.nop(), store, self.loads)


STAGES = [Program.image_attention, Program.top1_experts, Program.one_head, Program.batch_attention,
          Program.masked_attention, Program.scaled_feed_forward, Program.decoder_block, Program.mixture_attention]


def build(nc, dram, const_widths, const_b_widths):
    with ExitStack() as ctx:
        p = Program(nc, ctx, dram, const_widths, const_b_widths)
        p.open()
        for stage in STAGES:
            stage(p)
        p.close()
        p.finish()


def kernel(**inputs):
    import concourse.bacc as bacc
    from concourse.bass_utils import run_bass_kernel_spmd

    i = {k: np.asarray(v) for k, v in inputs.items()}
    const, const_widths, const_b, const_b_widths = constants()
    arrays = {
        "x": i["x"].reshape(TOKENS, P), "ctx": i["ctx_1024"].reshape(CTX_ROWS, P),
        "mask": i["mask_BxSxS2_bf0"].reshape(TOKENS, CTX),
        "rows": np.concatenate([i[k].reshape(-1) for k in ROWS])[None],
        "small": np.concatenate([i["L0_ffn_b2"], i["L1_ffn_b2"]], 1),
        "const": const, "const_b": const_b,
    }
    for k, parts in enumerate(WEIGHTS):
        arrays[f"weights{k}"] = np.concatenate([lay(i) for _, lay in parts.values()], 1)
    nc = bacc.Bacc("TRN2", target_bir_lowering=False, num_devices=1)
    dram, feed = {}, {}
    for name, a in arrays.items():
        a = np.ascontiguousarray(a)
        feed[f"in_{name}"] = a
        dram[name] = nc.dram_tensor(f"in_{name}", a.shape, mybir.dt.from_np(a.dtype), kind="ExternalInput").ap()
    dram["out"] = nc.dram_tensor("out", (TOKENS, P), F32, kind="ExternalOutput").ap()
    build(nc, dram, const_widths, const_b_widths)
    r = run_bass_kernel_spmd(nc, [feed], core_ids=[0])
    return r.results[0]["out"].reshape(BATCH, SEQ, P)
```

```python
from contextlib import ExitStack

import numpy as np

import concourse.bass as bass
from concourse import mybir

ALU = mybir.AluOpType
ACT = mybir.ActivationFunctionType
F32 = mybir.dt.float32
BF16 = mybir.dt.bfloat16
U8 = mybir.dt.uint8
U16 = mybir.dt.uint16
AX_X = mybir.AxisListType.X

P = 128
BATCH, SEQ, CTX = 4, 512, 154
TOKENS = BATCH * SEQ
TILES = TOKENS // P
QT = SEQ // P
CTX_ROWS = BATCH * CTX
CTX_TILES = -(-CTX_ROWS // P)
CTX_LAST = CTX_ROWS - (CTX_TILES - 1) * P
CTX_REST = CTX - P
BANK = 512
EPS = 1e-5
MASKED = -1e18
CAUSAL = -1e30

H0, D0 = 16, 64
PAIRS = H0 // 2
KEYS0 = SEQ + CTX
KT0 = -(-KEYS0 // P)
EXPERTS, FF = 8, 512
ROOM = 10
FT = FF // P
E3, D3 = 16, 64


def _cols(v):
    return v.reshape(-1, P).T


def _kt(w):
    k = w.shape[0] // P
    return w.reshape(k, P, -1).transpose(1, 0, 2).reshape(P, -1)


WEIGHTS = [
    {
        "ln1_g": (1, lambda i: _cols(i["L0_xattn_ln1_g"])), "ln1_b": (1, lambda i: _cols(i["L0_xattn_ln1_b"])),
        "ln2_g": (1, lambda i: _cols(i["L0_xattn_ln2_g"])), "ln2_b": (1, lambda i: _cols(i["L0_xattn_ln2_b"])),
        "wq": (1024, lambda i: i["L0_xattn_Wq"]), "wkv": (2048, lambda i: i["L0_xattn_Wkv"]),
        "wo": (1024, lambda i: _kt(i["L0_xattn_Wo"])),
    },
    {
        "gate": (EXPERTS, lambda i: i["L0_ffn_gate_w"].T),
        "w1": (EXPERTS * FF, lambda i: i["L0_ffn_w1"].transpose(1, 0, 2).reshape(P, -1)),
        "b1": (EXPERTS * FT, lambda i: _cols(i["L0_ffn_b1"].reshape(-1))),
        "w2": (EXPERTS * FF, lambda i: _kt(i["L0_ffn_w2"].reshape(-1, P))),
    },
    {
        "wq": (P, lambda i: i["L1_xattn_Wq"].T), "wk": (P, lambda i: i["L1_xattn_Wk"].T),
        "wv": (P, lambda i: i["L1_xattn_Wv"].T),
        "bq": (1, lambda i: _cols(i["L1_xattn_bq"])), "bk": (1, lambda i: _cols(i["L1_xattn_bk"])),
    },
    {
        "in": (3 * P, lambda i: i["L1_ffn_in_proj_w"].T), "out": (P, lambda i: i["L1_ffn_out_w"].T),
        "router": (EXPERTS, lambda i: i["L1_ffn_router_w"].T),
        "w1": (EXPERTS * P, lambda i: i["L1_ffn_w1"].transpose(2, 0, 1).reshape(P, -1)),
        "w2": (EXPERTS * P, lambda i: i["L1_ffn_w2"].transpose(2, 0, 1).reshape(P, -1)),
        "b1": (EXPERTS, lambda i: i["L1_ffn_b1"].T),
    },
    {
        "wq": (P, lambda i: i["L2_xattn_Wq"].T), "wk": (P, lambda i: i["L2_xattn_Wk"].T),
        "wv": (P, lambda i: i["L2_xattn_Wv"].T), "wo": (P, lambda i: i["L2_xattn_Wo"].T),
        "bq": (1, lambda i: _cols(i["L2_xattn_bq"])), "bk": (1, lambda i: _cols(i["L2_xattn_bk"])),
        "bv": (1, lambda i: _cols(i["L2_xattn_bv"])),
    },
    {
        "w1": (FF, lambda i: i["L2_ffn_w1_w"].T), "w2": (FF, lambda i: i["L2_ffn_w2_w"].T),
        "h1": (FT * FF, lambda i: _kt(i["L2_ffn_h1_w"].T)), "h2": (FT * FF, lambda i: _kt(i["L2_ffn_h2_w"].T)),
        "w3": (FT * P, lambda i: _kt(i["L2_ffn_w3_w"].T)),
        "s1": (FT, lambda i: _cols(i["L2_ffn_w1_s"])), "s2": (FT, lambda i: _cols(i["L2_ffn_w2_s"])),
        "sh1": (FT, lambda i: _cols(i["L2_ffn_h1_s"])), "sh2": (FT, lambda i: _cols(i["L2_ffn_h2_s"])),
    },
    {
        "qkv": (3 * P, lambda i: i["L3_xattn_qkv_w"].T), "sa_out": (P, lambda i: i["L3_xattn_sa_out_w"].T),
        "in": (3 * P, lambda i: i["L3_xattn_in_proj_w"].T), "mha_out": (P, lambda i: i["L3_xattn_mha_out_w"].T),
        "lin1": (FF, lambda i: i["L3_xattn_lin1_w"].T), "lin2": (FT * P, lambda i: _kt(i["L3_xattn_lin2_w"].T)),
        "in_b": (3, lambda i: _cols(i["L3_xattn_in_proj_b"])), "lin1_b": (FT, lambda i: _cols(i["L3_xattn_lin1_b"])),
    },
    {
        "sim": (E3, lambda i: i["L3_ffn_sim_matrix"]),
        "qk": (E3 * 2 * D3, lambda i: np.concatenate([i["L3_ffn_q_proj"], i["L3_ffn_k_proj"]], 2)
               .transpose(1, 0, 2).reshape(P, -1)),
        "v": (E3 * D3, lambda i: i["L3_ffn_v_proj"].transpose(1, 0, 2).reshape(P, -1)),
        "o": (E3 // 2 * P, lambda i: _kt(i["L3_ffn_o_proj"].reshape(-1, P))),
    },
]

ROWS = {
    "g_xattn": 4, "g_ffn": 4, "L0_ffn_gate_b": 8, "L0_ffn_expert_bias": 8, "L1_xattn_bv": P,
    "L1_ffn_in_proj_b": 3 * P, "L1_ffn_out_b": P, "L1_ffn_ln1_g": P, "L1_ffn_ln1_b": P, "L1_ffn_router_b": 8,
    "L1_ffn_ln2_g": P, "L1_ffn_ln2_b": P, "L2_xattn_bo": P, "L2_ffn_w3_s": P, "L3_xattn_qkv_b": 3 * P,
    "L3_xattn_sa_out_b": P, "L3_xattn_mha_out_b": P, "L3_xattn_lin2_b": P, "L3_xattn_ln1_g": P,
    "L3_xattn_ln1_b": P, "L3_xattn_ln2_g": P, "L3_xattn_ln2_b": P, "L3_xattn_ln3_g": P, "L3_xattn_ln3_b": P,
    "L3_ffn_gates": 16,
}


def _offsets(widths):
    at, out = 0, {}
    for name, n in widths.items():
        out[name] = (at, n)
        at += n
    return out, at


GROUPS, WIDE = 4, P // 4


def flat_chunks(heads):
    n = heads // GROUPS * CTX
    return [(c * P, min(P, n - c * P)) for c in range(-(-n // P))]


def constants():
    eye = np.eye(P, dtype=np.float32)
    c = {"eye": eye}
    for heads in (16, 8):
        d = P // heads
        c[f"head{heads}"] = (np.arange(P)[:, None] // d == np.arange(heads)[None]).astype(np.float32)
        chunks = flat_chunks(heads)
        m = np.zeros((P, len(chunks), GROUPS, heads // GROUPS), np.float32)
        for n, (f0, rows) in enumerate(chunks):
            for r in range(rows):
                m[r, n, :, (f0 + r) // CTX] = 1.0
        c[f"block{heads}"] = m.reshape(P, -1)
    c["down8"] = np.tile(np.arange(8, 0, -1, dtype=np.float32), (P, 1))
    c["down16"] = np.tile(np.arange(16, 0, -1, dtype=np.float32), (P, 1))
    c["fold"] = np.tile(np.eye(D3, dtype=np.float32), (2, 2))
    b = {"eye_b": eye}
    b["causal"] = np.where(np.arange(P)[None] <= np.arange(P)[:, None], 0.0, CAUSAL).astype(np.float32)
    one = np.zeros((P, E3, P), np.float32)
    two = np.zeros((P, E3 // 2, P), np.float32)
    for part in range(3):
        for e in range(E3):
            one[32 * part + e, e, :] = 1.0
            two[32 * part + e, e // 2, (e % 2) * D3:(e % 2 + 1) * D3] = 1.0
    b["spread1"], b["spread2"] = one.reshape(P, -1), two.reshape(P, -1)
    f = np.concatenate(list(c.values()), 1)
    bb = (np.concatenate(list(b.values()), 1).view(np.uint32) >> 16).astype(np.uint16)
    return f, {k: v.shape[1] for k, v in c.items()}, bb, {k: v.shape[1] for k, v in b.items()}


class Step:

    def __init__(self, engine, emit, after):
        self.engine, self.emit, self.after = engine, emit, after
        self.sem, self.value, self.wanted = None, None, False


def _flat(after):
    for a in after:
        if isinstance(a, (list, tuple)):
            yield from _flat(a)
        elif a is not None:
            yield a


class Engine:
    def __init__(self, name):
        self.name, self.queue, self.sem = name, [], None

    def do(self, emit, *after):
        step = Step(self, emit, list(_flat(after)))
        for a in step.after:
            a.wanted = True
        step.sem = self.sem
        self.queue.append(step)
        return step

    def count(self):
        at = {}
        for s in self.queue:
            if s.wanted and s.value is None:
                at[s.sem] = at.get(s.sem, 0) + 1
                s.value = at[s.sem]

    def run(self, eng):
        seen = {}
        for s in self.queue:
            need = {}
            for a in s.after:
                need[a.sem] = max(need.get(a.sem, 0), a.value)
            for sem, value in need.items():
                if seen.get(sem, 0) < value:
                    eng.wait_ge(sem, value)
                    seen[sem] = value
            last = s.emit(eng)
            if s.wanted:
                last.then_inc(s.sem, 16 if isinstance(s, Load) else 1)


class Load(Step):
    pass


class Bank:

    def __init__(self, ap):
        self.ap, self.free = ap, []


class Ring:

    def __init__(self, aps):
        self.slots, self.at = [Bank(a) for a in aps], -1

    def next(self):
        self.at = (self.at + 1) % len(self.slots)
        return self.slots[self.at]


class Program:
    def __init__(self, nc, ctx, dram, const_widths, const_b_widths):
        self.nc, self.ctx, self.dram = nc, ctx, dram
        self.pe, self.ve, self.ac, self.po, self.sp = (Engine(n) for n in
                                                       ("tensor", "vector", "scalar", "gpsimd", "sync"))
        self.engines = [self.pe, self.ve, self.ac, self.po, self.sp]
        self.loads = []
        self.widths = {"const": const_widths, "const_b": const_b_widths}
        self.evacuations = 0

    def sb(self, name, shape, dt=F32):
        return self.ctx.enter_context(self.nc.sbuf_tensor(name, shape, dt))

    def stage(self, name):
        for e in self.engines[:4]:
            e.sem = self.ctx.enter_context(self.nc.semaphore(f"{e.name}_{name}"))

    def load_sem(self, name):
        return self.ctx.enter_context(self.nc.semaphore(f"dma_{name}"))

    def dma(self, name, out, in_, *after, sem=None, turn=1, engine=None):
        engine = engine or self.sp
        step = Load(engine, lambda e: e.dma_start(out, in_), list(_flat(after)))
        for a in step.after:
            a.wanted = True
        step.sem = sem or self.load_sem(name)
        step.value, step.wanted = 16 * turn, True
        engine.queue.append(step)
        self.loads.append(step)
        return step

    def evacuate(self, out, psum, *after):
        self.evacuations += 1
        if self.evacuations % 2:
            return self.ac.do(lambda e: e.activation(out, psum, ACT.Copy), *after)
        return self.ve.do(lambda e: e.tensor_copy(out, psum), *after)

    def finish(self):
        for e in self.engines:
            e.count()
        with self.nc.Block() as block:
            for e in self.engines:
                place = {"tensor": block.tensor, "vector": block.vector, "scalar": block.scalar,
                         "gpsimd": block.gpsimd, "sync": block.sync}[e.name]
                place(lambda eng, e=e: e.run(eng))

    def carve(self, *shape, dt=F32):
        n = int(np.prod(shape))
        words = n if dt == F32 else -(-n // 2)
        ap = self.work[:, self.work_at:self.work_at + words]
        self.work_at += words
        assert self.work_at <= self.work_words, self.work_at
        if dt != F32:
            ap = ap.bitcast(dt)
        if len(shape) == 2:
            return ap.rearrange("p (a b) -> p a b", a=shape[0])
        if len(shape) == 3:
            return ap.rearrange("p (a b c) -> p a b c", a=shape[0], b=shape[1])
        if len(shape) == 4:
            return ap.rearrange("p (a b c d) -> p a b c d", a=shape[0], b=shape[1], c=shape[2])
        return ap

    def begin(self, name):
        before = [e.queue[-1] for e in self.engines[:4] if e.queue]
        self.do_chores(keep=1)
        self.stage(name)
        self.work_at = 0
        self.before = before
        for e in self.engines[:4]:
            e.fence = e.do(lambda g: g.nop(), *before)

    def chore(self):
        if self.chores:
            self.chores.pop(0)()

    def store(self, b):
        rows = slice(QT * b, QT * b + QT)
        out = self.dram["out"].rearrange("(t p) d -> p t d", p=P)
        self.stores.append(self.dma(f"out{b}", out[:, rows, :], self.x[:, rows, :], self.x_last[rows]))

    def do_chores(self, keep=0):
        while len(self.chores) > keep:
            self.chore()

    def follow(self, b):
        rows = slice(QT * b, QT * b + QT)
        self.parity[b] ^= 1
        room = self.room[:, 2 * b + self.parity[b], :]
        ((measure, scale),), normed = self.norm_groups(
            self.x[:, rows, :], self.xn[:, rows, :], self.x_last[rows], QT, room=room, free=self.xn_free[b])

        def pause():
            pass

        def turn():
            turned = self.turn(self.xn[:, rows, :], self.xt[:, b * SEQ:(b + 1) * SEQ], normed, n=QT, after=(self.xt_free[b],))
            self.next_normed[rows], self.next_turned[rows] = normed, turned

        self.chores += [measure, scale, pause, turn]

    def stream(self):
        return self.next_normed, self.next_turned

    def norm_groups(self, src, dst, ready, n=TILES, rows=P, gain=None, bias=None, room=None, free=None):
        ve, po = self.ve, self.po
        room = self.carve(ROOM * n) if room is None else room
        stats, mv = (room[:, a * n:z * n].rearrange("p (t k) -> p t k", t=n) for a, z in ((0, 6), (6, 8)))
        var, rstd = room[:, 8 * n:9 * n], room[:, 9 * n:10 * n]
        full = n if rows == P else n - 1
        groups = [(P, a, min(a + QT, full)) for a in range(0, full, QT)] + ([(rows, full, n)] if full < n else [])
        out, power = [None] * n, {}

        def measure(r, a, b):
            for t in range(a, b):
                s = ve.do(lambda e, t=t: e.bn_stats(stats[0:r, t, :], src[0:r, t, :]), ready[t])
            for t in range(a, b):
                m = ve.do(lambda e, t=t: e.bn_aggr(mv[0:r, t, :], stats[0:r, t, :]), s)
            s = ve.do(lambda e: e.tensor_scalar(var[0:r, a:b], mv[0:r, a:b, 1], EPS, None, ALU.add), m)
            power[a] = po.do(lambda e: e.tensor_tensor(rstd[0:r, a:b], var[0:r, a:b], self.minus_half[0:r, 0:b - a], ALU.pow),
                             s, self.halves)

        def scale(r, a, b):
            for t in range(a, b):
                out[t] = ve.do(lambda e, t=t: e.tensor_scalar(dst[0:r, t, :], src[0:r, t, :], mv[0:r, t, 0:1],
                                                              rstd[0:r, t:t + 1], ALU.subtract, ALU.mult), power[a], free)
            if gain is not None:
                o, wide = dst[0:r, a:b, :], [r, b - a, P]
                s = ve.do(lambda e: e.tensor_tensor(o, o, gain[0:r].unsqueeze(1).to_broadcast(wide), ALU.mult), out[a:b])
                s = ve.do(lambda e: e.tensor_tensor(o, o, bias[0:r].unsqueeze(1).to_broadcast(wide), ALU.add), s)
                out[a:b] = [s] * (b - a)

        return [(lambda g=g: measure(*g), lambda g=g: scale(*g)) for g in groups], out

    def normalize(self, *args, **kwargs):
        groups, out = self.norm_groups(*args, **kwargs)
        last = None
        for measure, scale in groups:
            measure()
            if last:
                last()
            last = scale
        last()
        return out

    def turn(self, src, dst, ready, rows=P, n=TILES, scale=None, shift=None, after=()):
        out = []
        for g in range(0, n, 4):
            bank = self.banks.next()
            tiles = range(g, min(g + 4, n))
            width = sum(rows if t == n - 1 else P for t in tiles)
            for t in tiles:
                r = rows if t == n - 1 else P
                s = self.pe.do(lambda e, t=t, r=r, c=(t - g) * P, b=bank.ap: e.transpose(
                    b[:, c:c + r], src[0:r, t, :], self.eye[0:r, 0:r]), ready[t], bank.free, self.setup)
            o, i = dst[:, g * P:g * P + width], bank.ap[:, 0:width]
            if scale is not None:
                if (g // 4) % 2:
                    v = self.ve.do(lambda e, o=o, i=i: e.tensor_scalar(o, i, scale, shift, ALU.mult, ALU.add), s, *after)
                else:
                    v = self.ac.do(lambda e, o=o, i=i: e.activation(o, i, ACT.Identity, bias=shift, scale=scale), s, *after)
            else:
                v = self.evacuate(o, i, s, *after)
            bank.free = [v]
            out += [v] * len(tiles)
        return out

    def add_to_x(self, tile, psum, gate, ready, row=None, factor=None, op=ALU.add):
        ve, x = self.ve, self.x[:, tile, :]
        g = self.gates[:, gate:gate + 1]
        if row is None:
            self.x_last[tile] = ve.do(lambda e: e.scalar_tensor_tensor(x, psum, g, x, ALU.mult, ALU.add),
                                      ready, self.x_last[tile], self.rows_ready)
            return self.x_last[tile]
        t = self.scratch[:, tile % 4, :]
        if factor is None:
            s = ve.do(lambda e: e.tensor_tensor(t, psum, row, op), ready, self.rows_ready, self.scratch_free[tile % 4])
        else:
            s = ve.do(lambda e: e.scalar_tensor_tensor(t, psum, factor, row, ALU.mult, ALU.add), ready,
                      self.scratch_free[tile % 4])
        self.x_last[tile] = ve.do(lambda e: e.scalar_tensor_tensor(x, t, g, x, ALU.mult, ALU.add), s, self.x_last[tile])
        self.scratch_free[tile % 4] = self.x_last[tile]
        return s

    def add_batch_to_x(self, b, y, gate, ready):
        rows = slice(QT * b, QT * b + QT)
        x, g = self.x[:, rows, :], self.gates[:, gate:gate + 1]
        s = self.ve.do(lambda e: e.scalar_tensor_tensor(x, y[:, rows, :], g, x, ALU.mult, ALU.add), ready, self.x_last[rows],
                       self.rows_ready)
        self.x_last[rows] = [s] * QT
        return s

    def open(self):
        ve, po, pe, nc = self.ve, self.po, self.pe, self.nc
        self.stage("setup")
        d = self.dram
        psum = self.ctx.enter_context(nc.psum_tensor("banks", [P, 8 * BANK], F32))
        self.psum = psum
        self.banks = Ring([psum[:, b * BANK:(b + 1) * BANK] for b in range(8)])
        self.x = self.sb("x", [P, TILES, P])
        self.xn = self.sb("xn", [P, TILES, P])
        self.xt = self.sb("xt", [P, TOKENS])
        self.context = self.sb("context", [P, BATCH, 2 * CTX])
        self.room = self.sb("norm_room", [P, 2 * BATCH, ROOM * QT])
        self.parity, self.chores = [0] * BATCH, []
        self.next_normed, self.next_turned = [None] * TILES, [None] * TILES
        self.stores = []
        self.xn_free, self.xt_free = [None] * BATCH, [None] * BATCH
        self.scratch = self.sb("scratch", [P, 4, P])
        self.gates = self.sb("gates", [P, 8])
        self.x_last = [None] * TILES
        self.scratch_free = [None] * 4
        self.minus_half = self.sb("minus_half", [P, TILES])
        self.half = self.sb("half", [P, TILES])
        self.sim, self.gate = self.sb("similarity", [P, E3])[:, :], self.sb("router_gate", [P, E3])[:, :]
        slots = {"a": self.sb("weights_a", [P, 4116]), "b": self.sb("weights_b", [P, 8232]),
                 "c": self.sb("weights_c", [P, 3480])}
        self.work_words = 21800
        self.work = self.sb("work", [P, self.work_words])
        const, cw = self.sb("const", [P, sum(self.widths["const"].values())]), self.widths["const"]
        cb = self.sb("const_b", [P, sum(self.widths["const_b"].values())], BF16)
        rows_at, rows_n = _offsets(ROWS)
        rows = self.sb("rows", [P, rows_n])
        self.small = self.sb("small", [8, 2 * P])
        self.row = {k: rows[:, a:a + n] for k, (a, n) in rows_at.items()}
        self.c = {k: const[:, a:a + n] for k, (a, n) in _offsets(cw)[0].items()}
        self.cb = {k: cb[:, a:a + n] for k, (a, n) in _offsets(self.widths["const_b"])[0].items()}
        self.eye = self.c["eye"]

        self.w, self.w_ready, self.weight_plan = [], [], []
        for k, (slot, base) in enumerate([("a", 0), ("b", 0), ("c", 0), ("c", 386), ("c", 386 + 2576),
                                          ("b", 0), ("b", 5648), ("a", 0)]):
            at, n = _offsets({name: w for name, (w, _) in WEIGHTS[k].items()})
            assert base + n <= slots[slot].shape[1], (k, base + n)
            self.w.append({name: slots[slot][:, base + a:base + a + m] for name, (a, m) in at.items()})
            self.weight_plan.append((slots[slot][:, base:base + n], d[f"weights{k}"]))

        self.begin_work()
        self.ctx_rows = ctx_rows = self.carve(CTX_TILES, P)
        xr = d["x"].rearrange("(t p) d -> p t d", p=P)
        self.load_x = [self.dma(f"x{b}", self.x[:, QT * b:QT * b + QT, :], xr[:, QT * b:QT * b + QT, :])
                       for b in range(BATCH)]
        load_c = self.dma("const", const[:, :], d["const"])
        full = CTX_TILES - 1
        self.load_ctx = [self.dma("context", ctx_rows[:, 0:full, :],
                                  d["ctx"][0:full * P, :].rearrange("(t p) d -> p t d", p=P)),
                         self.dma("context_last", ctx_rows[0:CTX_LAST, full, :], d["ctx"][full * P:CTX_ROWS, :])]
        self.load_weights(0)
        load_rows = self.dma("rows", rows[:, :], d["rows"].to_broadcast([P, rows_n]))
        load_cb = self.dma("const_b", cb[:, :].bitcast(U16), d["const_b"])
        load_small = self.dma("small", self.small[:, :], d["small"])
        for k in (1, 2, 3, 4):
            self.load_weights(k)

        halves = [po.do(lambda e: e.memset(self.minus_half[:, :], -0.5)), po.do(lambda e: e.memset(self.half[:, :], 0.5))]
        clean = ve.do(lambda e: e.memset(psum[:, 5 * BANK:6 * BANK], 0.0))
        self.setup, self.halves = [load_c, clean], halves
        self.ctxn_t = self.sb("ctxn_t", [P, CTX_ROWS])

        def late():
            tanh = self.ac.do(lambda e: e.activation(self.gates[:, :], rows[:, 0:8], ACT.Tanh), load_rows)
            self.rows_ready = [load_rows, load_small, load_cb, tanh]
        self.late_tables = late

    def open_context(self):
        ctxn, whole = self.carve(CTX_TILES, P), self.carve(CTX_ROWS)
        w, ve = self.w[0], self.ve
        ready = self.normalize(self.ctx_rows, ctxn, [self.load_ctx] * CTX_TILES, CTX_TILES, CTX_LAST)
        self.ctxn_ready = self.turn(ctxn, self.ctxn_t, ready, rows=CTX_LAST, n=CTX_TILES,
                                    scale=w["ln1_g"], shift=w["ln1_b"], after=(self.w_ready[0],))
        turned = self.turn(self.ctx_rows, whole, [self.load_ctx] * CTX_TILES, rows=CTX_LAST, n=CTX_TILES)
        by_batch = whole.rearrange("p (b k) -> p b k", b=BATCH)
        self.context_ready = [self.po.do(lambda e, c=c: e.tensor_copy(self.context[:, :, c * CTX:(c + 1) * CTX], by_batch),
                                         turned) for c in range(2)]

    def begin_work(self):
        self.work_at = 0

    def load_weights(self, k, *after):
        out, src = self.weight_plan[k]
        self.w_ready += [None] * (k + 1 - len(self.w_ready))
        self.w_ready[k] = self.dma(f"weights{k}", out, src, *after)

    def image_attention(self):
        pe, ve, ac, po = self.pe, self.ve, self.ac, self.po
        w, x = self.w[0], self.x
        first = self.normalize(x[:, 0:QT, :], self.xn[:, 0:QT, :], [self.load_x[0]] * QT, QT)
        second = self.normalize(self.xn[:, 0:QT, :], self.xn[:, 0:QT, :], first, QT)
        ln2 = {"scale": w["ln2_g"], "shift": w["ln2_b"], "after": (self.w_ready[0],)}
        latents = self.turn(self.xn[:, 0:QT, :], self.xt[:, 0:SEQ], second, n=QT, **ln2)
        self.open_context()
        self.begin("image")

        q_split = Ring([self.carve(2, SEQ, dt=BF16) for _ in range(2)])
        k_split = Ring([self.carve(2, 2, KEYS0, dt=BF16) for _ in range(2)])
        values = Ring([self.carve(KT0, P) for _ in range(3)])
        probs = Ring([self.carve(KEYS0) for _ in range(4)])
        probs_t = Ring([self.carve(2, KT0, 2 * P) for _ in range(2)])
        sums = Ring([self.carve(4) for _ in range(2)])
        inverse = Ring([self.carve(4) for _ in range(2)])
        spread = Ring([self.carve(2, 2, D0) for _ in range(2)])
        neg_max = Ring([self.carve(1) for _ in range(4)])
        mixed = self.carve(PAIRS, SEQ)
        mixed_free = [None, None]
        scores = Ring([self.psum[:, 0:2 * BANK], self.psum[:, 2 * BANK:4 * BANK]])
        turned = [Bank(self.psum[:, 4 * BANK:5 * BANK]), Bank(self.psum[:, 5 * BANK:6 * BANK])]
        out_bank = Bank(self.psum[:, 6 * BANK:7 * BANK])
        side = Bank(self.psum[:, 7 * BANK:8 * BANK])
        for bank in (*scores.slots, *turned, out_bank, side):
            bank.free = [b.free for b in self.banks.slots]
        self.banks = Ring([])
        self.banks.slots = turned

        copy_sems = {(s, h): self.load_sem(f"keys{s}{h}") for s in range(2) for h in range(2)}
        copy_turn = {key: 0 for key in copy_sems}
        groups = [(b, p) for b in range(BATCH) for p in range(PAIRS)]
        state = {}

        def project_q(g, n):
            b, p = g
            st = state[g] = {"q": q_split.next(), "k": k_split.next(), "v": values.next(), "n": n}
            m = pe.do(lambda e: e.matmul(side.ap[:, 0:SEQ], w["wq"][:, p * P:(p + 1) * P],
                                         self.xt[:, b * SEQ:(b + 1) * SEQ], start=True, stop=True),
                      latents[4 * b + 3], side.free)
            q, hi = st["q"].ap, []
            for h in (0, 1):
                own = slice(64 * h, 64 * h + 64)
                hi.append(ac.do(lambda e, h=h, own=own: e.activation(q[own, h, :], side.ap[own, 0:SEQ], ACT.Copy, scale=D0 ** -0.5),
                                m, st["q"].free))
            side.free = [None]

            def low(h):
                own, other = slice(64 * h, 64 * h + 64), slice(64 - 64 * h, 128 - 64 * h)
                return ve.do(lambda e, h=h, own=own, other=other: e.scalar_tensor_tensor(
                    q[other, h, :], side.ap[own, 0:SEQ], D0 ** -0.5, q[own, h, :], ALU.mult, ALU.subtract), hi[h], st["q"].free)

            def rest():
                for h in (0, 1):
                    st[f"q{h}"] = low(h)
                side.free = [hi, st["q0"], st["q1"]]
            return rest

        def project_k(g, part):
            b, p = g
            st = state[g]
            src, n, c0 = ((self.xt[:, b * SEQ:(b + 1) * SEQ], SEQ, 0) if part == 0 else
                          (self.ctxn_t[:, b * CTX:(b + 1) * CTX], CTX, SEQ))
            m = pe.do(lambda e: e.matmul(side.ap[:, 0:n], w["wkv"][:, p * P:(p + 1) * P], src, start=True, stop=True),
                      side.free, self.ctxn_ready if part else None)
            if part == 1:
                for c, r0, rows in ((P * 2, 0, P), (P * 3, P, CTX_REST)):
                    m = pe.do(lambda e, c=c, r0=r0, rows=rows: e.matmul(
                        side.ap[0:rows, c:c + P], self.ctxn_t[:, b * CTX + r0:b * CTX + r0 + rows],
                        w["wkv"][:, 1024 + p * P:1024 + (p + 1) * P], start=True, stop=True))
            k, hi = st["k"].ap, []
            for h in (0, 1):
                own = slice(64 * h, 64 * h + 64)
                hi.append(ac.do(lambda e, h=h, own=own: e.activation(k[own, h, 0, c0:c0 + n], side.ap[own, 0:n], ACT.Copy),
                                m, st["k"].free))
            if part == 1:
                v, free = st["v"].ap, st["v"].free
                st["v_ready"] = [
                    ac.do(lambda e: e.activation(v[:, 4, :], side.ap[:, 2 * P:3 * P], ACT.Copy), free),
                    ac.do(lambda e: e.activation(v[0:CTX_REST, 5, :], side.ap[0:CTX_REST, 3 * P:4 * P], ACT.Copy))]

            def rest():
                low = []
                for h in (0, 1):
                    own = slice(64 * h, 64 * h + 64)
                    low.append(ve.do(lambda e, h=h, own=own: e.tensor_tensor(
                        k[own, h, 1, c0:c0 + n], side.ap[own, 0:n], k[own, h, 0, c0:c0 + n], ALU.subtract), hi[h],
                        st["v_ready"] if part else None))
                    if part == 1:
                        slot, other = st["n"] % 2, slice(64 - 64 * h, 128 - 64 * h)
                        copy_turn[slot, h] += 1
                        st[f"k{h}"] = self.dma("keys", k[other, h, :, :], k[own, h, :, :], low[h], st["k"].free,
                                               sem=copy_sems[slot, h], turn=copy_turn[slot, h])
                side.free = [low]
            return rest

        def project_v(g, n):
            b, p = g
            st = state[g]
            for t in range(QT):
                m = pe.do(lambda e, t=t: e.matmul(
                    side.ap[:, t * P:(t + 1) * P], self.xt[:, b * SEQ + t * P:b * SEQ + (t + 1) * P],
                    w["wkv"][:, 1024 + p * P:1024 + (p + 1) * P], start=True, stop=True), side.free)
            self.xt_free[b] = m
            a = ac.do(lambda e: e.activation(st["v"].ap[:, 0:QT, :], side.ap.rearrange("p (t n) -> p t n", t=QT), ACT.Copy),
                      m, st["v"].free)
            side.free = [a]
            st["v_ready"].append(a)

        pieces = {0: project_q, 2: lambda g, n: project_k(g, 0), 4: lambda g, n: project_k(g, 1),
                  6: project_v}
        for s in sorted(pieces):
            rest = pieces[s](groups[0], 0)
            if rest:
                rest()

        def scores_of(u, h, j):
            g, half = u["group"], u["half"]
            st, slot, qt = state[g], scores.next(), 2 * half + j
            lhs = st["q"].ap[:, h, qt * P:(qt + 1) * P]
            k = st["k"].ap
            for a, z in ((0, SEQ), (SEQ, KEYS0)):
                for part in (0, 1):
                    m = pe.do(lambda e, a=a, z=z, part=part: e.matmul(slot.ap[:, a:z], lhs, k[:, h, part, a:z],
                                                                      start=part == 0, stop=part == 1),
                              slot.free, st["q0"], st["q1"], st[f"k{h}"])
            st.setdefault("scores", []).append(m)
            big, prob, col = neg_max.next(), probs.next(), 2 * j + h
            v = ve.do(lambda e: e.tensor_reduce(big.ap, slot.ap[:, 0:KEYS0], AX_X, ALU.max, negate=True), m, big.free)
            a = ac.do(lambda e: e.activation(prob.ap, slot.ap[:, 0:KEYS0], ACT.Exp, bias=big.ap,
                                             accum_out=u["sums"].ap[:, col:col + 1]), v, prob.free, u["sums"].free)
            big.free, slot.free = [a], [a]
            u.setdefault("exps", []).append(a)
            return prob, a

        def turn_probs(u, h, j, prob, ready):
            for n, (bank, tiles) in enumerate(zip(turned, (range(0, 4), range(4, KT0)))):
                for t in tiles:
                    rows = min(P, KEYS0 - t * P)
                    m = pe.do(lambda e, t=t, rows=rows, c=(t - tiles[0]) * P, bank=bank: e.transpose(
                        bank.ap[0:rows, c:c + P], prob.ap[:, t * P:t * P + rows], self.eye), ready, bank.free)
                out = u["probs"].ap[:, h, tiles[0]:tiles[-1] + 1, j * P:(j + 1) * P]
                src = bank.ap[:, 0:P * len(tiles)].rearrange("p (t n) -> p t n", t=len(tiles))
                if n == 0:
                    s = ac.do(lambda e, out=out, src=src: e.activation(out, src, ACT.Copy), m, u["probs"].free)
                else:
                    s = ve.do(lambda e, out=out, src=src: e.tensor_copy(out, src), m, u["probs"].free)
                bank.free = [s]
                u.setdefault("turned", []).append(s)
            prob.free = [m]

        def weigh(u, tiles):
            st = state[u["group"]]
            for t in tiles:
                rows = min(P, KEYS0 - t * P)
                for h in (0, 1):
                    m = pe.do(lambda e, t=t, rows=rows, h=h: e.matmul(
                        out_bank.ap[64 * h:64 * h + 64, 0:2 * P], st["v"].ap[0:rows, t, 64 * h:64 * h + 64],
                        u["probs"].ap[0:rows, h, t, :], start=t == 0, stop=t == KT0 - 1),
                        u["turned"], st["v_ready"], out_bank.free)
            if tiles[-1] == KT0 - 1:
                u["weighed"] = m
                u["probs"].free = [m]

        def invert(u):
            u["inverse"], u["spread"] = inverse.next(), spread.next()
            r, s = u["inverse"].ap, u["spread"].ap
            v = ve.do(lambda e: e.reciprocal(r, u["sums"].ap), u["exps"], u["inverse"].free)
            u["sums"].free = [v]
            by_head = r.rearrange("p (j h) -> p j h", j=2).unsqueeze(3).to_broadcast([P, 2, 2, D0])
            u["spread_done"] = po.do(lambda e: e.tensor_copy(s, by_head), v, u["spread"].free)
            u["inverse"].free = [u["spread_done"]]

        def scale_out(u):
            (b, p), half = u["group"], u["half"]
            for j in (0, 1):
                m = pe.do(lambda e, j=j: e.transpose(out_bank.ap[:, (2 + j) * P:(3 + j) * P],
                                                     u["spread"].ap[:, j, :, :].rearrange("p h d -> p (h d)"), self.eye),
                          u["spread_done"])
            u["spread"].free = [m]
            out = mixed[:, p, half * 2 * P:(half + 1) * 2 * P]
            a = ac.do(lambda e: e.activation(out, out_bank.ap[:, 2 * P:4 * P], ACT.Copy), m, mixed_free[half])
            s = ve.do(lambda e: e.tensor_tensor(out, out_bank.ap[:, 0:2 * P], out, ALU.mult), a)
            out_bank.free = [s]
            u["mixed"] = s
            if half == 1:
                st = state[u["group"]]
                st["q"].free = st["k"].free = list(st["scores"])
                st["v"].free = [u["weighed"]]

        def project_out(b, t, ready):
            for p in range(PAIRS):
                m = pe.do(lambda e, p=p: e.matmul(side.ap[:, 0:P], mixed[:, p, t * P:(t + 1) * P],
                                                  w["wo"][:, p * P:(p + 1) * P], start=p == 0, stop=p == PAIRS - 1),
                          ready, side.free)
            mixed_free[t // 2] = m
            side.free = [self.add_to_x(b * QT + t, side.ap[:, 0:P], 0, m)]
            if t == QT - 1:
                self.follow(b)

        units = [{"group": g, "half": half} for g in groups for half in (0, 1)]
        subs = [(u, h, j) for u in units for h in (0, 1) for j in (0, 1)]
        self.chores = [self.late_tables]
        for b in range(1, BATCH):
            rows = slice(QT * b, QT * b + QT)
            (once,), steps = self.norm_groups(x[:, rows, :], self.xn[:, rows, :], [self.load_x[b]] * QT, QT)
            (again,), done = self.norm_groups(self.xn[:, rows, :], self.xn[:, rows, :], steps, QT)
            self.chores += [*once, *again, lambda b=b, rows=rows, done=done: latents.extend(self.turn(
                self.xn[:, rows, :], self.xt[:, b * SEQ:(b + 1) * SEQ], done, n=QT, **ln2))]
        parts = [(0, 1), (2, 3), (4,), (5,)]
        waiting, rest = [], None
        for i in range(len(subs) + 15):
            if i < len(subs):
                u, h, j = subs[i]
                if i % 4 == 0:
                    u["sums"], u["probs"] = sums.next(), probs_t.next()
                waiting.append((u, h, j, *scores_of(u, h, j)))
            if rest:
                rest()
                rest = None
            back = (i - 3) // 4 - 1
            if 0 <= back < len(units):
                part = (i - 3) % 4
                if part == 0:
                    invert(units[back])
                weigh(units[back], parts[part])
                if part == 3:
                    scale_out(units[back])
            if i >= 2 and waiting:
                turn_probs(*waiting.pop(0))
            if i >= 4:
                self.chore()
            late = i - 8 * PAIRS - 7
            if late >= 0 and late % (8 * PAIRS) in (0, 2, 4, 6):
                b = late // (8 * PAIRS)
                own = units[2 * PAIRS * b:2 * PAIRS * (b + 1)]
                project_out(b, late % (8 * PAIRS) // 2, [v["mixed"] for v in own])
            if i // 8 + 1 < len(groups) and i % 8 in pieces:
                rest = pieces[i % 8](groups[i // 8 + 1], i // 8 + 1)
        self.banks = Ring([self.psum[:, b * BANK:(b + 1) * BANK] for b in range(8)])
        for bank, last in zip(self.banks.slots, (scores.slots[0],) * 2 + (scores.slots[1],) * 2 + (*turned, out_bank, side)):
            bank.free = last.free

    def one_hot_of_max(self, values, down, n, *ready):
        ve = self.ve
        top, key, hot = self.carve(TILES), self.carve(TILES, n), self.carve(TILES, n)
        best = self.carve(TILES)
        wide = [P, TILES, n]
        places = down.unsqueeze(1).to_broadcast(wide)
        a = ve.do(lambda e: e.tensor_reduce(top, values, AX_X, ALU.max), *ready)
        b = ve.do(lambda e: e.tensor_tensor(hot, values, top.unsqueeze(2).to_broadcast(wide), ALU.is_equal), a)
        c = ve.do(lambda e: e.tensor_tensor(key, hot, places, ALU.mult), b)
        d = ve.do(lambda e: e.tensor_reduce(best, key, AX_X, ALU.max), c)
        f = ve.do(lambda e: e.tensor_tensor(hot, places, best.unsqueeze(2).to_broadcast(wide), ALU.is_equal), d)
        return hot, best, f

    def token_products(self, weights, n, ready, row, *others):
        bank = self.banks.next()
        out = self.carve(TILES, n)
        for t in range(TILES):
            m = self.pe.do(lambda e, t=t: e.matmul(bank.ap[:, t * n:(t + 1) * n], self.xt[:, t * P:(t + 1) * P], weights,
                                                   start=True, stop=True), ready[t], bank.free, *others)
        src = bank.ap[:, 0:TILES * n].rearrange("p (t n) -> p t n", t=TILES)
        if row is None:
            s = self.ve.do(lambda e: e.tensor_copy(out, src), m)
        else:
            s = self.ve.do(lambda e: e.tensor_tensor(out, src, row.unsqueeze(1).to_broadcast([P, TILES, n]), ALU.add), m)
        bank.free = [s]
        return out, s

    def turn_small(self, src, n, ready):
        out, steps = self.carve(TOKENS), []
        for b in range(BATCH):
            bank = self.banks.next()
            for j in range(QT):
                m = self.pe.do(lambda e, t=QT * b + j, j=j, bank=bank: e.transpose(
                    bank.ap[0:n, j * P:(j + 1) * P], src[:, t, :], self.eye), ready, bank.free)
            s = self.evacuate(out[0:n, b * SEQ:(b + 1) * SEQ], bank.ap[0:n, :], m)
            bank.free = [s]
            steps.append(s)
        return out, steps

    def top1_experts(self):
        pe, ve, ac = self.pe, self.ve, self.ac
        self.begin("experts")
        self.load_weights(7, self.before)
        w = self.w[1]
        _, turned = self.stream()
        hidden = Ring([self.carve(FT, SEQ) for _ in range(2)])
        def up(b, x):
            h, steps = hidden.next(), []
            for f in range(FT):
                bank = self.banks.next()
                m = pe.do(lambda e, f=f, bank=bank: e.matmul(
                    bank.ap, w["w1"][:, x * FF + f * P:x * FF + (f + 1) * P], self.xt[:, b * SEQ:(b + 1) * SEQ],
                    start=True, stop=True), turned[QT * b], bank.free, self.w_ready[1])
                col = w["b1"][:, x * FT + f:x * FT + f + 1]
                if f % 4 == 3:
                    s = ve.do(lambda e, f=f, bank=bank, col=col: e.tensor_scalar(h.ap[:, f, :], bank.ap, col, 0.0, ALU.add, ALU.max),
                              m, h.free)
                else:
                    s = ac.do(lambda e, f=f, bank=bank, col=col: e.activation(h.ap[:, f, :], bank.ap, ACT.Relu, bias=col), m, h.free)
                bank.free = [s]
                steps.append(s)
            self.xt_free[b] = m
            return b, x, h, steps

        waiting = [up(0, 0), up(0, 1)]
        self.do_chores()
        logits, s = self.token_products(w["gate"], EXPERTS, turned, self.row["L0_ffn_gate_b"], self.w_ready[1], self.rows_ready)
        s = ve.do(lambda e: e.tensor_tensor(logits, logits, self.row["L0_ffn_expert_bias"].unsqueeze(1)
                                            .to_broadcast([P, TILES, EXPERTS]), ALU.add), s)
        hot, _, s_hot = self.one_hot_of_max(logits, self.c["down8"], EXPERTS, s)
        hot_t, hot_t_ready = self.turn_small(hot, EXPERTS, s_hot)
        weight = self.carve(TILES, EXPERTS)
        s_weight = ve.do(lambda e: e.tensor_scalar(weight, hot, self.gates[:, 4:5], None, ALU.mult), s_hot)

        for b in range(BATCH):
            bank = self.banks.next()
            for j in range(QT):
                t = QT * b + j
                m = pe.do(lambda e, t=t, j=j, bank=bank: e.matmul(
                    bank.ap[:, j * P:(j + 1) * P], hot_t[0:EXPERTS, t * P:(t + 1) * P], self.small[:, 0:P],
                    start=True, stop=True), hot_t_ready[b], bank.free, self.rows_ready)
            bank.free = [self.add_to_x(QT * b + j, bank.ap[:, j * P:(j + 1) * P], 4, m) for j in range(QT)]

        def down(b, x, h, steps):
            bank = self.banks.next()
            for j in range(QT):
                for f in range(FT):
                    m = pe.do(lambda e, j=j, f=f: e.matmul(
                        bank.ap[:, j * P:(j + 1) * P], h.ap[:, f, j * P:(j + 1) * P],
                        w["w2"][:, (x * FT + f) * P:(x * FT + f + 1) * P], start=f == 0, stop=f == FT - 1), steps, bank.free)
            h.free = [m]
            bank.free = []
            for j in range(QT):
                t = QT * b + j
                self.x_last[t] = ve.do(lambda e, t=t, j=j: e.scalar_tensor_tensor(
                    self.x[:, t, :], bank.ap[:, j * P:(j + 1) * P], weight[:, t, x:x + 1], self.x[:, t, :],
                    ALU.mult, ALU.add), m, s_weight, self.x_last[t])
                bank.free.append(self.x_last[t])
            if x == EXPERTS - 1:
                self.follow(b)

        for b in range(BATCH):
            for x in range(EXPERTS):
                if (b, x) > (0, 1):
                    waiting.append(up(b, x))
                if (b, x) >= (0, 1):
                    down(*waiting.pop(0))
                self.chore()
        down(*waiting.pop(0))

    def one_head(self):
        pe, ve, ac = self.pe, self.ve, self.ac
        self.begin("onehead")
        self.load_weights(5, self.before)
        self.load_weights(6, self.before)
        w = self.w[2]
        _, turned = self.stream()
        k_t, k_ready = self.project_context(w["wk"], w["bk"], self.w_ready[2])
        q_t, q_ready = self.project(w["wq"], w["bq"], self.xt, turned)
        self.xt_free = [q_ready[QT * b] for b in range(BATCH)]
        v, v_ready = self.carve(2 * BATCH, P), []
        for b in range(BATCH):
            bank = self.banks.next()
            for n, rows in ((0, P), (1, CTX_REST)):
                m = pe.do(lambda e, b=b, n=n, rows=rows, bank=bank: e.matmul(
                    bank.ap[0:rows, n * P:(n + 1) * P], self.context[:, b, n * P:n * P + rows], w["wv"],
                    start=True, stop=True), bank.free, self.context_ready)
            s = [ve.do(lambda e, b=b, n=n, rows=rows, bank=bank: e.tensor_copy(
                v[0:rows, 2 * b + n, :], bank.ap[0:rows, n * P:(n + 1) * P]), m) for n, rows in ((0, P), (1, CTX_REST))]
            bank.free = s
            v_ready.append(s)
        probs = Ring([self.carve(QT, CTX) for _ in range(2)])
        probs_t = Ring([self.carve(2, SEQ) for _ in range(2)])
        small = [(self.carve(QT), self.carve(QT), self.carve(QT)) for _ in range(BATCH)]

        def scores_of(b):
            neg, total, inv = small[b]
            prob, exps = probs.next(), []
            for g, tiles in enumerate(((0, 1), (2, 3))):
                bank = self.banks.next()
                for n, t in enumerate(tiles):
                    m = pe.do(lambda e, n=n, t=t, bank=bank: e.matmul(
                        bank.ap[:, n * CTX:(n + 1) * CTX], q_t[:, (QT * b + t) * P:(QT * b + t + 1) * P],
                        k_t[:, b * CTX:(b + 1) * CTX], start=True, stop=True), q_ready[QT * b + t], k_ready, bank.free)
                src = bank.ap[:, 0:2 * CTX].rearrange("p (t k) -> p t k", t=2)
                s = ve.do(lambda e, g=g, src=src: e.tensor_reduce(neg[:, 2 * g:2 * g + 2], src, AX_X, ALU.max, negate=True), m)
                bank.free = []
                for n, t in enumerate(tiles):
                    a = ac.do(lambda e, n=n, t=t, src=src: e.activation(prob.ap[:, t, :], src[:, n, :], ACT.Exp, bias=neg[:, t:t + 1],
                                                                        accum_out=total[:, t:t + 1]), s, prob.free)
                    bank.free.append(a)
                exps += bank.free
            r = ve.do(lambda e: e.reciprocal(inv, total), exps)
            return b, prob, exps, inv, r

        def weigh(b, prob, exps, inv, r):
            pt, steps = probs_t.next(), []
            for n, rows in ((0, P), (1, CTX_REST)):
                bank = self.banks.next()
                for t in range(QT):
                    m = pe.do(lambda e, n=n, t=t, rows=rows, bank=bank: e.transpose(
                        bank.ap[0:rows, t * P:(t + 1) * P], prob.ap[:, t, n * P:n * P + rows], self.eye), exps, bank.free)
                s = self.evacuate(pt.ap[0:rows, n, :], bank.ap[0:rows, :], m, pt.free)
                bank.free = [s]
                steps.append(s)
            prob.free = [m]
            bank = self.banks.next()
            for t in range(QT):
                for n, rows in ((0, P), (1, CTX_REST)):
                    m = pe.do(lambda e, n=n, t=t, rows=rows: e.matmul(
                        bank.ap[:, t * P:(t + 1) * P], pt.ap[0:rows, n, t * P:(t + 1) * P], v[0:rows, 2 * b + n, :],
                        start=n == 0, stop=n == 1), steps, v_ready[b], bank.free)
            pt.free = [m]
            bank.free = [self.add_to_x(QT * b + t, bank.ap[:, t * P:(t + 1) * P], 1, [m, r], row=self.row["L1_xattn_bv"],
                                       factor=inv[:, t:t + 1]) for t in range(QT)]
            self.follow(b)

        waiting = None
        for b in range(BATCH):
            now = scores_of(b)
            self.do_chores()
            if waiting:
                weigh(*waiting)
            waiting = now
        weigh(*waiting)

    def project(self, weights, bias, src, ready, *others, scale=None, out=None):
        out = self.carve(TOKENS) if out is None else out
        steps = []
        for b in range(BATCH):
            if b == BATCH - 1:
                self.do_chores()
            bank = self.banks.next()
            m = self.pe.do(lambda e, b=b, bank=bank: e.matmul(bank.ap, weights, src[:, b * SEQ:(b + 1) * SEQ], start=True, stop=True),
                           ready[QT * b:QT * b + QT], bank.free, *others)
            o = out[:, b * SEQ:(b + 1) * SEQ]
            if scale is None and b % 2:
                s = self.ac.do(lambda e, o=o, bank=bank: e.activation(o, bank.ap, ACT.Identity, bias=bias), m)
            else:
                s = self.ve.do(lambda e, o=o, bank=bank: e.tensor_scalar(o, bank.ap, bias, 1.0 if scale is None else scale,
                                                                         ALU.add, ALU.mult), m)
            bank.free = [s]
            steps += [s] * QT
        return out, steps

    def project_context(self, weights, bias, *others):
        out, steps = self.carve(CTX_ROWS), []
        for b in range(0, BATCH, 2):
            bank = self.banks.next()
            for n in (0, 1):
                m = self.pe.do(lambda e, b=b, n=n, bank=bank: e.matmul(
                    bank.ap[:, n * CTX:(n + 1) * CTX], weights, self.context[:, b + n, 0:CTX], start=True, stop=True),
                    self.context_ready, bank.free, *others)
            s = self.ac.do(lambda e, b=b, bank=bank: e.activation(out[:, b * CTX:(b + 2) * CTX], bank.ap[:, 0:2 * CTX],
                                                                  ACT.Identity, bias=bias), m)
            bank.free = [s]
            steps.append(s)
        return out, steps

    def batch_attention(self):
        pe, ve, ac, po = self.pe, self.ve, self.ac, self.po
        self.begin("batch")
        w, y = self.w[3], self.xn
        heads, d = 16, 8
        _, turned = self.stream()
        qkv, qkv_ready = self.carve(TILES, 3 * P), []
        for t in range(TILES):
            if t == TILES - QT:
                self.do_chores()
            bank = self.banks.next()
            m = pe.do(lambda e, t=t, bank=bank: e.matmul(bank.ap[:, 0:3 * P], self.xt[:, t * P:(t + 1) * P], w["in"],
                                                         start=True, stop=True), turned[t], bank.free, self.w_ready[3])
            s = ve.do(lambda e, t=t, bank=bank: e.tensor_tensor(qkv[:, t, :], bank.ap[:, 0:3 * P],
                                                                self.row["L1_ffn_in_proj_b"], ALU.add), m, self.rows_ready)
            bank.free = [s]
            qkv_ready.append(s)
        part = lambda n: qkv[:, :, n * P:(n + 1) * P]
        pairs = [P, BATCH, QT, P]
        places = QT * heads
        product = [self.carve(BATCH * QT, P) for _ in range(2)]
        product_free = [None, None]
        score = self.carve(BATCH, BATCH, places)
        done = []
        for t in range(BATCH):
            o, slot = product[t % 2], t % 2
            a = ve.do(lambda e, t=t, o=o: e.tensor_tensor(
                o.rearrange("p (s j) c -> p s j c", s=BATCH), part(0)[:, QT * t:QT * t + QT, :].unsqueeze(1).to_broadcast(pairs),
                part(1).rearrange("p (s j) c -> p s j c", s=BATCH), ALU.mult), qkv_ready, product_free[slot])
            b = ve.do(lambda e, t=t, o=o: e.tensor_reduce(
                score[:, t, :, :].rearrange("p s c -> p (s c)"), o.rearrange("p s (h d) -> p (s h) d", d=d), AX_X, ALU.add), a)
            product_free[slot] = b
            done.append(b)
        by_key = score.rearrange("p t s c -> p t c s")
        most, total = self.carve(BATCH, places), self.carve(BATCH, places)
        over = lambda v: v.unsqueeze(2).to_broadcast([P, BATCH, BATCH, places])
        s = ve.do(lambda e: e.tensor_reduce(most, by_key, AX_X, ALU.max), done)
        s = ve.do(lambda e: e.tensor_tensor(score, score, over(most), ALU.subtract), s)
        s = ac.do(lambda e: e.activation(score, score, ACT.Exp, scale=d ** -0.5), s)
        s = ve.do(lambda e: e.tensor_reduce(total, by_key, AX_X, ALU.add), s)
        s = ve.do(lambda e: e.reciprocal(total, total), s)
        s = ve.do(lambda e: e.tensor_tensor(score, score, over(total), ALU.mult), s)
        mixed = self.carve(TILES, P)
        mixed_ready = []
        for t in range(BATCH):
            o, slot = product[t % 2], t % 2
            a = ve.do(lambda e, t=t, o=o: e.tensor_tensor(
                o.rearrange("p s (h d) -> p s h d", d=d),
                score[:, t, :, :].rearrange("p s (j h) -> p (s j) h", j=QT).unsqueeze(3).to_broadcast([P, TILES, heads, d]),
                part(2).rearrange("p s (h d) -> p s h d", d=d), ALU.mult), s, product_free[slot])
            b = ve.do(lambda e, t=t, o=o: e.tensor_reduce(
                mixed[:, QT * t:QT * t + QT, :].rearrange("p j c -> p (j c)"),
                o.rearrange("p (s j) c -> p (j c) s", s=BATCH), AX_X, ALU.add), a)
            product_free[slot] = b
            mixed_ready += [b] * QT
        turned = self.turn(mixed, self.xt, mixed_ready, after=(qkv_ready,))
        h = self.token_layer([(self.xt, w["out"])], turned, self.row["L1_ffn_out_b"], y)
        ready = self.normalize(y, y, h, gain=self.row["L1_ffn_ln1_g"], bias=self.row["L1_ffn_ln1_b"])
        turned = self.turn(y, self.xt, ready)

        probs, s = self.token_products(w["router"], EXPERTS, turned, self.row["L1_ffn_router_b"])
        wide = [P, TILES, EXPERTS]
        top, mass = self.carve(TILES), self.carve(TILES)
        s = ve.do(lambda e: e.tensor_reduce(top, probs, AX_X, ALU.max), s)
        s = ve.do(lambda e: e.tensor_tensor(probs, probs, top.unsqueeze(2).to_broadcast(wide), ALU.subtract), s)
        s = ac.do(lambda e: e.activation(probs, probs, ACT.Exp), s)
        s = ve.do(lambda e: e.tensor_reduce(mass, probs, AX_X, ALU.add), s)
        s = ve.do(lambda e: e.reciprocal(mass, mass), s)
        s = ve.do(lambda e: e.tensor_tensor(probs, probs, mass.unsqueeze(2).to_broadcast(wide), ALU.mult), s)
        hot1, key1, s = self.one_hot_of_max(probs, self.c["down8"], EXPERTS, s)
        s = ve.do(lambda e: e.scalar_tensor_tensor(probs, hot1, -4.0, probs, ALU.mult, ALU.add), s)
        hot2, key2, s = self.one_hot_of_max(probs, self.c["down8"], EXPERTS, s)
        s = ve.do(lambda e: e.tensor_tensor(key1, key1, key2, ALU.min), s)
        hot = hot1
        s_hot = ve.do(lambda e: e.tensor_tensor(hot, self.c["down8"].unsqueeze(1).to_broadcast(wide),
                                                key1.unsqueeze(2).to_broadcast(wide), ALU.is_equal), s)
        hot_t, hot_t_ready = self.turn_small(hot, EXPERTS, s_hot)
        last = list(ready)
        for b in range(BATCH):
            bank = self.banks.next()
            for j in range(QT):
                t = QT * b + j
                m = pe.do(lambda e, t=t, j=j, bank=bank: e.matmul(
                    bank.ap[:, j * P:(j + 1) * P], hot_t[0:EXPERTS, t * P:(t + 1) * P], self.small[:, P:2 * P],
                    start=True, stop=True), hot_t_ready[b], bank.free)
            o = y[:, QT * b:QT * b + QT, :]
            s = ve.do(lambda e, o=o, bank=bank: e.tensor_tensor(o, o, bank.ap.rearrange("p (t n) -> p t n", t=QT), ALU.add),
                      m, turned)
            bank.free = [s]
            for j in range(QT):
                last[QT * b + j] = s

        hidden = Ring([self.carve(SEQ) for _ in range(3)])

        def up(b, x):
            bank, g = self.banks.next(), hidden.next()
            m = pe.do(lambda e: e.matmul(bank.ap, w["w1"][:, x * P:(x + 1) * P], self.xt[:, b * SEQ:(b + 1) * SEQ],
                                         start=True, stop=True), bank.free)
            s = ac.do(lambda e: e.activation(g.ap, bank.ap, ACT.Gelu, bias=w["b1"][:, x:x + 1]), m, g.free)
            bank.free = [s]
            return b, x, g, s

        def down(b, x, g, ready):
            bank = self.banks.next()
            for j in range(QT):
                m = pe.do(lambda e, j=j: e.matmul(bank.ap[:, j * P:(j + 1) * P], g.ap[:, j * P:(j + 1) * P],
                                                  w["w2"][:, x * P:(x + 1) * P], start=True, stop=True), ready, bank.free)
            g.free, bank.free = [m], []
            for j in range(QT):
                t = QT * b + j
                last[t] = ve.do(lambda e, t=t, j=j: e.scalar_tensor_tensor(
                    y[:, t, :], bank.ap[:, j * P:(j + 1) * P], hot[:, t, x:x + 1], y[:, t, :], ALU.mult, ALU.add), m, last[t])
                bank.free.append(last[t])

        def close(b):
            rows = slice(QT * b, QT * b + QT)
            ((measure, scale),), done = self.norm_groups(y[:, rows, :], y[:, rows, :], last[rows], QT,
                                                         gain=self.row["L1_ffn_ln2_g"], bias=self.row["L1_ffn_ln2_b"])

            def update():
                self.xn_free[b] = self.add_batch_to_x(b, y, 5, done)
                self.follow(b)

            self.chores += [measure, scale, update]

        waiting = []
        for b in range(BATCH):
            for x in range(EXPERTS):
                waiting.append(up(b, x))
                if x == EXPERTS - 1:
                    self.xt_free[b] = waiting[-1][-1]
                if len(waiting) > 2:
                    old = waiting.pop(0)
                    down(*old)
                    if old[1] == EXPERTS - 1:
                        close(old[0])
                self.chore()
        for rest in waiting:
            down(*rest)
        close(BATCH - 1)

    def token_layer(self, parts, ready, row, into):
        out = []
        for b in range(BATCH):
            bank = self.banks.next()
            for j in range(QT):
                t = QT * b + j
                for n, (src, weights) in enumerate(parts):
                    m = self.pe.do(lambda e, t=t, j=j, n=n, src=src, weights=weights, bank=bank: e.matmul(
                        bank.ap[:, j * P:(j + 1) * P], src[:, t * P:(t + 1) * P], weights,
                        start=n == 0, stop=n == len(parts) - 1), ready[t], bank.free)
            o = into[:, QT * b:QT * b + QT, :]
            src = bank.ap.rearrange("p (t n) -> p t n", t=QT)
            s1 = self.ve.do(lambda e, o=o, src=src: e.tensor_tensor(o, src, o, ALU.add), m)
            bank.free = [s1]
            s2 = self.ve.do(lambda e, o=o: e.tensor_tensor(o, o, row.unsqueeze(1).to_broadcast([P, QT, P]), ALU.add), s1)
            out += [s2] * QT
        return out

    def context_attention(self, heads, q_t, q_ready, k_t, k_ready, wv, bv, masked=None, finish=None):
        pe, ve, ac, po = self.pe, self.ve, self.ac, self.po
        d = P // heads
        chunks = flat_chunks(heads)
        of_group = heads // GROUPS
        head_of = self.c[f"head{heads}"]
        block = self.c[f"block{heads}"].rearrange("p (c h) -> p c h", h=of_group)
        keys = Ring([self.carve(heads, CTX)])
        values = Ring([self.carve(GROUPS * len(chunks), WIDE) for _ in range(2)])
        probs = Ring([self.carve(heads * CTX) for _ in range(2)])
        probs_t = Ring([self.carve(GROUPS * len(chunks), 2 * P)])
        small = Ring([self.carve(heads) for _ in range(6)])
        spread = Ring([self.carve(heads, d) for _ in range(2)])
        factor = Ring([self.carve(2 * P) for _ in range(2)])
        mixed = Ring([self.carve(2 * P) for _ in range(2)])
        groups = [(h, min(3, heads - h)) for h in range(0, heads, 3)]
        operands = {}

        def prepare(b):
            k = keys.next()
            ks = po.do(lambda e: e.tensor_tensor(
                k.ap, k_t[:, b * CTX:(b + 1) * CTX].unsqueeze(1).to_broadcast([P, heads, CTX]),
                head_of.unsqueeze(2).to_broadcast([P, heads, CTX]), ALU.mult), k_ready, k.free)
            v, steps = values.next(), []
            full = GROUPS * sum(rows == P for _, rows in chunks)
            last = chunks[-1][1]
            for c0, c1, rows in ((0, full, P), (full, full + GROUPS, last)):
                bank = self.banks.next()
                for c in range(c0, c1):
                    f0, g = chunks[c // GROUPS][0] % CTX, c % GROUPS
                    m = pe.do(lambda e, c=c - c0, f0=f0, g=g, rows=rows, bank=bank: e.matmul(
                        bank.ap[0:rows, c * WIDE:(c + 1) * WIDE], self.context[:, b, f0:f0 + rows],
                        wv[:, g * WIDE:(g + 1) * WIDE], start=True, stop=True), bank.free, self.context_ready)
                step = ve.do(lambda e, c0=c0, c1=c1, rows=rows, bank=bank: e.tensor_tensor(
                    v.ap[0:rows, c0:c1, :].rearrange("p c (h d) -> p c h d", h=of_group),
                    bank.ap[0:rows, 0:(c1 - c0) * WIDE].rearrange("p (c h d) -> p c h d", c=c1 - c0, h=of_group),
                    block[0:rows, c0:c1, :].unsqueeze(3).to_broadcast([rows, c1 - c0, of_group, d]), ALU.mult), m, v.free)
                bank.free = [step]
                steps.append(step)
            operands[b] = (k, ks, v, steps)

        def scores_of(b, t):
            k, ks, _, _ = operands[b]
            tile, prob = QT * b + t, probs.next()
            neg, total, exps = small.next(), small.next(), []
            for h0, n in groups:
                bank = self.banks.next()
                src = bank.ap[:, 0:n * CTX]
                m = pe.do(lambda e, h0=h0, n=n, src=src: e.matmul(
                    src, q_t[:, tile * P:(tile + 1) * P], k.ap[:, h0:h0 + n, :].rearrange("p h k -> p (h k)"),
                    start=True, stop=masked is None), q_ready[tile], ks, bank.free)
                if masked is not None:
                    m = pe.do(lambda e, n=n, src=src: e.matmul(
                        src.rearrange("p (h k) -> p h k", h=n), self.cb["eye_b"], masked[0][:, tile, :].unsqueeze(1).to_broadcast([P, n, CTX]),
                        start=False, stop=True), masked[1])
                s = ve.do(lambda e, h0=h0, n=n, src=src: e.tensor_reduce(
                    neg.ap[:, h0:h0 + n], src.rearrange("p (h k) -> p h k", h=n), AX_X, ALU.max, negate=True), m, neg.free)
                bank.free = []
                for h in range(h0, h0 + n):
                    a = ac.do(lambda e, h=h, h0=h0, src=src: e.activation(
                        prob.ap[:, h * CTX:(h + 1) * CTX], src[:, (h - h0) * CTX:(h - h0 + 1) * CTX], ACT.Exp,
                        bias=neg.ap[:, h:h + 1], accum_out=total.ap[:, h:h + 1]), s, prob.free, total.free)
                exps.append(a)
                bank.free = [a]
            k.free = [m]
            if t == QT - 1:
                self.xn_free[b] = m
            neg.free = [a]
            r = ve.do(lambda e: e.reciprocal(total.ap, total.ap), exps)
            sp = spread.next()
            wide = po.do(lambda e: e.tensor_copy(sp.ap, total.ap.unsqueeze(2).to_broadcast([P, heads, d])), r, sp.free)
            total.free = [wide]
            return b, t, prob, exps, sp, wide

        unit = {}

        def turn_probs(b, t, prob, exps, sp, wide):
            j = t % 2
            if j == 0:
                unit["pt"], unit["steps"], unit["factor"] = probs_t.next(), [], factor.next()
                unit["side"] = None
            pt = unit["pt"]
            for c, (f0, rows) in enumerate(chunks):
                bank = self.banks.next()
                for g in range(GROUPS):
                    at = g * of_group * CTX + f0
                    m = pe.do(lambda e, g=g, at=at, rows=rows, bank=bank: e.transpose(
                        bank.ap[0:rows, g * P:(g + 1) * P], prob.ap[:, at:at + rows], self.eye), exps, bank.free)
                o = pt.ap[0:rows, GROUPS * c:GROUPS * (c + 1), j * P:(j + 1) * P]
                i = bank.ap[0:rows, :].rearrange("p (g q) -> p g q", g=GROUPS)
                s = self.evacuate(o, i, m, pt.free)
                bank.free = [s]
                unit["steps"].append(s)
            prob.free = [m]
            bank = self.banks.next()
            m = pe.do(lambda e, bank=bank: e.transpose(bank.ap[:, 0:P], sp.ap.rearrange("p h d -> p (h d)"), self.eye), wide, bank.free)
            sp.free = [m]
            f = unit["factor"]
            s = ac.do(lambda e, bank=bank, f=f: e.activation(f.ap[:, j * P:(j + 1) * P], bank.ap[:, 0:P], ACT.Copy), m, f.free)
            bank.free = [s]
            unit["steps"].append(s)
            if j == 1:
                weigh(b, t // 2)

        def weigh(b, half):
            _, _, v, v_ready = operands[b]
            bank, pt, f, steps = self.banks.next(), unit["pt"], unit["factor"], unit["steps"]
            for c, (_, rows) in enumerate(chunks):
                for g in range(GROUPS):
                    m = pe.do(lambda e, c=GROUPS * c + g, g=g, rows=rows, first=c == 0, last=c == len(chunks) - 1: e.matmul(
                        bank.ap[WIDE * g:WIDE * (g + 1), 0:2 * P], v.ap[0:rows, c, :], pt.ap[0:rows, c, :],
                        start=first, stop=last), steps, v_ready, bank.free)
            pt.free, v.free = [m], [m]
            o = mixed.next()
            s = ve.do(lambda e: e.tensor_tensor(o.ap, bank.ap[:, 0:2 * P], f.ap, ALU.mult), m, o.free)
            bank.free, f.free = [s], [s]
            s = ve.do(lambda e: e.tensor_scalar(o.ap, o.ap, bv, None, ALU.add), s)
            finish(b, half, o, s)

        waiting = None
        for b in range(BATCH):
            prepare(b)
            for t in range(QT):
                now = scores_of(b, t)
                if waiting:
                    turn_probs(*waiting)
                waiting = now
                self.chore()
        turn_probs(*waiting)

    def masked_attention(self):
        pe, ve = self.pe, self.ve
        self.begin("masked")
        w, heads = self.w[4], 16
        mask = self.carve(TILES, CTX, dt=BF16)
        raw = self.carve(TILES * CTX // 4).bitcast(U8).rearrange("p (t k) -> p t k", t=TILES)
        load = self.dma("mask", raw, self.dram["mask"].rearrange("(t p) k -> p t k", p=P), self.before)
        mask_ready = self.po.do(lambda e: e.tensor_scalar(mask, raw, MASKED, None, ALU.mult), load)
        _, turned = self.stream()
        k_t, k_ready = self.project_context(w["wk"], w["bk"], self.w_ready[4])
        q_t, q_ready = self.project(w["wq"], w["bq"], self.xt, turned, scale=(P // heads) ** -0.5,
                                    out=self.xn[:, :, :].rearrange("p t d -> p (t d)"))
        self.xt_free = [q_ready[QT * b] for b in range(BATCH)]

        def finish(b, half, o, ready):
            bank = self.banks.next()
            for j in (0, 1):
                m = pe.do(lambda e, j=j: e.matmul(bank.ap[:, j * P:(j + 1) * P], o.ap[:, j * P:(j + 1) * P], w["wo"],
                                                  start=True, stop=True), ready, bank.free)
            o.free = [m]
            bank.free = [self.add_to_x(QT * b + 2 * half + j, bank.ap[:, j * P:(j + 1) * P], 2, m, row=self.row["L2_xattn_bo"])
                         for j in (0, 1)]
            if half == 1:
                self.follow(b)

        self.context_attention(heads, q_t, q_ready, k_t, k_ready, w["wv"], w["bv"], (mask, mask_ready), finish)

    def scaled_feed_forward(self):
        pe, ve, ac = self.pe, self.ve, self.ac
        self.begin("scaled")
        w = self.w[5]
        _, turned = self.stream()
        self.xn_free = [None] * BATCH
        gated = self.carve(BATCH, FT, SEQ)
        silu = Ring([self.carve(SEQ) for _ in range(3)])
        hidden = [Ring([self.carve(FT, SEQ) for _ in range(2)]) for _ in range(2)]
        gated_ready = []
        for b in range(BATCH):
            if b == BATCH - 1:
                self.do_chores()
            steps = []
            for f in range(FT):
                bank_a, bank_g, s = self.banks.next(), self.banks.next(), silu.next()
                for bank, name in ((bank_a, "w1"), (bank_g, "w2")):
                    m = pe.do(lambda e, b=b, f=f, bank=bank, name=name: e.matmul(
                        bank.ap, w[name][:, f * P:(f + 1) * P], self.xt[:, b * SEQ:(b + 1) * SEQ], start=True, stop=True),
                        turned[QT * b + QT - 1], bank.free, self.w_ready[5])
                a = ac.do(lambda e, f=f, bank=bank_a, s=s: e.activation(s.ap, bank.ap, ACT.Silu, scale=w["s1"][:, f:f + 1]), m, s.free)
                v = ve.do(lambda e, b=b, f=f, bank=bank_g, s=s: e.scalar_tensor_tensor(
                    gated[:, b, f, :], bank.ap, w["s2"][:, f:f + 1], s.ap, ALU.mult, ALU.mult), a)
                bank_a.free, bank_g.free, s.free = [a], [v], [v]
                steps.append(v)
            gated_ready.append(steps)
            self.xt_free[b] = m

        def layer(src, ready, weights, scales, ring):
            out, steps = ring.next(), []
            for o in range(FT):
                bank = self.banks.next()
                for i in range(FT):
                    m = pe.do(lambda e, o=o, i=i, bank=bank: e.matmul(
                        bank.ap, weights[:, i * FF + o * P:i * FF + (o + 1) * P], src[:, i, :], start=i == 0, stop=i == FT - 1),
                        ready, bank.free)
                s = ac.do(lambda e, o=o, bank=bank: e.activation(out.ap[:, o, :], bank.ap, ACT.Gelu, scale=scales[:, o:o + 1]),
                          m, out.free)
                bank.free = [s]
                steps.append(s)
            return out, steps, m

        def last(b, h, ready):
            bank = self.banks.next()
            for j in range(QT):
                for i in range(FT):
                    m = pe.do(lambda e, i=i, j=j: e.matmul(bank.ap[:, j * P:(j + 1) * P], h.ap[:, i, j * P:(j + 1) * P],
                                                           w["w3"][:, i * P:(i + 1) * P], start=i == 0, stop=i == FT - 1),
                              ready, bank.free)
            h.free = [m]
            bank.free = [self.add_to_x(QT * b + j, bank.ap[:, j * P:(j + 1) * P], 6, m, row=self.row["L2_ffn_w3_s"], op=ALU.mult)
                         for j in range(QT)]
            self.follow(b)

        self.prepare_router()

        first, second = {}, {}
        for b in range(BATCH + 2):
            if b < BATCH:
                first[b] = layer(gated[:, b, :, :], gated_ready[b], w["h1"], w["sh1"], hidden[0])
            if 0 <= b - 1 < BATCH:
                h, ready, _ = first[b - 1]
                second[b - 1] = layer(h.ap, ready, w["h2"], w["sh2"], hidden[1])
                h.free = [second[b - 1][2]]
            if 0 <= b - 2 < BATCH:
                self.do_chores()
                last(b - 2, second[b - 2][0], second[b - 2][1])

    def decoder_block(self):
        pe, ve, ac = self.pe, self.ve, self.ac
        self.begin("decoder")
        w, y, heads = self.w[6], self.xn, 8
        d = P // heads
        _, turned = self.stream()
        values = self.carve(TILES, P)
        qkv = Ring([self.carve(3 * P) for _ in range(3)])
        junk = Ring([self.carve(P) for _ in range(2)])
        score, delta = self.carve(TILES), self.carve(TILES)
        steps, kept = [], []
        for t in range(TILES):
            if t == TILES - QT:
                self.do_chores()
            bank, q = self.banks.next(), qkv.next()
            m = pe.do(lambda e, t=t, bank=bank: e.matmul(bank.ap[:, 0:3 * P], self.xt[:, t * P:(t + 1) * P], w["qkv"],
                                                         start=True, stop=True), turned[t], bank.free, self.w_ready[6])
            s1 = ve.do(lambda e, q=q, bank=bank: e.tensor_tensor(q.ap[:, 0:2 * P], bank.ap[:, 0:2 * P],
                                                                 self.row["L3_xattn_qkv_b"][:, 0:2 * P], ALU.add), m, q.free)
            s2 = ve.do(lambda e, t=t, bank=bank: e.tensor_tensor(values[:, t, :], bank.ap[:, 2 * P:3 * P],
                                                                 self.row["L3_xattn_qkv_b"][:, 2 * P:3 * P], ALU.add), m)
            bank.free = [s1, s2]
            kept.append(s2)
            z = junk.next()
            s3 = ve.do(lambda e, t=t, q=q, z=z: e.tensor_tensor_reduce(
                z.ap, q.ap[:, 0:P], q.ap[:, P:2 * P], float(P) ** 0.5, 0.0, ALU.mult, ALU.add, score[:, t:t + 1]), s1, z.free)
            q.free, z.free = [s3], [s3]
            steps.append(s3)
        s = ve.do(lambda e: e.tensor_tensor(delta, score, score, ALU.subtract), steps)
        s = ac.do(lambda e: e.activation(delta, delta, ACT.Exp), s)
        s = ve.do(lambda e: e.reciprocal(score, delta), s)
        s = ve.do(lambda e: e.tensor_tensor(delta, delta, score, ALU.mult), s)
        s = ve.do(lambda e: e.tensor_tensor(values, values, delta.unsqueeze(2).to_broadcast([P, TILES, P]), ALU.mult), s, kept)
        turned = self.turn(values, self.xt, [s] * TILES)
        ready = self.token_layer([(self.xt, w["sa_out"])], turned, self.row["L3_xattn_sa_out_b"], y)
        ready = self.normalize(y, y, ready, gain=self.row["L3_xattn_ln1_g"], bias=self.row["L3_xattn_ln1_b"])
        turned = self.turn(y, self.xt, ready)
        q_t, q_ready = self.project(w["in"][:, 0:P], w["in_b"][:, 0:1], self.xt, turned, scale=d ** -0.5,
                                    out=values.rearrange("p t d -> p (t d)"))
        k_t, k_ready = self.project_context(w["in"][:, P:2 * P], w["in_b"][:, 1:2])
        after_mix = []

        def finish(b, half, o, ready):
            bank = self.banks.next()
            for j in (0, 1):
                m = pe.do(lambda e, j=j: e.matmul(bank.ap[:, j * P:(j + 1) * P], o.ap[:, j * P:(j + 1) * P], w["mha_out"],
                                                  start=True, stop=True), ready, bank.free)
            o.free = [m]
            t0 = QT * b + 2 * half
            rows = y[:, t0:t0 + 2, :]
            s1 = ve.do(lambda e: e.tensor_tensor(rows, bank.ap[:, 0:2 * P].rearrange("p (t n) -> p t n", t=2), rows, ALU.add), m)
            bank.free = [s1]
            s2 = ve.do(lambda e: e.tensor_tensor(rows, rows, self.row["L3_xattn_mha_out_b"].unsqueeze(1).to_broadcast([P, 2, P]),
                                                 ALU.add), s1)
            after_mix.extend([s2, s2])

        self.context_attention(heads, q_t, q_ready, k_t, k_ready, w["in"][:, 2 * P:3 * P], w["in_b"][:, 2:3], None, finish)
        ready = self.normalize(y, y, after_mix, gain=self.row["L3_xattn_ln2_g"], bias=self.row["L3_xattn_ln2_b"])
        turned = self.turn(y, self.xt, ready)
        hidden = self.carve(FT, SEQ)
        free = None

        def close(b, ready):
            rows = slice(QT * b, QT * b + QT)
            ((measure, scale),), done = self.norm_groups(y[:, rows, :], y[:, rows, :], [ready] * QT, QT,
                                                         gain=self.row["L3_xattn_ln3_g"], bias=self.row["L3_xattn_ln3_b"])

            def update():
                self.xn_free[b] = self.add_batch_to_x(b, y, 3, done)
                self.follow(b)
                self.chore()

            self.chores += [measure, scale, update]

        for b in range(BATCH):
            steps = []
            for f in range(FT):
                bank = self.banks.next()
                m = pe.do(lambda e, b=b, f=f, bank=bank: e.matmul(bank.ap, w["lin1"][:, f * P:(f + 1) * P],
                                                                  self.xt[:, b * SEQ:(b + 1) * SEQ], start=True, stop=True),
                          turned[QT * b + QT - 1], bank.free)
                s = ac.do(lambda e, f=f, bank=bank: e.activation(hidden[:, f, :], bank.ap, ACT.Relu, bias=w["lin1_b"][:, f:f + 1]),
                          m, free)
                bank.free = [s]
                steps.append(s)
                self.chore()
            self.xt_free[b] = m
            bank = self.banks.next()
            for j in range(QT):
                for f in range(FT):
                    m = pe.do(lambda e, f=f, j=j, bank=bank: e.matmul(
                        bank.ap[:, j * P:(j + 1) * P], hidden[:, f, j * P:(j + 1) * P], w["lin2"][:, f * P:(f + 1) * P],
                        start=f == 0, stop=f == FT - 1), steps, bank.free)
            free = m
            self.chore()
            o = y[:, QT * b:QT * b + QT, :]
            s1 = ve.do(lambda e, o=o, bank=bank: e.tensor_tensor(o, bank.ap.rearrange("p (t n) -> p t n", t=QT), o, ALU.add), m)
            bank.free = [s1]
            s2 = ve.do(lambda e, o=o: e.tensor_tensor(o, o, self.row["L3_xattn_lin2_b"].unsqueeze(1).to_broadcast([P, QT, P]), ALU.add), s1)
            close(b, s2)

    def prepare_router(self):
        pe, ve, ac, po, w = self.pe, self.ve, self.ac, self.po, self.w[7]
        square, ones, sim = self.carve(E3), self.carve(P), self.sim
        s_one = po.do(lambda e: e.memset(ones, 1.0))
        s = ve.do(lambda e: e.tensor_tensor(square, w["sim"], w["sim"], ALU.mult), self.w_ready[7])
        bank = self.banks.next()
        m = pe.do(lambda e, bank=bank: e.matmul(bank.ap[:, 0:E3], ones, square, start=True, stop=True), s, s_one, bank.free)
        s = ve.do(lambda e, bank=bank: e.tensor_copy(square, bank.ap[:, 0:E3]), m)
        bank.free = [s]
        s = po.do(lambda e: e.tensor_tensor(square, square, self.half[:, 0:E3], ALU.pow), s)
        s = ve.do(lambda e: e.tensor_scalar(square, square, 1e-12, None, ALU.max), s)
        s = ve.do(lambda e: e.reciprocal(square, square), s)
        self.sim_ready = ve.do(lambda e: e.tensor_tensor(sim, w["sim"], square, ALU.mult), s)
        gate = self.gate
        s = ac.do(lambda e: e.activation(gate, self.row["L3_ffn_gates"], ACT.Exp, scale=-1.0))
        s = ve.do(lambda e: e.tensor_scalar(gate, gate, 1.0, None, ALU.add), s)
        self.gate_ready = ve.do(lambda e: e.reciprocal(gate, gate), s)

    def mixture_attention(self):
        pe, ve, ac, po = self.pe, self.ve, self.ac, self.po
        self.begin("mixture")
        w, y = self.w[7], self.xn
        self.do_chores()
        normed, turned = self.stream()
        length, junk = self.carve(TILES), Ring([self.carve(P) for _ in range(2)])
        steps = []
        for t in range(TILES):
            z = junk.next()
            s = ac.do(lambda e, t=t, z=z: e.activation(z.ap, y[:, t, :], ACT.Square, accum_out=length[:, t:t + 1]),
                      normed[t], z.free)
            z.free = [s]
            steps.append(s)
        s = po.do(lambda e: e.tensor_tensor(length, length, self.half[:, :], ALU.pow), steps)
        s = ve.do(lambda e: e.tensor_scalar(length, length, 1e-12, None, ALU.max), s)
        s_len = ve.do(lambda e: e.reciprocal(length, length), s)
        logits, s = self.token_products(self.sim, E3, turned, None, self.sim_ready)
        wide = [P, TILES, E3]
        per_token = lambda v: v.unsqueeze(2).to_broadcast(wide)
        s = ve.do(lambda e: e.tensor_tensor(logits, logits, per_token(length), ALU.mult), s, s_len)
        s = ve.do(lambda e: e.tensor_tensor(logits, logits, self.gate.unsqueeze(1).to_broadcast(wide), ALU.subtract), s, self.gate_ready)
        active, idle, rest = self.carve(TILES, E3), self.carve(TILES), self.carve(TILES, E3)
        s1 = ve.do(lambda e: e.tensor_scalar(active, logits, 0.0, None, ALU.is_gt), s)
        s2 = ve.do(lambda e: e.tensor_reduce(idle, active, AX_X, ALU.add), s1)
        s_idle = ve.do(lambda e: e.tensor_scalar(idle, idle, 0.0, None, ALU.is_equal), s2)
        hot1, _, s3 = self.one_hot_of_max(logits, self.c["down16"], E3, s)
        s3 = ve.do(lambda e: e.scalar_tensor_tensor(rest, hot1, CAUSAL, logits, ALU.mult, ALU.add), s3)
        hot2, _, s3 = self.one_hot_of_max(rest, self.c["down16"], E3, s3)
        s3 = ve.do(lambda e: e.tensor_tensor(hot1, hot1, hot2, ALU.add), s3)
        s3 = ve.do(lambda e: e.tensor_tensor(hot1, hot1, per_token(idle), ALU.mult), s3, s_idle)
        s3 = ve.do(lambda e: e.tensor_tensor(active, active, hot1, ALU.add), s3)
        mix, top, total = logits, self.carve(TILES), self.carve(TILES)
        s3 = ve.do(lambda e: e.tensor_scalar(active, active, 1.0, -CAUSAL, ALU.subtract, ALU.mult), s3)
        s3 = ve.do(lambda e: e.scalar_tensor_tensor(mix, logits, 0.0, active, ALU.max, ALU.add), s3)
        s3 = ve.do(lambda e: e.tensor_reduce(top, mix, AX_X, ALU.max), s3)
        s3 = ve.do(lambda e: e.tensor_tensor(mix, mix, per_token(top), ALU.subtract), s3)
        s3 = ac.do(lambda e: e.activation(mix, mix, ACT.Exp), s3)
        s3 = ve.do(lambda e: e.tensor_reduce(total, mix, AX_X, ALU.add), s3)
        s3 = ve.do(lambda e: e.reciprocal(total, total), s3)
        s_mix = ve.do(lambda e: e.tensor_tensor(mix, mix, per_token(total), ALU.mult), s3)
        mix_t, mix_t_ready = self.turn_small(mix, E3, s_mix)
        parts = self.carve(TOKENS, dt=BF16)
        rest_t = self.carve(TOKENS)
        s_zero = po.do(lambda e: e.memset(parts[0:96, :], 0.0))
        s = ve.do(lambda e: e.tensor_copy(parts[0:E3, :], mix_t[0:E3, :]), mix_t_ready, s_zero)
        s = ve.do(lambda e: e.tensor_tensor(rest_t[0:E3, :], mix_t[0:E3, :], parts[0:E3, :], ALU.subtract), s)
        s = ve.do(lambda e: e.tensor_copy(parts[32:32 + E3, :], rest_t[0:E3, :]), s)
        second = self.carve(TOKENS, dt=BF16)
        s = ve.do(lambda e: e.tensor_copy(second[0:E3, :], rest_t[0:E3, :]), s)
        s_parts = ve.do(lambda e: e.tensor_tensor(parts[64:64 + E3, :], rest_t[0:E3, :], second[0:E3, :], ALU.subtract), s)
        spread1 = self.cb["spread1"].rearrange("p (e m) -> p e m", e=E3)
        spread2 = self.cb["spread2"].rearrange("p (e m) -> p e m", e=E3 // 2)

        def weights_of(selector, b):
            bank = self.banks.next()
            m = pe.do(lambda e: e.matmul(bank.ap, selector, parts[0:96, b * SEQ:(b + 1) * SEQ], start=True, stop=True),
                      s_parts, bank.free, self.setup)
            return bank, m

        scaled = Ring([self.carve(SEQ) for _ in range(4)])
        q_ring, k_ring = Ring([self.carve(SEQ) for _ in range(2)]), Ring([self.carve(SEQ) for _ in range(2)])
        v_half, v_full = Ring([self.carve(SEQ)]), Ring([self.carve(QT, P) for _ in range(2)])
        bank_qk, bank_v, bank_a, bank_o = self.banks.slots[4:8]
        self.banks.slots = self.banks.slots[0:4]

        def project(b, meanwhile):
            pending = []

            def products(x, z, s):
                m = pe.do(lambda e, x=x, z=z: e.matmul(bank_qk.ap, w["qk"][:, x * P:(x + 1) * P], z.ap,
                                                       start=x == 0, stop=x == E3 - 1), s, bank_qk.free)
                o = slice(64 * (x % 2), 64 * (x % 2) + 64)
                m2 = pe.do(lambda e, x=x, z=z, o=o: e.matmul(bank_v.ap[o, :], w["v"][:, x * D3:(x + 1) * D3], z.ap,
                                                             start=x < 2, stop=x >= E3 - 2), bank_v.free)
                z.free = [m2]
                return m2

            for x in range(E3):
                wb, m = weights_of(spread1[0:96, x, :], b)
                z = scaled.next()
                s = ve.do(lambda e, wb=wb, z=z: e.tensor_tensor(z.ap, wb.ap, self.xt[:, b * SEQ:(b + 1) * SEQ], ALU.mult), m, z.free)
                wb.free = [s]
                pending.append((x, z, s))
                if len(pending) > 2:
                    last = products(*pending.pop(0))
                meanwhile()
            for p in pending:
                last = products(*p)
            q, k, vh, vf = q_ring.next(), k_ring.next(), v_half.next(), v_full.next()
            sq = ac.do(lambda e: e.activation(q.ap[0:D3, :], bank_qk.ap[0:D3, :], ACT.Copy), last, q.free)
            sk = ac.do(lambda e: e.activation(k.ap[0:D3, :], bank_qk.ap[D3:P, :], ACT.Copy), last, k.free)
            sv = ac.do(lambda e: e.activation(vh.ap, bank_v.ap, ACT.Copy), last, vh.free)
            bank_qk.free, bank_v.free = [sq, sk], [sv]
            bank = self.banks.next()
            for j in range(QT):
                m = pe.do(lambda e, j=j, bank=bank: e.matmul(bank.ap[:, j * P:(j + 1) * P], vh.ap[:, j * P:(j + 1) * P],
                                                             self.c["fold"], start=True, stop=True), sv, bank.free)
            vh.free = [m]
            s = ve.do(lambda e, bank=bank: e.tensor_copy(vf.ap.rearrange("p t n -> p (t n)"), bank.ap), m, vf.free)
            bank.free = [s]
            return b, q, k, vf, [sq, sk], s

        probs, probs_t = Ring([self.carve(SEQ) for _ in range(2)]), Ring([self.carve(QT, P) for _ in range(2)])
        attended = Ring([self.carve(SEQ) for _ in range(2)])
        mixed = Ring([self.carve(SEQ) for _ in range(3)])
        col = Ring([self.carve(3) for _ in range(4)])

        def attend(b, q, k, vf, qk_ready, v_ready):
            a_t, tiles, state = attended.next(), {}, {}

            def scores_of(t):
                n = (t + 1) * P
                bank, prob, c = self.banks.next(), probs.next(), col.next()
                for k0, k1 in ([(0, t * P)] if t else []) + [(t * P, n)]:
                    m = pe.do(lambda e, k0=k0, k1=k1: e.matmul(
                        bank.ap[:, k0:k1], q.ap[0:D3, t * P:n], k.ap[0:D3, k0:k1], start=True, stop=k1 < n), qk_ready, bank.free)
                m = pe.do(lambda e: e.matmul(bank.ap[:, t * P:n], self.cb["eye_b"], self.cb["causal"], start=False, stop=True))
                s = ve.do(lambda e: e.tensor_reduce(c.ap[:, 0:1], bank.ap[:, 0:n], AX_X, ALU.max, negate=True), m, c.free)
                s = ve.do(lambda e: e.tensor_scalar(c.ap[:, 0:1], c.ap[:, 0:1], D3 ** -0.5, None, ALU.mult), s)
                s = ac.do(lambda e: e.activation(prob.ap[:, 0:n], bank.ap[:, 0:n], ACT.Exp, bias=c.ap[:, 0:1], scale=D3 ** -0.5,
                                                 accum_out=c.ap[:, 1:2]), s, prob.free)
                bank.free = [s]
                tiles[t] = (prob, c, s)

            def turn_probs(t):
                n = (t + 1) * P
                prob, c, s = tiles[t]
                s = ve.do(lambda e: e.reciprocal(c.ap[:, 2:3], c.ap[:, 1:2]), s)
                s = ve.do(lambda e: e.tensor_scalar(prob.ap[:, 0:n], prob.ap[:, 0:n], c.ap[:, 2:3], None, ALU.mult), s)
                c.free = [s]
                bank, pt = self.banks.next(), probs_t.next()
                for kt in range(t + 1):
                    m = pe.do(lambda e, kt=kt: e.transpose(bank.ap[:, kt * P:(kt + 1) * P], prob.ap[:, kt * P:(kt + 1) * P],
                                                           self.eye), s, bank.free)
                prob.free = [m]
                s = ac.do(lambda e: e.activation(pt.ap[:, 0:t + 1, :].rearrange("p t n -> p (t n)"), bank.ap[:, 0:n], ACT.Copy),
                          m, pt.free)
                bank.free = [s]
                tiles[t] = (pt, s)

            def weigh(t):
                pt, s = tiles[t]
                for kt in range(t + 1):
                    m = pe.do(lambda e, kt=kt: e.matmul(bank_a.ap[:, t * P:(t + 1) * P], vf.ap[:, kt, :], pt.ap[:, kt, :],
                                                        start=kt == 0, stop=kt == t), s, v_ready, bank_a.free)
                pt.free = [m]
                if t == QT - 1:
                    q.free = k.free = vf.free = [m]
                    state["ready"] = ac.do(lambda e: e.activation(a_t.ap, bank_a.ap, ACT.Copy), m, a_t.free)
                    bank_a.free = [state["ready"]]

            def scale(p):
                wb, m = weights_of(spread2[0:96, p, :], b)
                z = mixed.next()
                s = ve.do(lambda e: e.tensor_tensor(z.ap, wb.ap, a_t.ap, ALU.mult), m, z.free, state["ready"])
                wb.free = a_t.free = [s]
                state[p] = (z, s)

            def products(p):
                z, s = state[p]
                for j in range(QT):
                    m = pe.do(lambda e, j=j: e.matmul(
                        bank_o.ap[:, j * P:(j + 1) * P], z.ap[:, j * P:(j + 1) * P], w["o"][:, p * P:(p + 1) * P],
                        start=p == 0 and j == 0, stop=p == E3 // 2 - 1, skip_group_check=True), s, bank_o.free)
                z.free = [m]
                if p == E3 // 2 - 1:
                    bank_o.free = [self.add_to_x(QT * b + j, bank_o.ap[:, j * P:(j + 1) * P], 7, m) for j in range(QT)]
                    self.store(b)

            pieces = []
            for i in range(QT + 2):
                pieces.append([(f, t) for f, t in ((turn_probs, i - 1), (scores_of, i), (weigh, i - 2)) if 0 <= t < QT])
            for p in range(E3 // 2 + 1):
                pieces.append([(f, n) for f, n in ((scale, p), (products, p - 1)) if 0 <= n < E3 // 2])
            return pieces

        def run(pieces, n):
            for _ in range(min(n, len(pieces))):
                for f, t in pieces.pop(0):
                    f(t)

        pieces = []
        for b in range(BATCH):
            now = project(b, lambda: run(pieces, 1))
            run(pieces, len(pieces))
            pieces = attend(*now)
        run(pieces, len(pieces))

    def close(self):
        self.sp.do(lambda e: e.nop(), self.stores, self.loads)


STAGES = [Program.image_attention, Program.top1_experts, Program.one_head, Program.batch_attention,
          Program.masked_attention, Program.scaled_feed_forward, Program.decoder_block, Program.mixture_attention]


def build(nc, dram, const_widths, const_b_widths):
    with ExitStack() as ctx:
        p = Program(nc, ctx, dram, const_widths, const_b_widths)
        p.open()
        for stage in STAGES:
            stage(p)
        p.close()
        p.finish()


def kernel(**inputs):
    import concourse.bacc as bacc
    from concourse.bass_utils import run_bass_kernel_spmd

    i = {k: np.asarray(v) for k, v in inputs.items()}
    const, const_widths, const_b, const_b_widths = constants()
    arrays = {
        "x": i["x"].reshape(TOKENS, P), "ctx": i["ctx_1024"].reshape(CTX_ROWS, P),
        "mask": i["mask_BxSxS2_bf0"].reshape(TOKENS, CTX),
        "rows": np.concatenate([i[k].reshape(-1) for k in ROWS])[None],
        "small": np.concatenate([i["L0_ffn_b2"], i["L1_ffn_b2"]], 1),
        "const": const, "const_b": const_b,
    }
    for k, parts in enumerate(WEIGHTS):
        arrays[f"weights{k}"] = np.concatenate([lay(i) for _, lay in parts.values()], 1)
    nc = bacc.Bacc("TRN2", target_bir_lowering=False, num_devices=1)
    dram, feed = {}, {}
    for name, a in arrays.items():
        a = np.ascontiguousarray(a)
        feed[f"in_{name}"] = a
        dram[name] = nc.dram_tensor(f"in_{name}", a.shape, mybir.dt.from_np(a.dtype), kind="ExternalInput").ap()
    dram["out"] = nc.dram_tensor("out", (TOKENS, P), F32, kind="ExternalOutput").ap()
    build(nc, dram, const_widths, const_b_widths)
    r = run_bass_kernel_spmd(nc, [feed], core_ids=[0])
    return r.results[0]["out"].reshape(BATCH, SEQ, P)
```

```python
from contextlib import ExitStack

import numpy as np

import concourse.bass as bass
from concourse import mybir

ALU = mybir.AluOpType
ACT = mybir.ActivationFunctionType
F32 = mybir.dt.float32
BF16 = mybir.dt.bfloat16
U8 = mybir.dt.uint8
U16 = mybir.dt.uint16
AX_X = mybir.AxisListType.X

P = 128
BATCH, SEQ, CTX = 4, 512, 154
TOKENS = BATCH * SEQ
TILES = TOKENS // P
QT = SEQ // P
CTX_ROWS = BATCH * CTX
CTX_TILES = -(-CTX_ROWS // P)
CTX_LAST = CTX_ROWS - (CTX_TILES - 1) * P
CTX_REST = CTX - P
BANK = 512
EPS = 1e-5
MASKED = -1e18
CAUSAL = -1e30

H0, D0 = 16, 64
PAIRS = H0 // 2
KEYS0 = SEQ + CTX
KT0 = -(-KEYS0 // P)
EXPERTS, FF = 8, 512
ROOM = 10
FT = FF // P
E3, D3 = 16, 64


def _cols(v):
    return v.reshape(-1, P).T


def _kt(w):
    k = w.shape[0] // P
    return w.reshape(k, P, -1).transpose(1, 0, 2).reshape(P, -1)


GROUPS, WIDE = 4, P // 4


def _by_group(v):
    return np.tile(v.reshape(GROUPS, WIDE), (1, 4)).T


WEIGHTS = [
    {
        "ln1_g": (1, lambda i: _cols(i["L0_xattn_ln1_g"])), "ln1_b": (1, lambda i: _cols(i["L0_xattn_ln1_b"])),
        "ln2_g": (1, lambda i: _cols(i["L0_xattn_ln2_g"])), "ln2_b": (1, lambda i: _cols(i["L0_xattn_ln2_b"])),
        "wq": (1024, lambda i: i["L0_xattn_Wq"]), "wkv": (2048, lambda i: i["L0_xattn_Wkv"]),
        "wo": (1024, lambda i: _kt(i["L0_xattn_Wo"])),
    },
    {
        "gate": (EXPERTS, lambda i: i["L0_ffn_gate_w"].T),
        "w1": (EXPERTS * FF, lambda i: i["L0_ffn_w1"].transpose(1, 0, 2).reshape(P, -1)),
        "b1": (EXPERTS * FT, lambda i: _cols(i["L0_ffn_b1"].reshape(-1))),
        "w2": (EXPERTS * FF, lambda i: _kt(i["L0_ffn_w2"].reshape(-1, P))),
    },
    {
        "wq": (P, lambda i: i["L1_xattn_Wq"].T), "wk": (P, lambda i: i["L1_xattn_Wk"].T),
        "wv": (P, lambda i: i["L1_xattn_Wv"].T),
        "bq": (1, lambda i: _cols(i["L1_xattn_bq"])), "bk": (1, lambda i: _cols(i["L1_xattn_bk"])),
    },
    {
        "in": (3 * P, lambda i: i["L1_ffn_in_proj_w"].T), "out": (P, lambda i: i["L1_ffn_out_w"].T),
        "router": (EXPERTS, lambda i: i["L1_ffn_router_w"].T),
        "w1": (EXPERTS * P, lambda i: i["L1_ffn_w1"].transpose(2, 0, 1).reshape(P, -1)),
        "w2": (EXPERTS * P, lambda i: i["L1_ffn_w2"].transpose(2, 0, 1).reshape(P, -1)),
        "b1": (EXPERTS, lambda i: i["L1_ffn_b1"].T),
    },
    {
        "wq": (P, lambda i: i["L2_xattn_Wq"].T), "wk": (P, lambda i: i["L2_xattn_Wk"].T),
        "wv": (P, lambda i: i["L2_xattn_Wv"].T), "wo": (P, lambda i: i["L2_xattn_Wo"].T),
        "bq": (GROUPS, lambda i: _by_group(i["L2_xattn_bq"])), "bk": (GROUPS, lambda i: _by_group(i["L2_xattn_bk"])),
        "bv": (1, lambda i: _cols(i["L2_xattn_bv"])),
    },
    {
        "w1": (FF, lambda i: i["L2_ffn_w1_w"].T), "w2": (FF, lambda i: i["L2_ffn_w2_w"].T),
        "h1": (FT * FF, lambda i: _kt(i["L2_ffn_h1_w"].T)), "h2": (FT * FF, lambda i: _kt(i["L2_ffn_h2_w"].T)),
        "w3": (FT * P, lambda i: _kt(i["L2_ffn_w3_w"].T)),
        "s1": (FT, lambda i: _cols(i["L2_ffn_w1_s"])), "s2": (FT, lambda i: _cols(i["L2_ffn_w2_s"])),
        "sh1": (FT, lambda i: _cols(i["L2_ffn_h1_s"])), "sh2": (FT, lambda i: _cols(i["L2_ffn_h2_s"])),
    },
    {
        "qkv": (3 * P, lambda i: i["L3_xattn_qkv_w"].T), "sa_out": (P, lambda i: i["L3_xattn_sa_out_w"].T),
        "in": (3 * P, lambda i: i["L3_xattn_in_proj_w"].T), "mha_out": (P, lambda i: i["L3_xattn_mha_out_w"].T),
        "lin1": (FF, lambda i: i["L3_xattn_lin1_w"].T), "lin2": (FT * P, lambda i: _kt(i["L3_xattn_lin2_w"].T)),
        "bq": (GROUPS, lambda i: _by_group(i["L3_xattn_in_proj_b"][0:P])),
        "bk": (GROUPS, lambda i: _by_group(i["L3_xattn_in_proj_b"][P:2 * P])),
        "bv": (1, lambda i: _cols(i["L3_xattn_in_proj_b"][2 * P:3 * P])), "lin1_b": (FT, lambda i: _cols(i["L3_xattn_lin1_b"])),
    },
    {
        "sim": (E3, lambda i: i["L3_ffn_sim_matrix"]),
        "qk": (E3 * 2 * D3, lambda i: np.concatenate([i["L3_ffn_q_proj"], i["L3_ffn_k_proj"]], 2)
               .transpose(1, 0, 2).reshape(P, -1)),
        "v": (E3 * D3, lambda i: i["L3_ffn_v_proj"].transpose(1, 0, 2).reshape(P, -1)),
        "o": (E3 // 2 * P, lambda i: _kt(i["L3_ffn_o_proj"].reshape(-1, P))),
    },
]

ROWS = {
    "g_xattn": 4, "g_ffn": 4, "L0_ffn_gate_b": 8, "L0_ffn_expert_bias": 8, "L1_xattn_bv": P,
    "L1_ffn_in_proj_b": 3 * P, "L1_ffn_out_b": P, "L1_ffn_ln1_g": P, "L1_ffn_ln1_b": P, "L1_ffn_router_b": 8,
    "L1_ffn_ln2_g": P, "L1_ffn_ln2_b": P, "L2_xattn_bo": P, "L2_ffn_w3_s": P, "L3_xattn_qkv_b": 3 * P,
    "L3_xattn_sa_out_b": P, "L3_xattn_mha_out_b": P, "L3_xattn_lin2_b": P, "L3_xattn_ln1_g": P,
    "L3_xattn_ln1_b": P, "L3_xattn_ln2_g": P, "L3_xattn_ln2_b": P, "L3_xattn_ln3_g": P, "L3_xattn_ln3_b": P,
    "L3_ffn_gates": 16,
}


def _offsets(widths):
    at, out = 0, {}
    for name, n in widths.items():
        out[name] = (at, n)
        at += n
    return out, at


def flat_chunks(heads):
    n = heads // GROUPS * CTX
    return [(c * P, min(P, n - c * P)) for c in range(-(-n // P))]


def constants():
    eye = np.eye(P, dtype=np.float32)
    c = {"eye": eye}
    for heads in (16, 8):
        d = P // heads
        c[f"head{heads}"] = (np.arange(P)[:, None] % WIDE // d == np.arange(heads // GROUPS)[None]).astype(np.float32)
        chunks = flat_chunks(heads)
        m = np.zeros((P, len(chunks), GROUPS, heads // GROUPS), np.float32)
        for n, (f0, rows) in enumerate(chunks):
            for r in range(rows):
                m[r, n, :, (f0 + r) // CTX] = 1.0
        c[f"block{heads}"] = m.reshape(P, -1)
    c["down8"] = np.tile(np.arange(8, 0, -1, dtype=np.float32), (P, 1))
    c["down16"] = np.tile(np.arange(16, 0, -1, dtype=np.float32), (P, 1))
    c["fold"] = np.tile(np.eye(D3, dtype=np.float32), (2, 2))
    b = {"eye_b": eye}
    b["causal"] = np.where(np.arange(P)[None] <= np.arange(P)[:, None], 0.0, CAUSAL).astype(np.float32)
    one = np.zeros((P, E3, P), np.float32)
    two = np.zeros((P, E3 // 2, P), np.float32)
    for part in range(3):
        for e in range(E3):
            one[32 * part + e, e, :] = 1.0
            two[32 * part + e, e // 2, (e % 2) * D3:(e % 2 + 1) * D3] = 1.0
    b["spread1"], b["spread2"] = one.reshape(P, -1), two.reshape(P, -1)
    f = np.concatenate(list(c.values()), 1)
    bb = (np.concatenate(list(b.values()), 1).view(np.uint32) >> 16).astype(np.uint16)
    return f, {k: v.shape[1] for k, v in c.items()}, bb, {k: v.shape[1] for k, v in b.items()}


class Step:

    def __init__(self, engine, emit, after):
        self.engine, self.emit, self.after = engine, emit, after
        self.sem, self.value, self.wanted = None, None, False


def _flat(after):
    for a in after:
        if isinstance(a, (list, tuple)):
            yield from _flat(a)
        elif a is not None:
            yield a


class Engine:
    def __init__(self, name):
        self.name, self.queue, self.sem = name, [], None

    def do(self, emit, *after):
        step = Step(self, emit, list(_flat(after)))
        for a in step.after:
            a.wanted = True
        step.sem = self.sem
        self.queue.append(step)
        return step

    def count(self):
        at = {}
        for s in self.queue:
            if s.wanted and s.value is None:
                at[s.sem] = at.get(s.sem, 0) + 1
                s.value = at[s.sem]

    def run(self, eng):
        seen = {}
        for s in self.queue:
            need = {}
            for a in s.after:
                need[a.sem] = max(need.get(a.sem, 0), a.value)
            for sem, value in need.items():
                if seen.get(sem, 0) < value:
                    eng.wait_ge(sem, value)
                    seen[sem] = value
            last = s.emit(eng)
            if s.wanted:
                last.then_inc(s.sem, 16 if isinstance(s, Load) else 1)


class Load(Step):
    pass


class Bank:

    def __init__(self, ap):
        self.ap, self.free = ap, []


class Ring:

    def __init__(self, aps):
        self.slots, self.at = [Bank(a) for a in aps], -1

    def next(self):
        self.at = (self.at + 1) % len(self.slots)
        return self.slots[self.at]


class Program:
    def __init__(self, nc, ctx, dram, const_widths, const_b_widths):
        self.nc, self.ctx, self.dram = nc, ctx, dram
        self.pe, self.ve, self.ac, self.po, self.sp = (Engine(n) for n in
                                                       ("tensor", "vector", "scalar", "gpsimd", "sync"))
        self.engines = [self.pe, self.ve, self.ac, self.po, self.sp]
        self.loads = []
        self.widths = {"const": const_widths, "const_b": const_b_widths}
        self.evacuations = 0

    def sb(self, name, shape, dt=F32):
        return self.ctx.enter_context(self.nc.sbuf_tensor(name, shape, dt))

    def stage(self, name):
        for e in self.engines[:4]:
            e.sem = self.ctx.enter_context(self.nc.semaphore(f"{e.name}_{name}"))

    def load_sem(self, name):
        return self.ctx.enter_context(self.nc.semaphore(f"dma_{name}"))

    def dma(self, name, out, in_, *after, sem=None, turn=1, engine=None):
        engine = engine or self.sp
        step = Load(engine, lambda e: e.dma_start(out, in_), list(_flat(after)))
        for a in step.after:
            a.wanted = True
        step.sem = sem or self.load_sem(name)
        step.value, step.wanted = 16 * turn, True
        engine.queue.append(step)
        self.loads.append(step)
        return step

    def evacuate(self, out, psum, *after):
        self.evacuations += 1
        if self.evacuations % 2:
            return self.ac.do(lambda e: e.activation(out, psum, ACT.Copy), *after)
        return self.ve.do(lambda e: e.tensor_copy(out, psum), *after)

    def finish(self):
        for e in self.engines:
            e.count()
        with self.nc.Block() as block:
            for e in self.engines:
                place = {"tensor": block.tensor, "vector": block.vector, "scalar": block.scalar,
                         "gpsimd": block.gpsimd, "sync": block.sync}[e.name]
                place(lambda eng, e=e: e.run(eng))

    def carve(self, *shape, dt=F32):
        n = int(np.prod(shape))
        words = n if dt == F32 else -(-n // 2)
        ap = self.work[:, self.work_at:self.work_at + words]
        self.work_at += words
        assert self.work_at <= self.work_words, self.work_at
        if dt != F32:
            ap = ap.bitcast(dt)
        if len(shape) == 2:
            return ap.rearrange("p (a b) -> p a b", a=shape[0])
        if len(shape) == 3:
            return ap.rearrange("p (a b c) -> p a b c", a=shape[0], b=shape[1])
        if len(shape) == 4:
            return ap.rearrange("p (a b c d) -> p a b c d", a=shape[0], b=shape[1], c=shape[2])
        return ap

    def begin(self, name):
        before = [e.queue[-1] for e in self.engines[:4] if e.queue]
        self.do_chores(keep=1)
        self.stage(name)
        self.work_at = 0
        self.before = before
        for e in self.engines[:4]:
            e.fence = e.do(lambda g: g.nop(), *before)

    def chore(self):
        if self.chores:
            self.chores.pop(0)()

    def split_weights(self, stage, names, scalar=False):
        po, w = self.po, self.w[stage]
        split = {name: w[name].bitcast(BF16).rearrange("p (c s n) -> p c s n", s=2, n=BANK) for name in names}
        self.split, self.split_ready = split, []
        pair = self.pair

        def copy(out, src, *after):
            if scalar:
                return self.ac.do(lambda e: e.activation(out, src, ACT.Copy), *after)
            return po.do(lambda e: e.tensor_copy(out, src), *after)

        def part(src, high_low):
            s = copy(high_low[:, 0, :], src, self.w_ready[stage], pair.free)
            return po.do(lambda e: e.tensor_tensor(high_low[:, 1, :], src, high_low[:, 0, :], ALU.subtract), s)

        for name in names:
            for c in range(w[name].shape[1] // BANK):
                s = part(w[name][:, c * BANK:(c + 1) * BANK], pair.ap)
                yield
                self.split_ready = pair.free = [copy(split[name][:, c, :, :], pair.ap, s)]
                yield

    def products(self, out, left, right, start, stop, *after):
        for n, (a, b) in enumerate(((0, 0), (0, 1), (1, 0))):
            m = self.pe.do(lambda e, n=n, l=left(a), r=right(b): e.matmul(out, l, r, start=start and n == 0,
                                                                          stop=stop and n == 2), *after)
        return m

    def store(self, b):
        rows = slice(QT * b, QT * b + QT)
        out = self.dram["out"].rearrange("(t p) d -> p t d", p=P)
        self.stores.append(self.dma(f"out{b}", out[:, rows, :], self.x[:, rows, :], self.x_last[rows]))

    def do_chores(self, keep=0):
        while len(self.chores) > keep:
            self.chore()

    def follow(self, b):
        rows = slice(QT * b, QT * b + QT)
        self.parity[b] ^= 1
        room = self.room[:, 2 * b + self.parity[b], :]
        ((measure, scale),), normed = self.norm_groups(
            self.x[:, rows, :], self.xn[:, rows, :], self.x_last[rows], QT, room=room, free=self.xn_free[b])

        def pause():
            pass

        def turn():
            turned = self.turn(self.xn[:, rows, :], self.xt[:, b * SEQ:(b + 1) * SEQ], normed, n=QT, after=(self.xt_free[b],))
            self.next_normed[rows], self.next_turned[rows] = normed, turned

        self.chores += [measure, scale, pause, turn]

    def stream(self):
        return self.next_normed, self.next_turned

    def norm_groups(self, src, dst, ready, n=TILES, rows=P, gain=None, bias=None, room=None, free=None):
        ve, po = self.ve, self.po
        room = self.carve(ROOM * n) if room is None else room
        stats, mv = (room[:, a * n:z * n].rearrange("p (t k) -> p t k", t=n) for a, z in ((0, 6), (6, 8)))
        var, rstd = room[:, 8 * n:9 * n], room[:, 9 * n:10 * n]
        full = n if rows == P else n - 1
        groups = [(P, a, min(a + QT, full)) for a in range(0, full, QT)] + ([(rows, full, n)] if full < n else [])
        out, power = [None] * n, {}

        def measure(r, a, b):
            for t in range(a, b):
                s = ve.do(lambda e, t=t: e.bn_stats(stats[0:r, t, :], src[0:r, t, :]), ready[t])
            for t in range(a, b):
                m = ve.do(lambda e, t=t: e.bn_aggr(mv[0:r, t, :], stats[0:r, t, :]), s)
            s = ve.do(lambda e: e.tensor_scalar(var[0:r, a:b], mv[0:r, a:b, 1], EPS, None, ALU.add), m)
            power[a] = po.do(lambda e: e.tensor_tensor(rstd[0:r, a:b], var[0:r, a:b], self.minus_half[0:r, 0:b - a], ALU.pow),
                             s, self.halves)

        def scale(r, a, b):
            for t in range(a, b):
                out[t] = ve.do(lambda e, t=t: e.tensor_scalar(dst[0:r, t, :], src[0:r, t, :], mv[0:r, t, 0:1],
                                                              rstd[0:r, t:t + 1], ALU.subtract, ALU.mult), power[a], free)
            if gain is not None:
                o, wide = dst[0:r, a:b, :], [r, b - a, P]
                s = ve.do(lambda e: e.tensor_tensor(o, o, gain[0:r].unsqueeze(1).to_broadcast(wide), ALU.mult), out[a:b])
                s = ve.do(lambda e: e.tensor_tensor(o, o, bias[0:r].unsqueeze(1).to_broadcast(wide), ALU.add), s)
                out[a:b] = [s] * (b - a)

        return [(lambda g=g: measure(*g), lambda g=g: scale(*g)) for g in groups], out

    def normalize(self, *args, **kwargs):
        groups, out = self.norm_groups(*args, **kwargs)
        last = None
        for measure, scale in groups:
            measure()
            if last:
                last()
            last = scale
        last()
        return out

    def turn(self, src, dst, ready, rows=P, n=TILES, scale=None, shift=None, after=()):
        out = []
        for g in range(0, n, 4):
            bank = self.banks.next()
            tiles = range(g, min(g + 4, n))
            width = sum(rows if t == n - 1 else P for t in tiles)
            for t in tiles:
                r = rows if t == n - 1 else P
                s = self.pe.do(lambda e, t=t, r=r, c=(t - g) * P, b=bank.ap: e.transpose(
                    b[:, c:c + r], src[0:r, t, :], self.eye[0:r, 0:r]), ready[t], bank.free, self.setup)
            o, i = dst[:, g * P:g * P + width], bank.ap[:, 0:width]
            if scale is not None:
                if (g // 4) % 2:
                    v = self.ve.do(lambda e, o=o, i=i: e.tensor_scalar(o, i, scale, shift, ALU.mult, ALU.add), s, *after)
                else:
                    v = self.ac.do(lambda e, o=o, i=i: e.activation(o, i, ACT.Identity, bias=shift, scale=scale), s, *after)
            else:
                v = self.evacuate(o, i, s, *after)
            bank.free = [v]
            out += [v] * len(tiles)
        return out

    def add_to_x(self, tile, psum, gate, ready, row=None, factor=None, op=ALU.add):
        ve, x = self.ve, self.x[:, tile, :]
        g = self.gates[:, gate:gate + 1]
        if row is None:
            self.x_last[tile] = ve.do(lambda e: e.scalar_tensor_tensor(x, psum, g, x, ALU.mult, ALU.add),
                                      ready, self.x_last[tile], self.rows_ready)
            return self.x_last[tile]
        t = self.scratch[:, tile % 4, :]
        if factor is None:
            s = ve.do(lambda e: e.tensor_tensor(t, psum, row, op), ready, self.rows_ready, self.scratch_free[tile % 4])
        else:
            s = ve.do(lambda e: e.scalar_tensor_tensor(t, psum, factor, row, ALU.mult, ALU.add), ready,
                      self.scratch_free[tile % 4])
        self.x_last[tile] = ve.do(lambda e: e.scalar_tensor_tensor(x, t, g, x, ALU.mult, ALU.add), s, self.x_last[tile])
        self.scratch_free[tile % 4] = self.x_last[tile]
        return s

    def add_batch_to_x(self, b, y, gate, ready):
        rows = slice(QT * b, QT * b + QT)
        x, g = self.x[:, rows, :], self.gates[:, gate:gate + 1]
        s = self.ve.do(lambda e: e.scalar_tensor_tensor(x, y[:, rows, :], g, x, ALU.mult, ALU.add), ready, self.x_last[rows],
                       self.rows_ready)
        self.x_last[rows] = [s] * QT
        return s

    def open(self):
        ve, po, pe, nc = self.ve, self.po, self.pe, self.nc
        self.stage("setup")
        d = self.dram
        psum = self.ctx.enter_context(nc.psum_tensor("banks", [P, 8 * BANK], F32))
        self.psum = psum
        self.banks = Ring([psum[:, b * BANK:(b + 1) * BANK] for b in range(8)])
        self.x = self.sb("x", [P, TILES, P])
        self.xn = self.sb("xn", [P, TILES, P])
        self.xt = self.sb("xt", [P, TOKENS])
        self.context = self.sb("context", [P, BATCH, 2 * CTX])
        self.room = self.sb("norm_room", [P, 3 * BATCH, ROOM * QT])
        self.parity, self.chores = [0] * BATCH, []
        self.next_normed, self.next_turned = [None] * TILES, [None] * TILES
        self.stores = []
        self.pair = Bank(self.sb("split", [P, 2, BANK], BF16)[:, :, :])
        self.xn_free, self.xt_free = [None] * BATCH, [None] * BATCH
        self.scratch = self.sb("scratch", [P, 4, P])
        self.gates = self.sb("gates", [P, 8])
        self.x_last = [None] * TILES
        self.scratch_free = [None] * 4
        self.minus_half = self.sb("minus_half", [P, TILES])
        self.half = self.sb("half", [P, TILES])
        self.sim, self.gate = self.sb("similarity", [P, E3])[:, :], self.sb("router_gate", [P, E3])[:, :]
        slots = {"a": self.sb("weights_a", [P, 4116]), "b": self.sb("weights_b", [P, 8232]),
                 "c": self.sb("weights_c", [P, 3484])}
        self.work_words = 21800
        self.work = self.sb("work", [P, self.work_words])
        const, cw = self.sb("const", [P, sum(self.widths["const"].values())]), self.widths["const"]
        cb = self.sb("const_b", [P, sum(self.widths["const_b"].values())], BF16)
        rows_at, rows_n = _offsets(ROWS)
        rows = self.sb("rows", [P, rows_n])
        self.small = self.sb("small", [8, 2 * P])
        self.row = {k: rows[:, a:a + n] for k, (a, n) in rows_at.items()}
        self.c = {k: const[:, a:a + n] for k, (a, n) in _offsets(cw)[0].items()}
        self.cb = {k: cb[:, a:a + n] for k, (a, n) in _offsets(self.widths["const_b"])[0].items()}
        self.eye = self.c["eye"]

        self.w, self.w_ready, self.weight_plan = [], [], []
        for k, (slot, base) in enumerate([("a", 0), ("b", 0), ("c", 0), ("c", 386), ("c", 386 + 2576),
                                          ("b", 0), ("b", 5648), ("a", 0)]):
            at, n = _offsets({name: w for name, (w, _) in WEIGHTS[k].items()})
            assert base + n <= slots[slot].shape[1], (k, base + n)
            self.w.append({name: slots[slot][:, base + a:base + a + m] for name, (a, m) in at.items()})
            self.weight_plan.append((slots[slot][:, base:base + n], d[f"weights{k}"]))

        self.begin_work()
        self.ctx_rows = ctx_rows = self.carve(CTX_TILES, P)
        xr = d["x"].rearrange("(t p) d -> p t d", p=P)
        self.load_x = [self.dma(f"x{b}", self.x[:, QT * b:QT * b + QT, :], xr[:, QT * b:QT * b + QT, :])
                       for b in range(BATCH)]
        load_c = self.dma("const", const[:, :], d["const"])
        full = CTX_TILES - 1
        self.load_ctx = [self.dma("context", ctx_rows[:, 0:full, :],
                                  d["ctx"][0:full * P, :].rearrange("(t p) d -> p t d", p=P)),
                         self.dma("context_last", ctx_rows[0:CTX_LAST, full, :], d["ctx"][full * P:CTX_ROWS, :])]
        self.load_weights(0)
        load_rows = self.dma("rows", rows[:, :], d["rows"].to_broadcast([P, rows_n]))
        load_cb = self.dma("const_b", cb[:, :].bitcast(U16), d["const_b"])
        load_small = self.dma("small", self.small[:, :], d["small"])
        for k in (1, 2, 3, 4):
            self.load_weights(k)

        halves = [po.do(lambda e: e.memset(self.minus_half[:, :], -0.5)), po.do(lambda e: e.memset(self.half[:, :], 0.5))]
        clean = ve.do(lambda e: e.memset(psum[:, 5 * BANK:6 * BANK], 0.0))
        self.setup, self.halves = [load_c, clean], halves
        self.ctxn_t = self.sb("ctxn_t", [P, CTX_ROWS])

        def late():
            tanh = self.ac.do(lambda e: e.activation(self.gates[:, :], rows[:, 0:8], ACT.Tanh), load_rows)
            self.rows_ready = [load_rows, load_small, load_cb, tanh]
        self.late_tables = late

    def open_context(self):
        ctxn, whole = self.carve(CTX_TILES, P), self.carve(CTX_ROWS)
        w, ve = self.w[0], self.ve
        ready = self.normalize(self.ctx_rows, ctxn, [self.load_ctx] * CTX_TILES, CTX_TILES, CTX_LAST)
        self.ctxn_ready = self.turn(ctxn, self.ctxn_t, ready, rows=CTX_LAST, n=CTX_TILES,
                                    scale=w["ln1_g"], shift=w["ln1_b"], after=(self.w_ready[0],))
        turned = self.turn(self.ctx_rows, whole, [self.load_ctx] * CTX_TILES, rows=CTX_LAST, n=CTX_TILES)
        by_batch = whole.rearrange("p (b k) -> p b k", b=BATCH)
        self.context_ready = [self.po.do(lambda e, c=c: e.tensor_copy(self.context[:, :, c * CTX:(c + 1) * CTX], by_batch),
                                         turned) for c in range(2)]

    def begin_work(self):
        self.work_at = 0

    def load_weights(self, k, *after):
        out, src = self.weight_plan[k]
        self.w_ready += [None] * (k + 1 - len(self.w_ready))
        self.w_ready[k] = self.dma(f"weights{k}", out, src, *after)

    def image_attention(self):
        pe, ve, ac, po = self.pe, self.ve, self.ac, self.po
        w, x = self.w[0], self.x
        first = self.normalize(x[:, 0:QT, :], self.xn[:, 0:QT, :], [self.load_x[0]] * QT, QT)
        second = self.normalize(self.xn[:, 0:QT, :], self.xn[:, 0:QT, :], first, QT)
        ln2 = {"scale": w["ln2_g"], "shift": w["ln2_b"], "after": (self.w_ready[0],)}
        latents = self.turn(self.xn[:, 0:QT, :], self.xt[:, 0:SEQ], second, n=QT, **ln2)
        self.open_context()
        self.begin("image")

        q_split = Ring([self.carve(2, SEQ, dt=BF16) for _ in range(2)])
        k_split = Ring([self.carve(2, 2, KEYS0, dt=BF16) for _ in range(2)])
        values = Ring([self.carve(KT0, P) for _ in range(3)])
        probs = Ring([self.carve(KEYS0) for _ in range(4)])
        probs_t = Ring([self.carve(2, KT0, 2 * P) for _ in range(2)])
        sums = Ring([self.carve(4) for _ in range(2)])
        inverse = Ring([self.carve(4) for _ in range(2)])
        spread = Ring([self.carve(2, 2, D0) for _ in range(2)])
        neg_max = Ring([self.carve(1) for _ in range(4)])
        mixed = self.carve(PAIRS, SEQ)
        mixed_free = [None, None]
        scores = Ring([self.psum[:, 0:2 * BANK], self.psum[:, 2 * BANK:4 * BANK]])
        turned = [Bank(self.psum[:, 4 * BANK:5 * BANK]), Bank(self.psum[:, 5 * BANK:6 * BANK])]
        out_bank = Bank(self.psum[:, 6 * BANK:7 * BANK])
        side = Bank(self.psum[:, 7 * BANK:8 * BANK])
        for bank in (*scores.slots, *turned, out_bank, side):
            bank.free = [b.free for b in self.banks.slots]
        self.banks = Ring([])
        self.banks.slots = turned

        copy_sems = {(s, h): self.load_sem(f"keys{s}{h}") for s in range(2) for h in range(2)}
        copy_turn = {key: 0 for key in copy_sems}
        groups = [(b, p) for b in range(BATCH) for p in range(PAIRS)]
        state = {}

        def project_q(g, n):
            b, p = g
            st = state[g] = {"q": q_split.next(), "k": k_split.next(), "v": values.next(), "n": n}
            m = pe.do(lambda e: e.matmul(side.ap[:, 0:SEQ], w["wq"][:, p * P:(p + 1) * P],
                                         self.xt[:, b * SEQ:(b + 1) * SEQ], start=True, stop=True),
                      latents[4 * b + 3], side.free)
            q, hi = st["q"].ap, []
            for h in (0, 1):
                own = slice(64 * h, 64 * h + 64)
                hi.append(ac.do(lambda e, h=h, own=own: e.activation(q[own, h, :], side.ap[own, 0:SEQ], ACT.Copy, scale=D0 ** -0.5),
                                m, st["q"].free))
            side.free = [None]

            def low(h):
                own, other = slice(64 * h, 64 * h + 64), slice(64 - 64 * h, 128 - 64 * h)
                return ve.do(lambda e, h=h, own=own, other=other: e.scalar_tensor_tensor(
                    q[other, h, :], side.ap[own, 0:SEQ], D0 ** -0.5, q[own, h, :], ALU.mult, ALU.subtract), hi[h], st["q"].free)

            def rest():
                for h in (0, 1):
                    st[f"q{h}"] = low(h)
                side.free = [hi, st["q0"], st["q1"]]
            return rest

        def project_k(g, part):
            b, p = g
            st = state[g]
            src, n, c0 = ((self.xt[:, b * SEQ:(b + 1) * SEQ], SEQ, 0) if part == 0 else
                          (self.ctxn_t[:, b * CTX:(b + 1) * CTX], CTX, SEQ))
            m = pe.do(lambda e: e.matmul(side.ap[:, 0:n], w["wkv"][:, p * P:(p + 1) * P], src, start=True, stop=True),
                      side.free, self.ctxn_ready if part else None)
            if part == 1:
                for c, r0, rows in ((P * 2, 0, P), (P * 3, P, CTX_REST)):
                    m = pe.do(lambda e, c=c, r0=r0, rows=rows: e.matmul(
                        side.ap[0:rows, c:c + P], self.ctxn_t[:, b * CTX + r0:b * CTX + r0 + rows],
                        w["wkv"][:, 1024 + p * P:1024 + (p + 1) * P], start=True, stop=True))
            k, hi = st["k"].ap, []
            for h in (0, 1):
                own = slice(64 * h, 64 * h + 64)
                hi.append(ac.do(lambda e, h=h, own=own: e.activation(k[own, h, 0, c0:c0 + n], side.ap[own, 0:n], ACT.Copy),
                                m, st["k"].free))
            if part == 1:
                v, free = st["v"].ap, st["v"].free
                st["v_ready"] = [
                    ac.do(lambda e: e.activation(v[:, 4, :], side.ap[:, 2 * P:3 * P], ACT.Copy), free),
                    ac.do(lambda e: e.activation(v[0:CTX_REST, 5, :], side.ap[0:CTX_REST, 3 * P:4 * P], ACT.Copy))]

            def rest():
                low = []
                for h in (0, 1):
                    own = slice(64 * h, 64 * h + 64)
                    low.append(ve.do(lambda e, h=h, own=own: e.tensor_tensor(
                        k[own, h, 1, c0:c0 + n], side.ap[own, 0:n], k[own, h, 0, c0:c0 + n], ALU.subtract), hi[h],
                        st["v_ready"] if part else None))
                    if part == 1:
                        slot, other = st["n"] % 2, slice(64 - 64 * h, 128 - 64 * h)
                        copy_turn[slot, h] += 1
                        st[f"k{h}"] = self.dma("keys", k[other, h, :, :], k[own, h, :, :], low[h], st["k"].free,
                                               sem=copy_sems[slot, h], turn=copy_turn[slot, h])
                side.free = [low]
            return rest

        def project_v(g, n):
            b, p = g
            st = state[g]
            for t in range(QT):
                m = pe.do(lambda e, t=t: e.matmul(
                    side.ap[:, t * P:(t + 1) * P], self.xt[:, b * SEQ + t * P:b * SEQ + (t + 1) * P],
                    w["wkv"][:, 1024 + p * P:1024 + (p + 1) * P], start=True, stop=True), side.free)
            self.xt_free[b] = m
            a = ac.do(lambda e: e.activation(st["v"].ap[:, 0:QT, :], side.ap.rearrange("p (t n) -> p t n", t=QT), ACT.Copy),
                      m, st["v"].free)
            side.free = [a]
            st["v_ready"].append(a)

        pieces = {0: project_q, 2: lambda g, n: project_k(g, 0), 4: lambda g, n: project_k(g, 1),
                  6: project_v}
        for s in sorted(pieces):
            rest = pieces[s](groups[0], 0)
            if rest:
                rest()

        def scores_of(u, h, j):
            g, half = u["group"], u["half"]
            st, slot, qt = state[g], scores.next(), 2 * half + j
            lhs = st["q"].ap[:, h, qt * P:(qt + 1) * P]
            k = st["k"].ap
            for a, z in ((0, SEQ), (SEQ, KEYS0)):
                for part in (0, 1):
                    m = pe.do(lambda e, a=a, z=z, part=part: e.matmul(slot.ap[:, a:z], lhs, k[:, h, part, a:z],
                                                                      start=part == 0, stop=part == 1),
                              slot.free, st["q0"], st["q1"], st[f"k{h}"])
            st.setdefault("scores", []).append(m)
            big, prob, col = neg_max.next(), probs.next(), 2 * j + h
            v = ve.do(lambda e: e.tensor_reduce(big.ap, slot.ap[:, 0:KEYS0], AX_X, ALU.max, negate=True), m, big.free)
            a = ac.do(lambda e: e.activation(prob.ap, slot.ap[:, 0:KEYS0], ACT.Exp, bias=big.ap,
                                             accum_out=u["sums"].ap[:, col:col + 1]), v, prob.free, u["sums"].free)
            big.free, slot.free = [a], [a]
            u.setdefault("exps", []).append(a)
            return prob, a

        def turn_probs(u, h, j, prob, ready):
            for n, (bank, tiles) in enumerate(zip(turned, (range(0, 4), range(4, KT0)))):
                for t in tiles:
                    rows = min(P, KEYS0 - t * P)
                    m = pe.do(lambda e, t=t, rows=rows, c=(t - tiles[0]) * P, bank=bank: e.transpose(
                        bank.ap[0:rows, c:c + P], prob.ap[:, t * P:t * P + rows], self.eye), ready, bank.free)
                out = u["probs"].ap[:, h, tiles[0]:tiles[-1] + 1, j * P:(j + 1) * P]
                src = bank.ap[:, 0:P * len(tiles)].rearrange("p (t n) -> p t n", t=len(tiles))
                if n == 0:
                    s = ac.do(lambda e, out=out, src=src: e.activation(out, src, ACT.Copy), m, u["probs"].free)
                else:
                    s = ve.do(lambda e, out=out, src=src: e.tensor_copy(out, src), m, u["probs"].free)
                bank.free = [s]
                u.setdefault("turned", []).append(s)
            prob.free = [m]

        def weigh(u, tiles):
            st = state[u["group"]]
            for t in tiles:
                rows = min(P, KEYS0 - t * P)
                for h in (0, 1):
                    m = pe.do(lambda e, t=t, rows=rows, h=h: e.matmul(
                        out_bank.ap[64 * h:64 * h + 64, 0:2 * P], st["v"].ap[0:rows, t, 64 * h:64 * h + 64],
                        u["probs"].ap[0:rows, h, t, :], start=t == 0, stop=t == KT0 - 1),
                        u["turned"], st["v_ready"], out_bank.free)
            if tiles[-1] == KT0 - 1:
                u["weighed"] = m
                u["probs"].free = [m]

        def invert(u):
            u["inverse"], u["spread"] = inverse.next(), spread.next()
            r, s = u["inverse"].ap, u["spread"].ap
            v = ve.do(lambda e: e.reciprocal(r, u["sums"].ap), u["exps"], u["inverse"].free)
            u["sums"].free = [v]
            by_head = r.rearrange("p (j h) -> p j h", j=2).unsqueeze(3).to_broadcast([P, 2, 2, D0])
            u["spread_done"] = po.do(lambda e: e.tensor_copy(s, by_head), v, u["spread"].free)
            u["inverse"].free = [u["spread_done"]]

        def scale_out(u):
            (b, p), half = u["group"], u["half"]
            for j in (0, 1):
                m = pe.do(lambda e, j=j: e.transpose(out_bank.ap[:, (2 + j) * P:(3 + j) * P],
                                                     u["spread"].ap[:, j, :, :].rearrange("p h d -> p (h d)"), self.eye),
                          u["spread_done"])
            u["spread"].free = [m]
            out = mixed[:, p, half * 2 * P:(half + 1) * 2 * P]
            a = ac.do(lambda e: e.activation(out, out_bank.ap[:, 2 * P:4 * P], ACT.Copy), m, mixed_free[half])
            s = ve.do(lambda e: e.tensor_tensor(out, out_bank.ap[:, 0:2 * P], out, ALU.mult), a)
            out_bank.free = [s]
            u["mixed"] = s
            if half == 1:
                st = state[u["group"]]
                st["q"].free = st["k"].free = list(st["scores"])
                st["v"].free = [u["weighed"]]

        def project_out(b, t, ready):
            for p in range(PAIRS):
                m = pe.do(lambda e, p=p: e.matmul(side.ap[:, 0:P], mixed[:, p, t * P:(t + 1) * P],
                                                  w["wo"][:, p * P:(p + 1) * P], start=p == 0, stop=p == PAIRS - 1),
                          ready, side.free)
            mixed_free[t // 2] = m
            side.free = [self.add_to_x(b * QT + t, side.ap[:, 0:P], 0, m)]
            if t == QT - 1:
                self.follow(b)

        units = [{"group": g, "half": half} for g in groups for half in (0, 1)]
        subs = [(u, h, j) for u in units for h in (0, 1) for j in (0, 1)]
        self.chores = [self.late_tables]
        for b in range(1, BATCH):
            rows = slice(QT * b, QT * b + QT)
            (once,), steps = self.norm_groups(x[:, rows, :], self.xn[:, rows, :], [self.load_x[b]] * QT, QT)
            (again,), done = self.norm_groups(self.xn[:, rows, :], self.xn[:, rows, :], steps, QT)
            self.chores += [*once, *again, lambda b=b, rows=rows, done=done: latents.extend(self.turn(
                self.xn[:, rows, :], self.xt[:, b * SEQ:(b + 1) * SEQ], done, n=QT, **ln2))]
        parts = [(0, 1), (2, 3), (4,), (5,)]
        waiting, rest = [], None
        splits = self.split_weights(1, ("w1", "w2"))
        for i in range(len(subs) + 15):
            if i < len(subs):
                u, h, j = subs[i]
                if i % 4 == 0:
                    u["sums"], u["probs"] = sums.next(), probs_t.next()
                waiting.append((u, h, j, *scores_of(u, h, j)))
            if rest:
                rest()
                rest = None
            back = (i - 3) // 4 - 1
            if 0 <= back < len(units):
                part = (i - 3) % 4
                if part == 0:
                    invert(units[back])
                weigh(units[back], parts[part])
                if part == 3:
                    scale_out(units[back])
            if i >= 2 and waiting:
                turn_probs(*waiting.pop(0))
            if i >= 4:
                self.chore()
            if i >= 64 and i % 4 == 3:
                next(splits, None)
            late = i - 8 * PAIRS - 7
            if late >= 0 and late % (8 * PAIRS) in (0, 2, 4, 6):
                b = late // (8 * PAIRS)
                own = units[2 * PAIRS * b:2 * PAIRS * (b + 1)]
                project_out(b, late % (8 * PAIRS) // 2, [v["mixed"] for v in own])
            if i // 8 + 1 < len(groups) and i % 8 in pieces:
                rest = pieces[i % 8](groups[i // 8 + 1], i // 8 + 1)
        for _ in splits:
            pass
        self.banks = Ring([self.psum[:, b * BANK:(b + 1) * BANK] for b in range(8)])
        for bank, last in zip(self.banks.slots, (scores.slots[0],) * 2 + (scores.slots[1],) * 2 + (*turned, out_bank, side)):
            bank.free = last.free

    def one_hot_of_max(self, values, down, n, *ready):
        ve = self.ve
        top, key, hot = self.carve(TILES), self.carve(TILES, n), self.carve(TILES, n)
        best = self.carve(TILES)
        wide = [P, TILES, n]
        places = down.unsqueeze(1).to_broadcast(wide)
        a = ve.do(lambda e: e.tensor_reduce(top, values, AX_X, ALU.max), *ready)
        b = ve.do(lambda e: e.tensor_tensor(hot, values, top.unsqueeze(2).to_broadcast(wide), ALU.is_equal), a)
        c = ve.do(lambda e: e.tensor_tensor(key, hot, places, ALU.mult), b)
        d = ve.do(lambda e: e.tensor_reduce(best, key, AX_X, ALU.max), c)
        f = ve.do(lambda e: e.tensor_tensor(hot, places, best.unsqueeze(2).to_broadcast(wide), ALU.is_equal), d)
        return hot, best, f

    def token_products(self, weights, n, ready, row, *others):
        bank = self.banks.next()
        out = self.carve(TILES, n)
        for t in range(TILES):
            m = self.pe.do(lambda e, t=t: e.matmul(bank.ap[:, t * n:(t + 1) * n], self.xt[:, t * P:(t + 1) * P], weights,
                                                   start=True, stop=True), ready[t], bank.free, *others)
        src = bank.ap[:, 0:TILES * n].rearrange("p (t n) -> p t n", t=TILES)
        if row is None:
            s = self.ve.do(lambda e: e.tensor_copy(out, src), m)
        else:
            s = self.ve.do(lambda e: e.tensor_tensor(out, src, row.unsqueeze(1).to_broadcast([P, TILES, n]), ALU.add), m)
        bank.free = [s]
        return out, s

    def turn_small(self, src, n, ready):
        out, steps = self.carve(TOKENS), []
        for b in range(BATCH):
            bank = self.banks.next()
            for j in range(QT):
                m = self.pe.do(lambda e, t=QT * b + j, j=j, bank=bank: e.transpose(
                    bank.ap[0:n, j * P:(j + 1) * P], src[:, t, :], self.eye), ready, bank.free)
            s = self.evacuate(out[0:n, b * SEQ:(b + 1) * SEQ], bank.ap[0:n, :], m)
            bank.free = [s]
            steps.append(s)
        return out, steps

    def top1_experts(self):
        pe, ve, ac = self.pe, self.ve, self.ac
        self.begin("experts")
        self.load_weights(7, self.before)
        w = self.w[1]
        _, turned = self.stream()
        hidden = Ring([self.carve(2, FT, SEQ, dt=BF16) for _ in range(2)])
        whole = Ring([self.carve(SEQ) for _ in range(3)])
        w1, w2, split_ready = self.split["w1"], self.split["w2"], self.split_ready
        xt = self.carve(2, TOKENS, dt=BF16)
        xt_ready = {}

        def split_stream(b):
            cols = slice(b * SEQ, (b + 1) * SEQ)
            s1 = ac.do(lambda e: e.activation(xt[:, 0, cols], self.xt[:, cols], ACT.Copy), turned[QT * b])
            xt_ready[b] = ve.do(lambda e: e.tensor_tensor(xt[:, 1, cols], self.xt[:, cols], xt[:, 0, cols], ALU.subtract), s1)

        def up(b, x):
            h, steps = hidden.next(), []
            for f in range(FT):
                bank, v = self.banks.next(), whole.next()
                at = x * FF + f * P
                m = self.products(bank.ap, lambda part: w1[:, at // BANK, part, at % BANK:at % BANK + P],
                                  lambda part: xt[:, part, b * SEQ:(b + 1) * SEQ], True, True,
                                  xt_ready[b], bank.free, split_ready)
                col = w["b1"][:, x * FT + f:x * FT + f + 1]
                s1 = ac.do(lambda e, f=f, bank=bank, col=col: e.activation(h.ap[:, 0, f, :], bank.ap, ACT.Relu, bias=col), m, h.free)
                s2 = ac.do(lambda e, v=v, bank=bank, col=col: e.activation(v.ap, bank.ap, ACT.Relu, bias=col), v.free)
                s3 = ve.do(lambda e, f=f, v=v: e.tensor_tensor(h.ap[:, 1, f, :], v.ap, h.ap[:, 0, f, :], ALU.subtract), s2, h.free)
                bank.free, v.free = [s2], [s3]
                steps.append(s3)
            self.xt_free[b] = [m, xt_ready[b]]
            return b, x, h, steps

        split_stream(0)
        waiting = [up(0, 0), up(0, 1)]
        self.do_chores()
        logits, s = self.token_products(w["gate"], EXPERTS, turned, self.row["L0_ffn_gate_b"], self.w_ready[1], self.rows_ready)
        s = ve.do(lambda e: e.tensor_tensor(logits, logits, self.row["L0_ffn_expert_bias"].unsqueeze(1)
                                            .to_broadcast([P, TILES, EXPERTS]), ALU.add), s)
        hot, _, s_hot = self.one_hot_of_max(logits, self.c["down8"], EXPERTS, s)
        hot_t, hot_t_ready = self.turn_small(hot, EXPERTS, s_hot)
        weight = self.carve(TILES, EXPERTS)
        s_weight = ve.do(lambda e: e.tensor_scalar(weight, hot, self.gates[:, 4:5], None, ALU.mult), s_hot)

        for b in range(BATCH):
            bank = self.banks.next()
            for j in range(QT):
                t = QT * b + j
                m = pe.do(lambda e, t=t, j=j, bank=bank: e.matmul(
                    bank.ap[:, j * P:(j + 1) * P], hot_t[0:EXPERTS, t * P:(t + 1) * P], self.small[:, 0:P],
                    start=True, stop=True), hot_t_ready[b], bank.free, self.rows_ready)
            bank.free = [self.add_to_x(QT * b + j, bank.ap[:, j * P:(j + 1) * P], 4, m) for j in range(QT)]

        def down(b, x, h, steps):
            bank = self.banks.next()
            for j in range(QT):
                for f in range(FT):
                    at = x * FF + f * P
                    m = self.products(bank.ap[:, j * P:(j + 1) * P], lambda part: h.ap[:, part, f, j * P:(j + 1) * P],
                                      lambda part: w2[:, at // BANK, part, at % BANK:at % BANK + P], f == 0, f == FT - 1,
                                      steps, bank.free)
            h.free = [m]
            bank.free = []
            for j in range(QT):
                t = QT * b + j
                self.x_last[t] = ve.do(lambda e, t=t, j=j: e.scalar_tensor_tensor(
                    self.x[:, t, :], bank.ap[:, j * P:(j + 1) * P], weight[:, t, x:x + 1], self.x[:, t, :],
                    ALU.mult, ALU.add), m, s_weight, self.x_last[t])
                bank.free.append(self.x_last[t])
            if x == EXPERTS - 1:
                self.follow(b)

        for b in range(BATCH):
            for x in range(EXPERTS):
                if (b, x) > (0, 1):
                    waiting.append(up(b, x))
                if x == EXPERTS // 2 and b + 1 < BATCH:
                    split_stream(b + 1)
                if (b, x) >= (0, 1):
                    down(*waiting.pop(0))
                self.chore()
        down(*waiting.pop(0))

    def one_head(self):
        pe, ve, ac = self.pe, self.ve, self.ac
        self.begin("onehead")
        self.load_weights(5, self.before)
        self.load_weights(6, self.before)
        w = self.w[2]
        _, turned = self.stream()
        k_t, k_ready = self.project_context(w["wk"], w["bk"], self.w_ready[2])
        q_t, q_ready = self.project(w["wq"], w["bq"], self.xt, turned)
        self.xt_free = [q_ready[QT * b] for b in range(BATCH)]
        v, v_ready = self.carve(2 * BATCH, P), []
        for b in range(BATCH):
            bank = self.banks.next()
            for n, rows in ((0, P), (1, CTX_REST)):
                m = pe.do(lambda e, b=b, n=n, rows=rows, bank=bank: e.matmul(
                    bank.ap[0:rows, n * P:(n + 1) * P], self.context[:, b, n * P:n * P + rows], w["wv"],
                    start=True, stop=True), bank.free, self.context_ready)
            s = [ve.do(lambda e, b=b, n=n, rows=rows, bank=bank: e.tensor_copy(
                v[0:rows, 2 * b + n, :], bank.ap[0:rows, n * P:(n + 1) * P]), m) for n, rows in ((0, P), (1, CTX_REST))]
            bank.free = s
            v_ready.append(s)
        probs = Ring([self.carve(QT, CTX) for _ in range(2)])
        probs_t = Ring([self.carve(2, SEQ) for _ in range(2)])
        small = [(self.carve(QT), self.carve(QT), self.carve(QT)) for _ in range(BATCH)]

        def scores_of(b):
            neg, total, inv = small[b]
            prob, exps = probs.next(), []
            for g, tiles in enumerate(((0, 1), (2, 3))):
                bank = self.banks.next()
                for n, t in enumerate(tiles):
                    m = pe.do(lambda e, n=n, t=t, bank=bank: e.matmul(
                        bank.ap[:, n * CTX:(n + 1) * CTX], q_t[:, (QT * b + t) * P:(QT * b + t + 1) * P],
                        k_t[:, b * CTX:(b + 1) * CTX], start=True, stop=True), q_ready[QT * b + t], k_ready, bank.free)
                src = bank.ap[:, 0:2 * CTX].rearrange("p (t k) -> p t k", t=2)
                s = ve.do(lambda e, g=g, src=src: e.tensor_reduce(neg[:, 2 * g:2 * g + 2], src, AX_X, ALU.max, negate=True), m)
                bank.free = []
                for n, t in enumerate(tiles):
                    a = ac.do(lambda e, n=n, t=t, src=src: e.activation(prob.ap[:, t, :], src[:, n, :], ACT.Exp, bias=neg[:, t:t + 1],
                                                                        accum_out=total[:, t:t + 1]), s, prob.free)
                    bank.free.append(a)
                exps += bank.free
            r = ve.do(lambda e: e.reciprocal(inv, total), exps)
            return b, prob, exps, inv, r

        def weigh(b, prob, exps, inv, r):
            pt, steps = probs_t.next(), []
            for n, rows in ((0, P), (1, CTX_REST)):
                bank = self.banks.next()
                for t in range(QT):
                    m = pe.do(lambda e, n=n, t=t, rows=rows, bank=bank: e.transpose(
                        bank.ap[0:rows, t * P:(t + 1) * P], prob.ap[:, t, n * P:n * P + rows], self.eye), exps, bank.free)
                s = self.evacuate(pt.ap[0:rows, n, :], bank.ap[0:rows, :], m, pt.free)
                bank.free = [s]
                steps.append(s)
            prob.free = [m]
            bank = self.banks.next()
            for t in range(QT):
                for n, rows in ((0, P), (1, CTX_REST)):
                    m = pe.do(lambda e, n=n, t=t, rows=rows: e.matmul(
                        bank.ap[:, t * P:(t + 1) * P], pt.ap[0:rows, n, t * P:(t + 1) * P], v[0:rows, 2 * b + n, :],
                        start=n == 0, stop=n == 1), steps, v_ready[b], bank.free)
            pt.free = [m]
            bank.free = [self.add_to_x(QT * b + t, bank.ap[:, t * P:(t + 1) * P], 1, [m, r], row=self.row["L1_xattn_bv"],
                                       factor=inv[:, t:t + 1]) for t in range(QT)]
            self.follow(b)

        waiting = None
        for b in range(BATCH):
            now = scores_of(b)
            if waiting:
                weigh(*waiting)
                self.do_chores(keep=4)
                self.chore()
                self.chore()
            waiting = now
        weigh(*waiting)

    def project(self, weights, bias, src, ready, *others, scale=None, out=None):
        out = self.carve(TOKENS) if out is None else out
        steps = []
        for b in range(BATCH):
            if b == BATCH - 1:
                self.do_chores()
            bank = self.banks.next()
            m = self.pe.do(lambda e, b=b, bank=bank: e.matmul(bank.ap, weights, src[:, b * SEQ:(b + 1) * SEQ], start=True, stop=True),
                           ready[QT * b:QT * b + QT], bank.free, *others)
            o = out[:, b * SEQ:(b + 1) * SEQ]
            if scale is None and b % 2:
                s = self.ac.do(lambda e, o=o, bank=bank: e.activation(o, bank.ap, ACT.Identity, bias=bias), m)
            else:
                s = self.ve.do(lambda e, o=o, bank=bank: e.tensor_scalar(o, bank.ap, bias, 1.0 if scale is None else scale,
                                                                         ALU.add, ALU.mult), m)
            bank.free = [s]
            steps += [s] * QT
        return out, steps

    def project_context(self, weights, bias, *others):
        out, steps = self.carve(CTX_ROWS), []
        for b in range(0, BATCH, 2):
            bank = self.banks.next()
            for n in (0, 1):
                m = self.pe.do(lambda e, b=b, n=n, bank=bank: e.matmul(
                    bank.ap[:, n * CTX:(n + 1) * CTX], weights, self.context[:, b + n, 0:CTX], start=True, stop=True),
                    self.context_ready, bank.free, *others)
            s = self.ac.do(lambda e, b=b, bank=bank: e.activation(out[:, b * CTX:(b + 2) * CTX], bank.ap[:, 0:2 * CTX],
                                                                  ACT.Identity, bias=bias), m)
            bank.free = [s]
            steps.append(s)
        return out, steps

    def batch_attention(self):
        pe, ve, ac, po = self.pe, self.ve, self.ac, self.po
        self.begin("batch")
        w, y = self.w[3], self.xn
        heads, d = 16, 8
        _, turned = self.stream()
        qkv, qkv_ready = self.carve(TILES, 3 * P), []
        for t in range(TILES):
            if t == TILES - QT:
                self.do_chores()
            bank = self.banks.next()
            m = pe.do(lambda e, t=t, bank=bank: e.matmul(bank.ap[:, 0:3 * P], self.xt[:, t * P:(t + 1) * P], w["in"],
                                                         start=True, stop=True), turned[t], bank.free, self.w_ready[3])
            s = ve.do(lambda e, t=t, bank=bank: e.tensor_tensor(qkv[:, t, :], bank.ap[:, 0:3 * P],
                                                                self.row["L1_ffn_in_proj_b"], ALU.add), m, self.rows_ready)
            bank.free = [s]
            qkv_ready.append(s)
        part = lambda n: qkv[:, :, n * P:(n + 1) * P]
        pairs = [P, BATCH, QT, P]
        places = QT * heads
        product = [self.carve(BATCH * QT, P) for _ in range(2)]
        product_free = [None, None]
        score = self.carve(BATCH, BATCH, places)
        done = []
        for t in range(BATCH):
            o, slot = product[t % 2], t % 2
            a = ve.do(lambda e, t=t, o=o: e.tensor_tensor(
                o.rearrange("p (s j) c -> p s j c", s=BATCH), part(0)[:, QT * t:QT * t + QT, :].unsqueeze(1).to_broadcast(pairs),
                part(1).rearrange("p (s j) c -> p s j c", s=BATCH), ALU.mult), qkv_ready, product_free[slot])
            b = ve.do(lambda e, t=t, o=o: e.tensor_reduce(
                score[:, t, :, :].rearrange("p s c -> p (s c)"), o.rearrange("p s (h d) -> p (s h) d", d=d), AX_X, ALU.add), a)
            product_free[slot] = b
            done.append(b)
        by_key = score.rearrange("p t s c -> p t c s")
        most, total = self.carve(BATCH, places), self.carve(BATCH, places)
        over = lambda v: v.unsqueeze(2).to_broadcast([P, BATCH, BATCH, places])
        s = ve.do(lambda e: e.tensor_reduce(most, by_key, AX_X, ALU.max), done)
        s = ve.do(lambda e: e.tensor_tensor(score, score, over(most), ALU.subtract), s)
        s = ac.do(lambda e: e.activation(score, score, ACT.Exp, scale=d ** -0.5), s)
        s = ve.do(lambda e: e.tensor_reduce(total, by_key, AX_X, ALU.add), s)
        s = ve.do(lambda e: e.reciprocal(total, total), s)
        s = ve.do(lambda e: e.tensor_tensor(score, score, over(total), ALU.mult), s)
        mixed = self.carve(TILES, P)
        mixed_ready = []
        for t in range(BATCH):
            o, slot = product[t % 2], t % 2
            a = ve.do(lambda e, t=t, o=o: e.tensor_tensor(
                o.rearrange("p s (h d) -> p s h d", d=d),
                score[:, t, :, :].rearrange("p s (j h) -> p (s j) h", j=QT).unsqueeze(3).to_broadcast([P, TILES, heads, d]),
                part(2).rearrange("p s (h d) -> p s h d", d=d), ALU.mult), s, product_free[slot])
            b = ve.do(lambda e, t=t, o=o: e.tensor_reduce(
                mixed[:, QT * t:QT * t + QT, :].rearrange("p j c -> p (j c)"),
                o.rearrange("p (s j) c -> p (j c) s", s=BATCH), AX_X, ALU.add), a)
            product_free[slot] = b
            mixed_ready += [b] * QT
        turned = self.turn(mixed, self.xt, mixed_ready, after=(qkv_ready,))
        h = self.token_layer([(self.xt, w["out"])], turned, self.row["L1_ffn_out_b"], y)
        ready = self.normalize(y, y, h, gain=self.row["L1_ffn_ln1_g"], bias=self.row["L1_ffn_ln1_b"])
        turned = self.turn(y, self.xt, ready)

        probs, s = self.token_products(w["router"], EXPERTS, turned, self.row["L1_ffn_router_b"])
        wide = [P, TILES, EXPERTS]
        top, mass = self.carve(TILES), self.carve(TILES)
        s = ve.do(lambda e: e.tensor_reduce(top, probs, AX_X, ALU.max), s)
        s = ve.do(lambda e: e.tensor_tensor(probs, probs, top.unsqueeze(2).to_broadcast(wide), ALU.subtract), s)
        s = ac.do(lambda e: e.activation(probs, probs, ACT.Exp), s)
        s = ve.do(lambda e: e.tensor_reduce(mass, probs, AX_X, ALU.add), s)
        s = ve.do(lambda e: e.reciprocal(mass, mass), s)
        s = ve.do(lambda e: e.tensor_tensor(probs, probs, mass.unsqueeze(2).to_broadcast(wide), ALU.mult), s)
        hot1, key1, s = self.one_hot_of_max(probs, self.c["down8"], EXPERTS, s)
        s = ve.do(lambda e: e.scalar_tensor_tensor(probs, hot1, -4.0, probs, ALU.mult, ALU.add), s)
        hot2, key2, s = self.one_hot_of_max(probs, self.c["down8"], EXPERTS, s)
        s = ve.do(lambda e: e.tensor_tensor(key1, key1, key2, ALU.min), s)
        hot = hot1
        s_hot = ve.do(lambda e: e.tensor_tensor(hot, self.c["down8"].unsqueeze(1).to_broadcast(wide),
                                                key1.unsqueeze(2).to_broadcast(wide), ALU.is_equal), s)
        hot_t, hot_t_ready = self.turn_small(hot, EXPERTS, s_hot)
        last = list(ready)
        for b in range(BATCH):
            bank = self.banks.next()
            for j in range(QT):
                t = QT * b + j
                m = pe.do(lambda e, t=t, j=j, bank=bank: e.matmul(
                    bank.ap[:, j * P:(j + 1) * P], hot_t[0:EXPERTS, t * P:(t + 1) * P], self.small[:, P:2 * P],
                    start=True, stop=True), hot_t_ready[b], bank.free)
            o = y[:, QT * b:QT * b + QT, :]
            s = ve.do(lambda e, o=o, bank=bank: e.tensor_tensor(o, o, bank.ap.rearrange("p (t n) -> p t n", t=QT), ALU.add),
                      m, turned)
            bank.free = [s]
            for j in range(QT):
                last[QT * b + j] = s

        hidden = Ring([self.carve(SEQ) for _ in range(3)])

        def up(b, x):
            bank, g = self.banks.next(), hidden.next()
            m = pe.do(lambda e: e.matmul(bank.ap, w["w1"][:, x * P:(x + 1) * P], self.xt[:, b * SEQ:(b + 1) * SEQ],
                                         start=True, stop=True), bank.free)
            s = ac.do(lambda e: e.activation(g.ap, bank.ap, ACT.Gelu, bias=w["b1"][:, x:x + 1]), m, g.free)
            bank.free = [s]
            return b, x, g, s

        def down(b, x, g, ready):
            bank = self.banks.next()
            for j in range(QT):
                m = pe.do(lambda e, j=j: e.matmul(bank.ap[:, j * P:(j + 1) * P], g.ap[:, j * P:(j + 1) * P],
                                                  w["w2"][:, x * P:(x + 1) * P], start=True, stop=True), ready, bank.free)
            g.free, bank.free = [m], []
            for j in range(QT):
                t = QT * b + j
                last[t] = ve.do(lambda e, t=t, j=j: e.scalar_tensor_tensor(
                    y[:, t, :], bank.ap[:, j * P:(j + 1) * P], hot[:, t, x:x + 1], y[:, t, :], ALU.mult, ALU.add), m, last[t])
                bank.free.append(last[t])

        def close(b):
            rows = slice(QT * b, QT * b + QT)
            ((measure, scale),), done = self.norm_groups(y[:, rows, :], y[:, rows, :], last[rows], QT,
                                                         gain=self.row["L1_ffn_ln2_g"], bias=self.row["L1_ffn_ln2_b"],
                                                         room=self.room[:, 2 * BATCH + b, :])

            def update():
                self.xn_free[b] = self.add_batch_to_x(b, y, 5, done)
                self.follow(b)

            self.chores += [measure, scale, update]

        waiting = []
        splits = self.split_weights(5, ("w1", "w2", "h1", "h2", "w3"), scalar=True)
        for b in range(BATCH):
            for x in range(EXPERTS):
                next(splits, None)
                waiting.append(up(b, x))
                if x == EXPERTS - 1:
                    self.xt_free[b] = waiting[-1][-1]
                if len(waiting) > 2:
                    old = waiting.pop(0)
                    down(*old)
                    if old[1] == EXPERTS - 1:
                        close(old[0])
                self.chore()
        for rest in waiting:
            down(*rest)
        close(BATCH - 1)

    def token_layer(self, parts, ready, row, into):
        out = []
        for b in range(BATCH):
            bank = self.banks.next()
            for j in range(QT):
                t = QT * b + j
                for n, (src, weights) in enumerate(parts):
                    m = self.pe.do(lambda e, t=t, j=j, n=n, src=src, weights=weights, bank=bank: e.matmul(
                        bank.ap[:, j * P:(j + 1) * P], src[:, t * P:(t + 1) * P], weights,
                        start=n == 0, stop=n == len(parts) - 1), ready[t], bank.free)
            o = into[:, QT * b:QT * b + QT, :]
            src = bank.ap.rearrange("p (t n) -> p t n", t=QT)
            s1 = self.ve.do(lambda e, o=o, src=src: e.tensor_tensor(o, src, o, ALU.add), m)
            bank.free = [s1]
            s2 = self.ve.do(lambda e, o=o: e.tensor_tensor(o, o, row.unsqueeze(1).to_broadcast([P, QT, P]), ALU.add), s1)
            out += [s2] * QT
        return out

    def context_attention(self, heads, ready, loaded, wq, bq, wk, bk, wv, bv, masked=None, finish=None):
        pe, ve, ac, po = self.pe, self.ve, self.ac, self.po
        d = P // heads
        chunks = flat_chunks(heads)
        of_group = heads // GROUPS
        head_of = self.c[f"head{heads}"]
        block = self.c[f"block{heads}"].rearrange("p (c h) -> p c h", h=of_group)
        keys = Ring([self.carve(heads, CTX, dt=BF16) for _ in range(2)])
        values = Ring([self.carve(GROUPS * len(chunks), WIDE) for _ in range(2)])
        probs = Ring([self.carve(heads * CTX) for _ in range(2)])
        probs_t = Ring([self.carve(GROUPS * len(chunks), 2 * P)])
        small = Ring([self.carve(heads) for _ in range(6)])
        spread = Ring([self.carve(heads, d) for _ in range(2)])
        factor = Ring([self.carve(2 * P) for _ in range(2)])
        mixed = Ring([self.carve(2 * P) for _ in range(2)])
        operands = {}
        four, four_ready = {}, []
        for name, weights in (("k", wk), ("q", wq)):
            four[name] = self.carve(GROUPS, P)
            four_ready.append(ac.do(lambda e, out=four[name], weights=weights: e.activation(
                out.rearrange("p g (r d) -> p g r d", r=4),
                weights.rearrange("p (g d) -> p g d", g=GROUPS).unsqueeze(2).to_broadcast([P, GROUPS, 4, WIDE]), ACT.Copy), loaded))

        k4, k_ready = self.carve(GROUPS, CTX_ROWS, dt=BF16), []
        exact = Ring([self.carve(CTX_ROWS) for _ in range(2)])
        for g in range(GROUPS):
            v, part = exact.next(), []
            for n in (0, 1):
                bank = self.banks.next()
                for c in (0, 1):
                    m = pe.do(lambda e, g=g, n=n, c=c, bank=bank: e.matmul(
                        bank.ap[:, c * CTX:(c + 1) * CTX], four["k"][:, g, :], self.context[:, 2 * n + c, 0:CTX], start=True, stop=True),
                        bank.free, self.context_ready, four_ready)
                part.append(ac.do(lambda e, g=g, n=n, bank=bank, v=v: e.activation(
                    v.ap[:, 2 * n * CTX:2 * (n + 1) * CTX], bank.ap[:, 0:2 * CTX], ACT.Identity, bias=bk[:, g:g + 1]), m, v.free))
                bank.free = [part[-1]]
            s = ac.do(lambda e, g=g, v=v: e.activation(k4[:, g, :], v.ap, ACT.Copy), part)
            v.free = [ve.do(lambda e, g=g, v=v, o=slice(o, o + WIDE): e.tensor_tensor(
                k4[o, g, :], v.ap[o, :], k4[o, g, :], ALU.subtract), s) for o in (WIDE, 2 * WIDE)]
            k_ready += v.free

        q4 = Ring([self.carve(GROUPS, SEQ, dt=BF16) for _ in range(2)])
        q_of = {}

        def queries(b):
            cols, steps, q = slice(b * SEQ, (b + 1) * SEQ), [], q4.next()
            q_of[b] = (q, steps)

            def group(g):
                bank, v = self.banks.next(), exact.next()
                m = pe.do(lambda e, g=g, bank=bank: e.matmul(bank.ap, four["q"][:, g, :], self.xt[:, cols], start=True, stop=True),
                          ready[QT * b:QT * b + QT], bank.free)
                s1 = ve.do(lambda e, g=g, bank=bank, v=v: e.tensor_scalar(v.ap[:, 0:SEQ], bank.ap, bq[:, g:g + 1], d ** -0.5, ALU.add, ALU.mult),
                           m, v.free)
                bank.free = [s1]
                if b == 0:
                    s2 = ac.do(lambda e: e.activation(q.ap[:, g, :], v.ap[:, 0:SEQ], ACT.Copy), s1, q.free)
                else:
                    s2 = ve.do(lambda e: e.tensor_copy(q.ap[:, g, :], v.ap[:, 0:SEQ]), s1, q.free)
                s3 = ve.do(lambda e, g=g, v=v: e.tensor_tensor(q.ap[64:P, g, :], v.ap[64:P, 0:SEQ], q.ap[64:P, g, :], ALU.subtract), s2)
                v.free = [s3]
                steps.append(s3)
                self.xt_free[b] = m

            return [lambda g=g: group(g) for g in range(GROUPS)]

        def prepare(b):
            k = keys.next()
            ks = [(ve if b == 0 and g < 2 else po).do(lambda e, g=g: e.tensor_tensor(
                k.ap[:, g * of_group:(g + 1) * of_group, :],
                k4[:, g, b * CTX:(b + 1) * CTX].unsqueeze(1).to_broadcast([P, of_group, CTX]),
                head_of.unsqueeze(2).to_broadcast([P, of_group, CTX]), ALU.mult), k_ready, k.free) for g in range(GROUPS)]
            v, steps = values.next(), []
            full = GROUPS * sum(rows == P for _, rows in chunks)
            last = chunks[-1][1]
            for c0, c1, rows in ((0, full, P), (full, full + GROUPS, last)):
                bank = self.banks.next()
                for c in range(c0, c1, GROUPS):
                    f0 = chunks[c // GROUPS][0] % CTX
                    m = pe.do(lambda e, c=c - c0, f0=f0, rows=rows, bank=bank: e.matmul(
                        bank.ap[0:rows, c * WIDE:c * WIDE + P], self.context[:, b, f0:f0 + rows], wv, start=True, stop=True),
                        bank.free, self.context_ready)
                step = ve.do(lambda e, c0=c0, c1=c1, rows=rows, bank=bank: e.tensor_tensor(
                    v.ap[0:rows, c0:c1, :].rearrange("p c (h d) -> p c h d", h=of_group),
                    bank.ap[0:rows, 0:(c1 - c0) * WIDE].rearrange("p (c h d) -> p c h d", c=c1 - c0, h=of_group),
                    block[0:rows, c0:c1, :].unsqueeze(3).to_broadcast([rows, c1 - c0, of_group, d]), ALU.mult), m, v.free)
                bank.free = [step]
                steps.append(step)
            operands[b] = (k, ks, v, steps)

        def scores_of(b, t, pieces):
            k, ks, _, _ = operands[b]
            (q, q_steps), tile, prob = q_of[b], QT * b + t, probs.next()
            neg, total, exps, count = small.next(), small.next(), [], len(pieces)
            for h0 in range(0, heads, 2):
                n, g = 2, h0 // of_group
                bank = self.banks.next()
                src = bank.ap[:, 0:n * CTX]
                m = pe.do(lambda e, g=g, h0=h0, n=n, src=src: e.matmul(
                    src, q.ap[:, g, t * P:(t + 1) * P], k.ap[:, h0:h0 + n, :].rearrange("p h k -> p (h k)"),
                    start=True, stop=masked is None), q_steps, ks[g], bank.free)
                if masked is not None:
                    m = pe.do(lambda e, n=n, src=src: e.matmul(
                        src.rearrange("p (h k) -> p h k", h=n), self.cb["eye_b"], masked[0][b][0][:, t, :].unsqueeze(1).to_broadcast([P, n, CTX]),
                        start=False, stop=True), masked[0][b][1])
                s = ve.do(lambda e, h0=h0, n=n, src=src: e.tensor_reduce(
                    neg.ap[:, h0:h0 + n], src.rearrange("p (h k) -> p h k", h=n), AX_X, ALU.max, negate=True), m, neg.free)
                bank.free = []
                for h in range(h0, h0 + n):
                    a = ac.do(lambda e, h=h, h0=h0, src=src: e.activation(
                        prob.ap[:, h * CTX:(h + 1) * CTX], src[:, (h - h0) * CTX:(h - h0 + 1) * CTX], ACT.Exp,
                        bias=neg.ap[:, h:h + 1], accum_out=total.ap[:, h:h + 1]), s, prob.free, total.free)
                exps.append(a)
                bank.free = [a]
                while pieces and len(pieces) * heads > count * (heads - h0 - 2):
                    pieces.pop(0)()
            k.free = q.free = [m]
            if masked is not None:
                self.xn_free[b] = m
            neg.free = [a]
            r = ve.do(lambda e: e.reciprocal(total.ap, total.ap), exps)
            sp = spread.next()
            wide = po.do(lambda e: e.tensor_copy(sp.ap, total.ap.unsqueeze(2).to_broadcast([P, heads, d])), r, sp.free)
            total.free = [wide]
            return b, t, prob, exps, sp, wide

        unit = {}

        def turn_probs(b, t, prob, exps, sp, wide):
            j, first, last = t % 2, [], []
            if j == 0:
                if unit:
                    first = [lambda old=dict(unit): weigh(**old)]
                    last = [lambda: unit["finish"]()]
                unit.update(pt=probs_t.next(), steps=[], factor=factor.next(), factor_steps=[], b=b, half=t // 2)
            pt = unit["pt"]

            def turn(c, f0, rows):
                bank = self.banks.next()
                for g in range(GROUPS):
                    at = g * of_group * CTX + f0
                    m = pe.do(lambda e, g=g, at=at, rows=rows, bank=bank: e.transpose(
                        bank.ap[0:rows, g * P:(g + 1) * P], prob.ap[:, at:at + rows], self.eye), exps, bank.free)
                o = pt.ap[0:rows, GROUPS * c:GROUPS * (c + 1), j * P:(j + 1) * P]
                i = bank.ap[0:rows, :].rearrange("p (g q) -> p g q", g=GROUPS)
                if c in (1, 3) if heads == 16 else c != 1:
                    s = ac.do(lambda e: e.activation(o, i, ACT.Copy), m, pt.free)
                else:
                    s = ve.do(lambda e: e.tensor_copy(o, i), m, pt.free)
                bank.free = [s]
                unit["steps"].append(s)
                if c == len(chunks) - 1:
                    prob.free = [m]

            def turn_factor():
                bank, f = self.banks.next(), unit["factor"]
                m = pe.do(lambda e: e.transpose(bank.ap[:, 0:P], sp.ap.rearrange("p h d -> p (h d)"), self.eye), wide, bank.free)
                sp.free = [m]
                s = ac.do(lambda e: e.activation(f.ap[:, j * P:(j + 1) * P], bank.ap[:, 0:P], ACT.Copy), m, f.free)
                bank.free = [s]
                unit["factor_steps"].append(s)

            turns = [lambda c=c, f0=f0, rows=rows: turn(c, f0, rows) for c, (f0, rows) in enumerate(chunks)]
            return first + turns[:2] + last + turns[2:] + [turn_factor]

        def weigh(b, half, pt, steps, factor, factor_steps, **_):
            _, _, v, v_ready = operands[b]
            bank, f = self.banks.next(), factor
            for c, (_, rows) in enumerate(chunks):
                for g in range(GROUPS):
                    m = pe.do(lambda e, c=GROUPS * c + g, g=g, rows=rows, first=c == 0, last=c == len(chunks) - 1: e.matmul(
                        bank.ap[WIDE * g:WIDE * (g + 1), 0:2 * P], v.ap[0:rows, c, :], pt.ap[0:rows, c, :],
                        start=first, stop=last), steps, v_ready, bank.free)
            pt.free, v.free = [m], [m]
            o = mixed.next()
            s = ve.do(lambda e: e.tensor_tensor(o.ap, bank.ap[:, 0:2 * P], f.ap, ALU.mult), m, factor_steps, o.free)
            bank.free, f.free = [s], [s]
            s = ve.do(lambda e: e.tensor_scalar(o.ap, o.ap, bv, None, ALU.add), s)
            unit["finish"] = lambda: finish(b, half, o, s)

        pieces = []
        prepare(0)
        for piece in queries(0):
            piece()
        for b in range(BATCH):
            for t in range(QT):
                pieces = turn_probs(*scores_of(b, t, pieces))
                if b == 0 and t == 0:
                    self.do_chores()
                    if masked is not None:
                        masked[1](BATCH - 1)
                if t == 1 and b + 1 < BATCH:
                    prepare(b + 1)
                    extra = queries(b + 1)
                if t in (1, 2) and b + 1 < BATCH:
                    pieces[-1:-1] = [extra.pop(0)]
                    pieces[2:2] = [extra.pop(0)]
                self.chore()
        for piece in pieces:
            piece()
        weigh(**unit)
        unit["finish"]()

    def masked_attention(self):
        pe, ve = self.pe, self.ve
        self.begin("masked")
        w, heads = self.w[4], 16
        _, turned = self.stream()
        halves = self.xn[:, :, :].rearrange("p (b t) d -> p b (t d)", b=BATCH).bitcast(BF16)
        masks = {}

        def load_mask(b):
            wide = QT * CTX
            mask = halves[:, b, 0:wide].rearrange("p (t k) -> p t k", t=QT)
            raw = halves[:, b, wide:wide + wide // 2].bitcast(U8).rearrange("p (t k) -> p t k", t=QT)
            load = self.dma(f"mask{b}", raw, self.dram["mask"][b * SEQ:(b + 1) * SEQ, :].rearrange("(t p) k -> p t k", p=P),
                            turned[QT * b])
            masks[b] = mask, self.po.do(lambda e: e.tensor_scalar(mask, raw, MASKED, None, ALU.mult), load)

        for b in range(BATCH - 1):
            load_mask(b)

        def finish(b, half, o, ready):
            bank = self.banks.next()
            for j in (0, 1):
                m = pe.do(lambda e, j=j: e.matmul(bank.ap[:, j * P:(j + 1) * P], o.ap[:, j * P:(j + 1) * P], w["wo"],
                                                  start=True, stop=True), ready, bank.free)
            o.free = [m]
            bank.free = [self.add_to_x(QT * b + 2 * half + j, bank.ap[:, j * P:(j + 1) * P], 2, m, row=self.row["L2_xattn_bo"])
                         for j in (0, 1)]
            if half == 1:
                self.follow(b)

        self.context_attention(heads, turned, self.w_ready[4], w["wq"], w["bq"], w["wk"], w["bk"], w["wv"], w["bv"], (masks, load_mask), finish)

    def scaled_feed_forward(self):
        pe, ve, ac = self.pe, self.ve, self.ac
        self.begin("scaled")
        w = self.w[5]
        _, turned = self.stream()
        self.xn_free = [None] * BATCH
        split = self.split
        xt = self.carve(2, TOKENS, dt=BF16)
        gated = self.carve(BATCH, 2 * FT, SEQ, dt=BF16).rearrange("p b (s f) t -> p b s f t", s=2)
        silu = Ring([self.carve(SEQ) for _ in range(3)])
        whole = Ring([self.carve(SEQ) for _ in range(2)])
        hidden = [Ring([self.carve(2, FT, SEQ, dt=BF16) for _ in range(2)]) for _ in range(2)]

        def in_parts(v, high, low, ready, *free, scalar=False):
            if scalar:
                s = ac.do(lambda e: e.activation(high, v, ACT.Copy), ready, *free)
            else:
                s = ve.do(lambda e: e.tensor_copy(high, v), ready, *free)
            return ve.do(lambda e: e.tensor_tensor(low, v, high, ALU.subtract), s)

        xt_steps = {}

        def split_stream(b):
            cols = slice(b * SEQ, (b + 1) * SEQ)
            xt_steps[b] = in_parts(self.xt[:, cols], xt[:, 0, cols], xt[:, 1, cols], turned[QT * b])

        router = self.prepare_router()
        next(router)
        split_stream(0)
        gated_ready = []
        for b in range(BATCH):
            cols, steps, xt_ready = slice(b * SEQ, (b + 1) * SEQ), [], xt_steps[b]
            for f in range(FT):
                if f == 1 and b + 1 < BATCH:
                    if b + 1 == BATCH - 1:
                        self.do_chores()
                    split_stream(b + 1)
                bank_a, bank_g, s, v = self.banks.next(), self.banks.next(), silu.next(), whole.next()
                for bank, name in ((bank_a, "w1"), (bank_g, "w2")):
                    m = self.products(bank.ap, lambda part: split[name][:, 0, part, f * P:(f + 1) * P],
                                      lambda part: xt[:, part, cols], True, True, xt_ready, bank.free, self.split_ready)
                a = ac.do(lambda e, f=f, bank=bank_a, s=s: e.activation(s.ap, bank.ap, ACT.Silu, scale=w["s1"][:, f:f + 1]), m, s.free)
                g = ve.do(lambda e, f=f, bank=bank_g, s=s, v=v: e.scalar_tensor_tensor(
                    v.ap, bank.ap, w["s2"][:, f:f + 1], s.ap, ALU.mult, ALU.mult), a, v.free)
                bank_a.free, bank_g.free, s.free = [a], [g], [g]
                v.free = [in_parts(v.ap, gated[:, b, 0, f, :], gated[:, b, 1, f, :], g, scalar=True)]
                steps += v.free
            gated_ready.append(steps)
            self.xt_free[b] = xt_ready

        def layer(src, ready, weights, scales, ring):
            out, steps = ring.next(), []
            for o in range(FT):
                bank, v = self.banks.next(), whole.next()
                for i in range(FT):
                    m = self.products(bank.ap, lambda part: weights[:, i, part, o * P:(o + 1) * P], lambda part: src[:, part, i, :],
                                      i == 0, i == FT - 1, ready, bank.free)
                s = ac.do(lambda e, o=o, bank=bank, v=v: e.activation(v.ap, bank.ap, ACT.Gelu, scale=scales[:, o:o + 1]), m, v.free)
                bank.free = [s]
                v.free = [in_parts(v.ap, out.ap[:, 0, o, :], out.ap[:, 1, o, :], s, out.free)]
                steps += v.free
            return out, steps, m

        def last(b, h, ready):
            bank = self.banks.next()
            for j in range(QT):
                for i in range(FT):
                    m = self.products(bank.ap[:, j * P:(j + 1) * P], lambda part: h.ap[:, part, i, j * P:(j + 1) * P],
                                      lambda part: split["w3"][:, 0, part, i * P:(i + 1) * P], i == 0, i == FT - 1, ready, bank.free)
            h.free = [m]
            bank.free = [self.add_to_x(QT * b + j, bank.ap[:, j * P:(j + 1) * P], 6, m, row=self.row["L2_ffn_w3_s"], op=ALU.mult)
                         for j in range(QT)]
            self.follow(b)

        next(router, None)

        first, second = {}, {}
        for b in range(BATCH + 2):
            if b < BATCH:
                first[b] = layer(gated[:, b, :, :, :], gated_ready[b], split["h1"], w["sh1"], hidden[0])
            if 0 <= b - 1 < BATCH:
                h, ready, _ = first[b - 1]
                second[b - 1] = layer(h.ap, ready, split["h2"], w["sh2"], hidden[1])
                h.free = [second[b - 1][2]]
            if 0 <= b - 2 < BATCH:
                last(b - 2, second[b - 2][0], second[b - 2][1])
                self.do_chores(keep=4)
                self.chore()
                self.chore()

    def decoder_block(self):
        pe, ve, ac = self.pe, self.ve, self.ac
        self.begin("decoder")
        w, y, heads = self.w[6], self.xn, 8
        d = P // heads
        _, turned = self.stream()
        values = self.carve(TILES, P)
        qkv = Ring([self.carve(3 * P) for _ in range(3)])
        junk = Ring([self.carve(P) for _ in range(2)])
        score, delta = self.carve(TILES), self.carve(TILES)
        steps, kept = [], []
        for t in range(TILES):
            if t == TILES - QT:
                self.do_chores()
            bank, q = self.banks.next(), qkv.next()
            m = pe.do(lambda e, t=t, bank=bank: e.matmul(bank.ap[:, 0:3 * P], self.xt[:, t * P:(t + 1) * P], w["qkv"],
                                                         start=True, stop=True), turned[t], bank.free, self.w_ready[6])
            s1 = ve.do(lambda e, q=q, bank=bank: e.tensor_tensor(q.ap[:, 0:2 * P], bank.ap[:, 0:2 * P],
                                                                 self.row["L3_xattn_qkv_b"][:, 0:2 * P], ALU.add), m, q.free)
            s2 = ve.do(lambda e, t=t, bank=bank: e.tensor_tensor(values[:, t, :], bank.ap[:, 2 * P:3 * P],
                                                                 self.row["L3_xattn_qkv_b"][:, 2 * P:3 * P], ALU.add), m)
            bank.free = [s1, s2]
            kept.append(s2)
            z = junk.next()
            s3 = ve.do(lambda e, t=t, q=q, z=z: e.tensor_tensor_reduce(
                z.ap, q.ap[:, 0:P], q.ap[:, P:2 * P], float(P) ** 0.5, 0.0, ALU.mult, ALU.add, score[:, t:t + 1]), s1, z.free)
            q.free, z.free = [s3], [s3]
            steps.append(s3)
        s = ve.do(lambda e: e.tensor_tensor(delta, score, score, ALU.subtract), steps)
        s = ac.do(lambda e: e.activation(delta, delta, ACT.Exp), s)
        s = ve.do(lambda e: e.reciprocal(score, delta), s)
        s = ve.do(lambda e: e.tensor_tensor(delta, delta, score, ALU.mult), s)
        s = ve.do(lambda e: e.tensor_tensor(values, values, delta.unsqueeze(2).to_broadcast([P, TILES, P]), ALU.mult), s, kept)
        turned = self.turn(values, self.xt, [s] * TILES)
        ready = self.token_layer([(self.xt, w["sa_out"])], turned, self.row["L3_xattn_sa_out_b"], y)
        ready = self.normalize(y, y, ready, gain=self.row["L3_xattn_ln1_g"], bias=self.row["L3_xattn_ln1_b"])
        turned = self.turn(y, self.xt, ready)
        after_mix = []

        def finish(b, half, o, ready):
            bank = self.banks.next()
            for j in (0, 1):
                m = pe.do(lambda e, j=j: e.matmul(bank.ap[:, j * P:(j + 1) * P], o.ap[:, j * P:(j + 1) * P], w["mha_out"],
                                                  start=True, stop=True), ready, bank.free)
            o.free = [m]
            t0 = QT * b + 2 * half
            rows = y[:, t0:t0 + 2, :]
            s1 = ve.do(lambda e: e.tensor_tensor(rows, bank.ap[:, 0:2 * P].rearrange("p (t n) -> p t n", t=2), rows, ALU.add), m)
            bank.free = [s1]
            s2 = ve.do(lambda e: e.tensor_tensor(rows, rows, self.row["L3_xattn_mha_out_b"].unsqueeze(1).to_broadcast([P, 2, P]),
                                                 ALU.add), s1)
            after_mix.extend([s2, s2])

        self.context_attention(heads, turned, self.w_ready[6], w["in"][:, 0:P], w["bq"], w["in"][:, P:2 * P], w["bk"],
                               w["in"][:, 2 * P:3 * P], w["bv"], None, finish)
        ready = self.normalize(y, y, after_mix, gain=self.row["L3_xattn_ln2_g"], bias=self.row["L3_xattn_ln2_b"])
        turned = self.turn(y, self.xt, ready)
        hidden = self.carve(FT, SEQ)
        free = None

        def close(b, ready):
            rows = slice(QT * b, QT * b + QT)
            ((measure, scale),), done = self.norm_groups(y[:, rows, :], y[:, rows, :], [ready] * QT, QT,
                                                         gain=self.row["L3_xattn_ln3_g"], bias=self.row["L3_xattn_ln3_b"],
                                                         room=self.room[:, 2 * BATCH + b, :])

            def update():
                self.xn_free[b] = self.add_batch_to_x(b, y, 3, done)
                self.follow(b)
                self.chore()

            self.chores += [measure, scale, update]

        for b in range(BATCH):
            steps = []
            for f in range(FT):
                bank = self.banks.next()
                m = pe.do(lambda e, b=b, f=f, bank=bank: e.matmul(bank.ap, w["lin1"][:, f * P:(f + 1) * P],
                                                                  self.xt[:, b * SEQ:(b + 1) * SEQ], start=True, stop=True),
                          turned[QT * b + QT - 1], bank.free)
                s = ac.do(lambda e, f=f, bank=bank: e.activation(hidden[:, f, :], bank.ap, ACT.Relu, bias=w["lin1_b"][:, f:f + 1]),
                          m, free)
                bank.free = [s]
                steps.append(s)
                self.chore()
            self.xt_free[b] = m
            bank = self.banks.next()
            for j in range(QT):
                for f in range(FT):
                    m = pe.do(lambda e, f=f, j=j, bank=bank: e.matmul(
                        bank.ap[:, j * P:(j + 1) * P], hidden[:, f, j * P:(j + 1) * P], w["lin2"][:, f * P:(f + 1) * P],
                        start=f == 0, stop=f == FT - 1), steps, bank.free)
            free = m
            self.chore()
            o = y[:, QT * b:QT * b + QT, :]
            s1 = ve.do(lambda e, o=o, bank=bank: e.tensor_tensor(o, bank.ap.rearrange("p (t n) -> p t n", t=QT), o, ALU.add), m)
            bank.free = [s1]
            s2 = ve.do(lambda e, o=o: e.tensor_tensor(o, o, self.row["L3_xattn_lin2_b"].unsqueeze(1).to_broadcast([P, QT, P]), ALU.add), s1)
            close(b, s2)

    def prepare_router(self):
        pe, ve, ac, po, w = self.pe, self.ve, self.ac, self.po, self.w[7]
        square, ones, sim = self.carve(E3), self.carve(P), self.sim
        s_one = po.do(lambda e: e.memset(ones, 1.0))
        s = ve.do(lambda e: e.tensor_tensor(square, w["sim"], w["sim"], ALU.mult), self.w_ready[7])
        yield
        bank = self.banks.next()
        m = pe.do(lambda e, bank=bank: e.matmul(bank.ap[:, 0:E3], ones, square, start=True, stop=True), s, s_one, bank.free)
        s = ve.do(lambda e, bank=bank: e.tensor_copy(square, bank.ap[:, 0:E3]), m)
        bank.free = [s]
        s = po.do(lambda e: e.tensor_tensor(square, square, self.half[:, 0:E3], ALU.pow), s)
        s = ve.do(lambda e: e.tensor_scalar(square, square, 1e-12, None, ALU.max), s)
        s = ve.do(lambda e: e.reciprocal(square, square), s)
        self.sim_ready = ve.do(lambda e: e.tensor_tensor(sim, w["sim"], square, ALU.mult), s)
        gate = self.gate
        s = ac.do(lambda e: e.activation(gate, self.row["L3_ffn_gates"], ACT.Exp, scale=-1.0))
        s = ve.do(lambda e: e.tensor_scalar(gate, gate, 1.0, None, ALU.add), s)
        self.gate_ready = ve.do(lambda e: e.reciprocal(gate, gate), s)

    def mixture_attention(self):
        pe, ve, ac, po = self.pe, self.ve, self.ac, self.po
        self.begin("mixture")
        w, y = self.w[7], self.xn
        self.do_chores()
        normed, turned = self.stream()
        length, junk = self.carve(TILES), Ring([self.carve(P) for _ in range(2)])
        steps = []
        for t in range(TILES):
            z = junk.next()
            s = ac.do(lambda e, t=t, z=z: e.activation(z.ap, y[:, t, :], ACT.Square, accum_out=length[:, t:t + 1]),
                      normed[t], z.free)
            z.free = [s]
            steps.append(s)
        s = po.do(lambda e: e.tensor_tensor(length, length, self.half[:, :], ALU.pow), steps)
        s = ve.do(lambda e: e.tensor_scalar(length, length, 1e-12, None, ALU.max), s)
        s_len = ve.do(lambda e: e.reciprocal(length, length), s)
        logits, s = self.token_products(self.sim, E3, turned, None, self.sim_ready)
        wide = [P, TILES, E3]
        per_token = lambda v: v.unsqueeze(2).to_broadcast(wide)
        s = ve.do(lambda e: e.tensor_tensor(logits, logits, per_token(length), ALU.mult), s, s_len)
        s = ve.do(lambda e: e.tensor_tensor(logits, logits, self.gate.unsqueeze(1).to_broadcast(wide), ALU.subtract), s, self.gate_ready)
        active, idle, rest = self.carve(TILES, E3), self.carve(TILES), self.carve(TILES, E3)
        s1 = ve.do(lambda e: e.tensor_scalar(active, logits, 0.0, None, ALU.is_gt), s)
        s2 = ve.do(lambda e: e.tensor_reduce(idle, active, AX_X, ALU.add), s1)
        s_idle = ve.do(lambda e: e.tensor_scalar(idle, idle, 0.0, None, ALU.is_equal), s2)
        hot1, _, s3 = self.one_hot_of_max(logits, self.c["down16"], E3, s)
        s3 = ve.do(lambda e: e.scalar_tensor_tensor(rest, hot1, CAUSAL, logits, ALU.mult, ALU.add), s3)
        hot2, _, s3 = self.one_hot_of_max(rest, self.c["down16"], E3, s3)
        s3 = ve.do(lambda e: e.tensor_tensor(hot1, hot1, hot2, ALU.add), s3)
        s3 = ve.do(lambda e: e.tensor_tensor(hot1, hot1, per_token(idle), ALU.mult), s3, s_idle)
        s3 = ve.do(lambda e: e.tensor_tensor(active, active, hot1, ALU.add), s3)
        mix, top, total = logits, self.carve(TILES), self.carve(TILES)
        s3 = ve.do(lambda e: e.tensor_scalar(active, active, 1.0, -CAUSAL, ALU.subtract, ALU.mult), s3)
        s3 = ve.do(lambda e: e.scalar_tensor_tensor(mix, logits, 0.0, active, ALU.max, ALU.add), s3)
        s3 = ve.do(lambda e: e.tensor_reduce(top, mix, AX_X, ALU.max), s3)
        s3 = ve.do(lambda e: e.tensor_tensor(mix, mix, per_token(top), ALU.subtract), s3)
        s3 = ac.do(lambda e: e.activation(mix, mix, ACT.Exp), s3)
        s3 = ve.do(lambda e: e.tensor_reduce(total, mix, AX_X, ALU.add), s3)
        s3 = ve.do(lambda e: e.reciprocal(total, total), s3)
        s_mix = ve.do(lambda e: e.tensor_tensor(mix, mix, per_token(total), ALU.mult), s3)
        mix_t, mix_t_ready = self.turn_small(mix, E3, s_mix)
        parts = self.carve(TOKENS, dt=BF16)
        rest_t = self.carve(TOKENS)
        s_zero = po.do(lambda e: e.memset(parts[0:96, :], 0.0))
        s = ve.do(lambda e: e.tensor_copy(parts[0:E3, :], mix_t[0:E3, :]), mix_t_ready, s_zero)
        s = ve.do(lambda e: e.tensor_tensor(rest_t[0:E3, :], mix_t[0:E3, :], parts[0:E3, :], ALU.subtract), s)
        s = ve.do(lambda e: e.tensor_copy(parts[32:32 + E3, :], rest_t[0:E3, :]), s)
        second = self.carve(TOKENS, dt=BF16)
        s = ve.do(lambda e: e.tensor_copy(second[0:E3, :], rest_t[0:E3, :]), s)
        s_parts = ve.do(lambda e: e.tensor_tensor(parts[64:64 + E3, :], rest_t[0:E3, :], second[0:E3, :], ALU.subtract), s)
        spread1 = self.cb["spread1"].rearrange("p (e m) -> p e m", e=E3)
        spread2 = self.cb["spread2"].rearrange("p (e m) -> p e m", e=E3 // 2)

        def weights_of(selector, b):
            bank = self.banks.next()
            m = pe.do(lambda e: e.matmul(bank.ap, selector, parts[0:96, b * SEQ:(b + 1) * SEQ], start=True, stop=True),
                      s_parts, bank.free, self.setup)
            return bank, m

        scaled = Ring([self.carve(SEQ) for _ in range(4)])
        q_ring, k_ring = Ring([self.carve(SEQ) for _ in range(2)]), Ring([self.carve(SEQ) for _ in range(2)])
        v_half, v_full = Ring([self.carve(SEQ)]), Ring([self.carve(QT, P) for _ in range(2)])
        bank_qk, bank_v, bank_a, bank_o = self.banks.slots[4:8]
        self.banks.slots = self.banks.slots[0:4]

        def project(b, meanwhile):
            pending = []

            def products(x, z, s):
                m = pe.do(lambda e, x=x, z=z: e.matmul(bank_qk.ap, w["qk"][:, x * P:(x + 1) * P], z.ap,
                                                       start=x == 0, stop=x == E3 - 1), s, bank_qk.free)
                o = slice(64 * (x % 2), 64 * (x % 2) + 64)
                m2 = pe.do(lambda e, x=x, z=z, o=o: e.matmul(bank_v.ap[o, :], w["v"][:, x * D3:(x + 1) * D3], z.ap,
                                                             start=x < 2, stop=x >= E3 - 2), bank_v.free)
                z.free = [m2]
                return m2

            for x in range(E3):
                wb, m = weights_of(spread1[0:96, x, :], b)
                z = scaled.next()
                s = ve.do(lambda e, wb=wb, z=z: e.tensor_tensor(z.ap, wb.ap, self.xt[:, b * SEQ:(b + 1) * SEQ], ALU.mult), m, z.free)
                wb.free = [s]
                pending.append((x, z, s))
                if len(pending) > 2:
                    last = products(*pending.pop(0))
                meanwhile()
            for p in pending:
                last = products(*p)
            q, k, vh, vf = q_ring.next(), k_ring.next(), v_half.next(), v_full.next()
            sq = ac.do(lambda e: e.activation(q.ap[0:D3, :], bank_qk.ap[0:D3, :], ACT.Copy), last, q.free)
            sk = ac.do(lambda e: e.activation(k.ap[0:D3, :], bank_qk.ap[D3:P, :], ACT.Copy), last, k.free)
            sv = ac.do(lambda e: e.activation(vh.ap, bank_v.ap, ACT.Copy), last, vh.free)
            bank_qk.free, bank_v.free = [sq, sk], [sv]
            bank = self.banks.next()
            for j in range(QT):
                m = pe.do(lambda e, j=j, bank=bank: e.matmul(bank.ap[:, j * P:(j + 1) * P], vh.ap[:, j * P:(j + 1) * P],
                                                             self.c["fold"], start=True, stop=True), sv, bank.free)
            vh.free = [m]
            s = ve.do(lambda e, bank=bank: e.tensor_copy(vf.ap.rearrange("p t n -> p (t n)"), bank.ap), m, vf.free)
            bank.free = [s]
            return b, q, k, vf, [sq, sk], s

        probs, probs_t = Ring([self.carve(SEQ) for _ in range(2)]), Ring([self.carve(QT, P) for _ in range(2)])
        attended = Ring([self.carve(SEQ) for _ in range(2)])
        mixed = Ring([self.carve(SEQ) for _ in range(3)])
        col = Ring([self.carve(3) for _ in range(4)])

        def attend(b, q, k, vf, qk_ready, v_ready):
            a_t, tiles, state = attended.next(), {}, {}

            def scores_of(t):
                n = (t + 1) * P
                bank, prob, c = self.banks.next(), probs.next(), col.next()
                for k0, k1 in ([(0, t * P)] if t else []) + [(t * P, n)]:
                    m = pe.do(lambda e, k0=k0, k1=k1: e.matmul(
                        bank.ap[:, k0:k1], q.ap[0:D3, t * P:n], k.ap[0:D3, k0:k1], start=True, stop=k1 < n), qk_ready, bank.free)
                m = pe.do(lambda e: e.matmul(bank.ap[:, t * P:n], self.cb["eye_b"], self.cb["causal"], start=False, stop=True))
                s = ve.do(lambda e: e.tensor_reduce(c.ap[:, 0:1], bank.ap[:, 0:n], AX_X, ALU.max, negate=True), m, c.free)
                s = ve.do(lambda e: e.tensor_scalar(c.ap[:, 0:1], c.ap[:, 0:1], D3 ** -0.5, None, ALU.mult), s)
                s = ac.do(lambda e: e.activation(prob.ap[:, 0:n], bank.ap[:, 0:n], ACT.Exp, bias=c.ap[:, 0:1], scale=D3 ** -0.5,
                                                 accum_out=c.ap[:, 1:2]), s, prob.free)
                bank.free = [s]
                tiles[t] = (prob, c, s)

            def turn_probs(t):
                n = (t + 1) * P
                prob, c, s = tiles[t]
                s = ve.do(lambda e: e.reciprocal(c.ap[:, 2:3], c.ap[:, 1:2]), s)
                s = ve.do(lambda e: e.tensor_scalar(prob.ap[:, 0:n], prob.ap[:, 0:n], c.ap[:, 2:3], None, ALU.mult), s)
                c.free = [s]
                bank, pt = self.banks.next(), probs_t.next()
                for kt in range(t + 1):
                    m = pe.do(lambda e, kt=kt: e.transpose(bank.ap[:, kt * P:(kt + 1) * P], prob.ap[:, kt * P:(kt + 1) * P],
                                                           self.eye), s, bank.free)
                prob.free = [m]
                s = ac.do(lambda e: e.activation(pt.ap[:, 0:t + 1, :].rearrange("p t n -> p (t n)"), bank.ap[:, 0:n], ACT.Copy),
                          m, pt.free)
                bank.free = [s]
                tiles[t] = (pt, s)

            def weigh(t):
                pt, s = tiles[t]
                for kt in range(t + 1):
                    m = pe.do(lambda e, kt=kt: e.matmul(bank_a.ap[:, t * P:(t + 1) * P], vf.ap[:, kt, :], pt.ap[:, kt, :],
                                                        start=kt == 0, stop=kt == t), s, v_ready, bank_a.free)
                pt.free = [m]
                if t == QT - 1:
                    q.free = k.free = vf.free = [m]
                    state["ready"] = ac.do(lambda e: e.activation(a_t.ap, bank_a.ap, ACT.Copy), m, a_t.free)
                    bank_a.free = [state["ready"]]

            def scale(p):
                wb, m = weights_of(spread2[0:96, p, :], b)
                z = mixed.next()
                s = ve.do(lambda e: e.tensor_tensor(z.ap, wb.ap, a_t.ap, ALU.mult), m, z.free, state["ready"])
                wb.free = a_t.free = [s]
                state[p] = (z, s)

            def products(p):
                z, s = state[p]
                for j in range(QT):
                    m = pe.do(lambda e, j=j: e.matmul(
                        bank_o.ap[:, j * P:(j + 1) * P], z.ap[:, j * P:(j + 1) * P], w["o"][:, p * P:(p + 1) * P],
                        start=p == 0 and j == 0, stop=p == E3 // 2 - 1, skip_group_check=True), s, bank_o.free)
                z.free = [m]
                if p == E3 // 2 - 1:
                    bank_o.free = [self.add_to_x(QT * b + j, bank_o.ap[:, j * P:(j + 1) * P], 7, m) for j in range(QT)]
                    self.store(b)

            pieces = []
            for i in range(QT + 2):
                pieces.append([(f, t) for f, t in ((turn_probs, i - 1), (scores_of, i), (weigh, i - 2)) if 0 <= t < QT])
            for p in range(E3 // 2 + 1):
                pieces.append([(f, n) for f, n in ((scale, p), (products, p - 1)) if 0 <= n < E3 // 2])
            return pieces

        def run(pieces, n):
            for _ in range(min(n, len(pieces))):
                for f, t in pieces.pop(0):
                    f(t)

        pieces = []
        for b in range(BATCH):
            now = project(b, lambda: run(pieces, 1))
            run(pieces, len(pieces))
            pieces = attend(*now)
        run(pieces, len(pieces))

    def close(self):
        self.sp.do(lambda e: e.nop(), self.stores, self.loads)


STAGES = [Program.image_attention, Program.top1_experts, Program.one_head, Program.batch_attention,
          Program.masked_attention, Program.scaled_feed_forward, Program.decoder_block, Program.mixture_attention]


def build(nc, dram, const_widths, const_b_widths):
    with ExitStack() as ctx:
        p = Program(nc, ctx, dram, const_widths, const_b_widths)
        p.open()
        for stage in STAGES:
            stage(p)
        p.close()
        p.finish()


def kernel(**inputs):
    import concourse.bacc as bacc
    from concourse.bass_utils import run_bass_kernel_spmd

    i = {k: np.asarray(v) for k, v in inputs.items()}
    const, const_widths, const_b, const_b_widths = constants()
    arrays = {
        "x": i["x"].reshape(TOKENS, P), "ctx": i["ctx_1024"].reshape(CTX_ROWS, P),
        "mask": i["mask_BxSxS2_bf0"].reshape(TOKENS, CTX),
        "rows": np.concatenate([i[k].reshape(-1) for k in ROWS])[None],
        "small": np.concatenate([i["L0_ffn_b2"], i["L1_ffn_b2"]], 1),
        "const": const, "const_b": const_b,
    }
    for k, parts in enumerate(WEIGHTS):
        arrays[f"weights{k}"] = np.concatenate([lay(i) for _, lay in parts.values()], 1)
    nc = bacc.Bacc("TRN2", target_bir_lowering=False, num_devices=1)
    dram, feed = {}, {}
    for name, a in arrays.items():
        a = np.ascontiguousarray(a)
        feed[f"in_{name}"] = a
        dram[name] = nc.dram_tensor(f"in_{name}", a.shape, mybir.dt.from_np(a.dtype), kind="ExternalInput").ap()
    dram["out"] = nc.dram_tensor("out", (TOKENS, P), F32, kind="ExternalOutput").ap()
    build(nc, dram, const_widths, const_b_widths)
    r = run_bass_kernel_spmd(nc, [feed], core_ids=[0])
    return r.results[0]["out"].reshape(BATCH, SEQ, P)
```
